# Optimizing a Trainium2 kernel written in Bass

```python
import numpy as np
import jax
import jax.numpy as jnp

def _softmax(x, axis=-1):
    return jax.nn.softmax(x, axis=axis)

def _gelu(x):
    return jax.nn.gelu(x, approximate=True)

def _silu(x):
    return jax.nn.silu(x)

def _sigmoid(x):
    return jax.nn.sigmoid(x)

def _layernorm(x, axis=-1, eps=1e-05):
    m = jnp.mean(x, axis=axis, keepdims=True)
    v = jnp.var(x, axis=axis, keepdims=True)
    return (x - m) / jnp.sqrt(v + eps)

def _scatter_add(tgt, idx, src, axis=0):
    return tgt.at[idx].add(src)

def _segment_sum(src, seg, n):
    return jax.ops.segment_sum(src, seg, n)
kernel_name = 'mk_macaron_d2_jaxref_r4_a7f0a1'

def setup_inputs(seed: int=0):
    np.random.seed(seed)
    _w = jnp.asarray

    def _L0_attn_setup():
        import jax, jax.numpy as jnp
        import numpy as np
        D_MODEL = 256
        N_HEADS = 16
        LAMBDA = 0.5
        EPS = 1e-09
        key = jax.random.key(seed)
        ks = jax.random.split(key, 5)
        B, L, D = (2, 512, D_MODEL)
        scale = 1.0 / np.sqrt(D)
        return {'x': jax.random.normal(ks[0], (B, L, D), dtype=jnp.float32), 'Wq': jax.random.normal(ks[1], (D, D), dtype=jnp.float32) * scale, 'bq': jnp.zeros((D,), dtype=jnp.float32), 'Wk': jax.random.normal(ks[2], (D, D), dtype=jnp.float32) * scale, 'bk': jnp.zeros((D,), dtype=jnp.float32), 'Wv': jax.random.normal(ks[3], (D, D), dtype=jnp.float32) * scale, 'bv': jnp.zeros((D,), dtype=jnp.float32), 'Wo': jax.random.normal(ks[4], (D, D), dtype=jnp.float32) * scale, 'bo': jnp.zeros((D,), dtype=jnp.float32)}
    _L0_attn_in = _L0_attn_setup()

    def _L0_ffn_setup():
        import jax, jax.numpy as jnp
        import numpy as np
        DIM = 256
        HIDDEN = 768
        SCALE = 1.0 / 127.0

        def _dequant(w_int, dtype):
            return w_int.astype(dtype) * jnp.asarray(SCALE, dtype)
        key = jax.random.key(seed)
        k_x, k_g, k_u, k_d = jax.random.split(key, 4)
        x = jax.random.normal(k_x, (4, 512, DIM), dtype=jnp.float32)
        w_gate = jax.random.randint(k_g, (HIDDEN, DIM), -127, 128, dtype=jnp.int32)
        w_up = jax.random.randint(k_u, (HIDDEN, DIM), -127, 128, dtype=jnp.int32)
        w_down = jax.random.randint(k_d, (DIM, HIDDEN), -127, 128, dtype=jnp.int32)
        return {'x': x, 'w_gate': w_gate, 'w_up': w_up, 'w_down': w_down}
    _L0_ffn_in = _L0_ffn_setup()

    def _L1_attn_setup():
        import jax, jax.numpy as jnp
        import numpy as np
        B, N, D = (4, 512, 256)
        H = 16
        HD = D // H
        SCALE = 1.0 / HD
        NEG = -10000.0
        THETA = 10000.0

        def _rope(t):
            d, n = (t.shape[-1], t.shape[-2])
            inv_freq = 1.0 / THETA ** (jnp.arange(0, d, 2, dtype=jnp.float32) / d)
            ang = jnp.arange(n, dtype=jnp.float32)[:, None] * inv_freq[None, :]
            cos = jnp.repeat(jnp.cos(ang), 2, axis=-1)
            sin = jnp.repeat(jnp.sin(ang), 2, axis=-1)
            x1, x2 = (t[..., ::2], t[..., 1::2])
            rot = jnp.stack([-x2, x1], axis=-1).reshape(t.shape)
            return t * cos + rot * sin
        key = jax.random.key(seed)
        ks = jax.random.split(key, 6)
        s = (1.0 / D) ** 0.5
        return {'x': jax.random.normal(ks[0], (B, N, D), jnp.float32), 'Wq': jax.random.normal(ks[1], (D, D), jnp.float32) * s, 'Wk': jax.random.normal(ks[2], (D, D), jnp.float32) * s, 'Wv': jax.random.normal(ks[3], (D, D), jnp.float32) * s, 'Wo': jax.random.normal(ks[4], (D, D), jnp.float32) * s, 'bo': jnp.zeros((D,), jnp.float32)}
    _L1_attn_in = _L1_attn_setup()

    def _L1_ffn_setup():
        import jax, jax.numpy as jnp
        import numpy as np
        N_EMBD = 256
        N_STATE = 1024
        key = jax.random.key(seed)
        k_x, k_w1, k_b1, k_w2, k_b2 = jax.random.split(key, 5)
        x = jax.random.normal(k_x, (4, 512, N_EMBD), dtype=jnp.float32)
        w1 = jax.random.normal(k_w1, (N_EMBD, N_STATE), dtype=jnp.float32) * (1.0 / np.sqrt(N_EMBD))
        b1 = jax.random.normal(k_b1, (N_STATE,), dtype=jnp.float32) * 0.02
        w2 = jax.random.normal(k_w2, (N_STATE, N_EMBD), dtype=jnp.float32) * (1.0 / np.sqrt(N_STATE))
        b2 = jax.random.normal(k_b2, (N_EMBD,), dtype=jnp.float32) * 0.02
        return {'x': x, 'w1': w1, 'b1': b1, 'w2': w2, 'b2': b2}
    _L1_ffn_in = _L1_ffn_setup()
    _d = {'L0_attn_x': _L0_attn_in['x'], 'L0_attn_Wq': _L0_attn_in['Wq'], 'L0_attn_bq': _L0_attn_in['bq'], 'L0_attn_Wk': _L0_attn_in['Wk'], 'L0_attn_bk': _L0_attn_in['bk'], 'L0_attn_Wv': _L0_attn_in['Wv'], 'L0_attn_bv': _L0_attn_in['bv'], 'L0_attn_Wo': _L0_attn_in['Wo'], 'L0_attn_bo': _L0_attn_in['bo'], 'L0_ffn_w_gate': _L0_ffn_in['w_gate'], 'L0_ffn_w_up': _L0_ffn_in['w_up'], 'L0_ffn_w_down': _L0_ffn_in['w_down'], 'L1_attn_Wq': _L1_attn_in['Wq'], 'L1_attn_Wk': _L1_attn_in['Wk'], 'L1_attn_Wv': _L1_attn_in['Wv'], 'L1_attn_Wo': _L1_attn_in['Wo'], 'L1_attn_bo': _L1_attn_in['bo'], 'L1_ffn_w1': _L1_ffn_in['w1'], 'L1_ffn_b1': _L1_ffn_in['b1'], 'L1_ffn_w2': _L1_ffn_in['w2'], 'L1_ffn_b2': _L1_ffn_in['b2']}
    _x0 = _d['L0_attn_x']
    _d['L0_attn_x'] = jax.random.normal(jax.random.fold_in(jax.random.key(seed), 1), (4, 1024, 256), dtype=_x0.dtype)
    del _x0
    return _d

def reference(L0_attn_x, L0_attn_Wq, L0_attn_bq, L0_attn_Wk, L0_attn_bk, L0_attn_Wv, L0_attn_bv, L0_attn_Wo, L0_attn_bo, L0_ffn_w_gate, L0_ffn_w_up, L0_ffn_w_down, L1_attn_Wq, L1_attn_Wk, L1_attn_Wv, L1_attn_Wo, L1_attn_bo, L1_ffn_w1, L1_ffn_b1, L1_ffn_w2, L1_ffn_b2):

    def _L0_attn_ref(x, Wq, bq, Wk, bk, Wv, bv, Wo, bo):
        import jax, jax.numpy as jnp
        import numpy as np
        D_MODEL = 256
        N_HEADS = 16
        LAMBDA = 0.5
        EPS = 1e-09
        B, L, D = x.shape
        H = N_HEADS
        dk = D // H

        def heads(y):
            return y.reshape(B, L, H, dk).transpose(0, 2, 1, 3)
        Q = heads(x @ Wq.T + bq)
        K = heads(x @ Wk.T + bk)
        V = heads(x @ Wv.T + bv)
        scores = jnp.einsum('bhqd,bhkd->bhqk', Q, K) / jnp.sqrt(jnp.float32(dk))
        probs = jax.nn.softmax(scores, axis=-1)
        intervened = probs.at[:, :, :, 0].set(0.0)
        denom = jnp.clip(intervened.sum(axis=-1, keepdims=True), 1e-09, None)
        intervened = intervened / denom
        combined = probs + LAMBDA * (intervened - probs)
        attn_out = jnp.einsum('bhqk,bhkd->bhqd', combined, V)
        attn_out = attn_out.transpose(0, 2, 1, 3).reshape(B, L, D)
        return attn_out @ Wo.T + bo

    def _L0_ffn_ref(x, w_gate, w_up, w_down):
        import jax, jax.numpy as jnp
        import numpy as np
        DIM = 256
        HIDDEN = 768
        SCALE = 1.0 / 127.0

        def _dequant(w_int, dtype):
            return w_int.astype(dtype) * jnp.asarray(SCALE, dtype)
        wg = _dequant(w_gate, x.dtype)
        wu = _dequant(w_up, x.dtype)
        wd = _dequant(w_down, x.dtype)
        gate = jnp.einsum('bsd,hd->bsh', x, wg)
        up = jnp.einsum('bsd,hd->bsh', x, wu)
        h = jax.nn.silu(gate) * up
        return jnp.einsum('bsh,dh->bsd', h, wd)

    def _L1_attn_ref(x, Wq, Wk, Wv, Wo, bo):
        import jax, jax.numpy as jnp
        import numpy as np
        B, N, D = (4, 512, 256)
        H = 16
        HD = D // H
        SCALE = 1.0 / HD
        NEG = -10000.0
        THETA = 10000.0

        def _rope(t):
            d, n = (t.shape[-1], t.shape[-2])
            inv_freq = 1.0 / THETA ** (jnp.arange(0, d, 2, dtype=jnp.float32) / d)
            ang = jnp.arange(n, dtype=jnp.float32)[:, None] * inv_freq[None, :]
            cos = jnp.repeat(jnp.cos(ang), 2, axis=-1)
            sin = jnp.repeat(jnp.sin(ang), 2, axis=-1)
            x1, x2 = (t[..., ::2], t[..., 1::2])
            rot = jnp.stack([-x2, x1], axis=-1).reshape(t.shape)
            return t * cos + rot * sin
        b, n, _ = x.shape
        q = (x @ Wq.T).reshape(b, n, H, HD).transpose(0, 2, 1, 3)
        k = (x @ Wk.T).reshape(b, n, H, HD).transpose(0, 2, 1, 3)
        v = (x @ Wv.T).reshape(b, n, H, HD).transpose(0, 2, 1, 3)
        q = _rope(q)
        k = _rope(k)
        i = jnp.arange(n)
        add_mask = jnp.where(i[:, None] >= i[None, :], 0.0, NEG).astype(x.dtype)
        scores = jnp.einsum('bhqd,bhkd->bhqk', q, k) * SCALE + add_mask
        attn = jax.nn.softmax(scores, axis=-1)
        out = jnp.einsum('bhqk,bhkd->bhqd', attn, v)
        out = out.transpose(0, 2, 1, 3).reshape(b, n, H * HD)
        return out @ Wo.T + bo

    def _L1_ffn_ref(x, w1, b1, w2, b2):
        import jax, jax.numpy as jnp
        import numpy as np
        N_EMBD = 256
        N_STATE = 1024
        h = jax.nn.gelu(jnp.einsum('bse,eh->bsh', x, w1) + b1, approximate=False)
        return jnp.einsum('bsh,he->bse', h, w2) + b2
    x = L0_attn_x
    x = x + 0.5 * _L0_ffn_ref(_layernorm(x, axis=-1), L0_ffn_w_gate, L0_ffn_w_up, L0_ffn_w_down)
    x = x + _L0_attn_ref(_layernorm(x, axis=-1), L0_attn_Wq, L0_attn_bq, L0_attn_Wk, L0_attn_bk, L0_attn_Wv, L0_attn_bv, L0_attn_Wo, L0_attn_bo)
    x = x + 0.5 * _L0_ffn_ref(_layernorm(x, axis=-1), L0_ffn_w_gate, L0_ffn_w_up, L0_ffn_w_down)
    x = x + 0.5 * _L1_ffn_ref(_layernorm(x, axis=-1), L1_ffn_w1, L1_ffn_b1, L1_ffn_w2, L1_ffn_b2)
    x = x + _L1_attn_ref(_layernorm(x, axis=-1), L1_attn_Wq, L1_attn_Wk, L1_attn_Wv, L1_attn_Wo, L1_attn_bo)
    x = x + 0.5 * _L1_ffn_ref(_layernorm(x, axis=-1), L1_ffn_w1, L1_ffn_b1, L1_ffn_w2, L1_ffn_b2)
    return x

_drawn_inputs = setup_inputs


def setup_inputs(seed=0):
    import zlib

    import numpy as np

    out = dict(_drawn_inputs(seed))
    spreads = {'L0_attn_bq': (0.0, 0.8),
     'L0_attn_bk': (0.0, 2.0),
     'L0_attn_bv': (0.0, 2.0),
     'L0_attn_bo': (0.0, 2.0),
     'L1_attn_bo': (0.0, 2.0)}
    factors = {'L0_attn_Wq': 8.0,
     'L0_attn_Wk': 8.0,
     'L0_attn_Wv': 8.0,
     'L0_attn_Wo': 8.0,
     'L1_attn_Wq': 8.0,
     'L1_attn_Wk': 8.0,
     'L1_attn_Wv': 8.0,
     'L1_attn_Wo': 8.0,
     'L1_ffn_w1': 8.0,
     'L1_ffn_b1': 200.0,
     'L1_ffn_w2': 8.0,
     'L1_ffn_b2': 200.0}
    for name, (base, spread) in spreads.items():
        noise = np.random.default_rng([zlib.crc32(name.encode()), seed]).standard_normal(out[name].shape)
        drawn = base * np.exp(spread * noise) if base else spread * noise
        out[name] = jnp.asarray(drawn.astype(out[name].dtype))
    for name, factor in factors.items():
        out[name] = (out[name] * factor).astype(out[name].dtype)
    return out
```

```python
from contextlib import ExitStack

import concourse.bass as bass
from concourse import mybir

F32 = mybir.dt.float32
F32R = mybir.dt.float32r
BF16 = mybir.dt.bfloat16
F16 = mybir.dt.float16
I32 = mybir.dt.int32
ALU = mybir.AluOpType
ACT = mybir.ActivationFunctionType
AX = mybir.AxisListType

P = 128
B, S, D = 4, 1024, 256
H, HD = 16, 16
TILES = B * S // P
CT = 4
CHUNK = CT * P
CHUNKS = TILES // CT
KD = D // P
HID0, HID1 = 768, 1024
EPS = 1e-5
DEQ = 1.0 / 127.0
LAMBDA = 0.5
CLIP = 1e-9
GH = 4
GROUPS = H // GH
ITERS = B * GROUPS
SETS = 4
PARTS_Q = (0, 0, 0, 1, 1, 2)
PARTS_K = (0, 1, 2, 0, 1, 0)
SROWS = HD * len(PARTS_Q)
MROWS = 3
QT = S // P
KC = S // 512
VW = 32
MAXES = GH * QT * KC
STEPS = KC * QT
PACE = 5


def each_chunk(eng, body):
    body(0, 0, 0, True, False)
    with eng.Fori(0, (CHUNKS - 2) // 2) as k:
        body(k * 2 + 1, 1, k, False, False)
        body(k * 2 + 2, 0, k + 1, False, False)
    body(CHUNKS - 1, 1, (CHUNKS - 1) // 2, False, True)


def each_chunk_of_two(eng, body):
    body(0, 0, 0, True)
    body(1, 1, 0, True)
    with eng.Fori(0, (CHUNKS - 2) // 2) as k:
        body(k * 2 + 2, 0, k + 1, False)
        body(k * 2 + 3, 1, k + 1, False)


def each_chunk_of_pairs(eng, body):
    body(0, 0, 0, True, False)
    body(1, 1, 0, True, False)
    with eng.Fori(0, (CHUNKS - 4) // 2) as k:
        body(k * 2 + 2, 0, k + 1, False, False)
        body(k * 2 + 3, 1, k + 1, False, False)
    body(CHUNKS - 2, 0, (CHUNKS - 2) // 2, False, False)
    body(CHUNKS - 1, 1, (CHUNKS - 2) // 2, False, True)


class It:

    def __init__(self, k, r):
        self.k, self.r = k, r
        self.b = k + r // GROUPS
        self.hg = r % GROUPS
        self.set = r % SETS
        self.par = r % 2
        self.pair = k * 2 + r // 2

    def n(self, mult, plus):
        return self.k * (4 * mult) + (self.r * mult + plus)

    def ahead(self, d):
        return It(self.k, self.r + d)


def each_iteration(eng, body):
    body(It(0, 0), True, False)
    with eng.Fori(0, 3) as k:
        for r in range(1, 5):
            body(It(k, r), False, False)
    for n in range(13, ITERS):
        body(It(0, n), False, n == ITERS - 1)


class Env:
    pass


def three_pass(pe, out, left, right, first, last, skip=False):
    pe.matmul(out, left[0], right[1], start=first, stop=False, skip_group_check=skip)
    pe.matmul(out, left[1], right[0], start=False, stop=False, skip_group_check=skip)
    return pe.matmul(out, left[0], right[0], start=False, stop=last, skip_group_check=skip)


def pair(parts, *index):
    return parts[0][index], parts[1][index]


def alloc_norm(E, sb):
    E.mean, E.rstd = sb("ln_mean", [P, TILES], F32), sb("ln_rstd", [P, TILES], F32)
    E.ln_a, E.ln_b, E.ln_c = (sb(f"ln_{n}", [P, TILES], F32) for n in "abc")
    E.std = sb("ln_std", [P, TILES], F32)


def norm_scales_vector(v, E, ln_step, ln_var, ln_std):
    me, ve, mo, vo = (E.stats[:, :, i] for i in (1, 2, 4, 5))
    a, b, c = E.ln_a[:, :], E.ln_b[:, :], E.ln_c[:, :]
    n = 0

    def chain(ins):
        nonlocal n
        n += 1
        ins.then_inc(ln_step, 1)
        v.wait_ge(ln_step, n)

    chain(v.tensor_tensor(a, me, mo, ALU.add))
    chain(v.tensor_scalar(E.mean[:, :], a, 0.5, None, ALU.mult))
    chain(v.tensor_tensor(b, me, mo, ALU.subtract))
    chain(v.tensor_tensor(c, b, b, ALU.mult))
    chain(v.tensor_tensor(b, ve, vo, ALU.add))
    chain(v.tensor_scalar(a, b, 1.0 / D, EPS, ALU.mult, ALU.add))
    v.scalar_tensor_tensor(out=b, in0=c, scalar=0.25, in1=a, op0=ALU.mult, op1=ALU.add).then_inc(ln_var, 1)
    v.wait_ge(ln_std, 1)
    chain(v.reciprocal(a, E.std[:, :]))
    chain(v.tensor_tensor(c, b, a, ALU.mult))
    chain(v.tensor_tensor(a, c, E.std[:, :], ALU.add))
    chain(v.tensor_scalar(c, a, 0.5, None, ALU.mult))
    chain(v.reciprocal(E.rstd[:, :], c))


def norm_scales_scalar(act, E, ln_var, ln_std):
    act.wait_ge(ln_var, 1)
    act.activation(E.std[:, :], E.ln_b[:, :], ACT.Sqrt).then_inc(ln_std, 1)


def alloc_front(E, sb):
    E.xn = sb("xn", [P, 2, CT, D], F32)
    E.xt = [sb(f"xt_{n}", [P, 2, KD, CHUNK], F32R) for n in ("hi", "lo")]


def normalise(v, E, c, par, s):
    for t in range(CT):
        at = bass.ds(c * CT + t, 1)
        ins = v.tensor_scalar(E.xn[:, par, t:t + 1, :], E.x[:, at, :], E.mean[:, at], E.rstd[:, at],
                              ALU.subtract, ALU.mult)
    ins.then_inc(s["xn_ready"], 1)


def turn(pe, E, T, c, par, s, first=False):
    pe.wait_ge(s["xn_ready"], c + 1)
    if not first:
        pe.wait_ge(s["hi_ready"], c * KD)
        pe.wait_ge(s["lo_ready"], c * KD)
    for k in range(KD):
        for t in range(CT):
            mm = pe.transpose(T[:, k, t * P:(t + 1) * P], E.xn[:, par, t, k * P:(k + 1) * P], E.ident[:, :])
        mm.then_inc(s["turned"], 1)


def part_hi(act, E, T, c, par, s):
    for k in range(KD):
        act.wait_ge(s["turned"], c * KD + k + 1)
        act.activation(E.xt[0][:, par, k, :], T[:, k, :], ACT.Copy).then_inc(s["hi_ready"], 1)


def part_lo(v, E, T, c, par, s):
    for k in range(KD):
        v.wait_ge(s["hi_ready"], c * KD + k + 1)
        v.tensor_tensor(E.xt[1][:, par, k, :], T[:, k, :], E.xt[0][:, par, k, :].bitcast(F32),
                        ALU.subtract).then_inc(s["lo_ready"], 1)


def new_semaphore(nc, E, name):
    sem = nc.alloc_semaphore(name)
    E.semaphores.append(sem)
    return sem


def semaphores(nc, E, name, *names):
    return {n: new_semaphore(nc, E, f"{name}_{n}") for n in names}


def clear_semaphores(nc, E):
    nc.clear_and_free_semaphores(E.semaphores)
    nc.all_engine_barrier()
    E.semaphores = []


def statistics(v, E, c):
    for t in range(CT):
        ins = v.bn_stats(E.stats[:, bass.ds(c * CT + t, 1), :], E.x[:, bass.ds(c * CT + t, 1), :])
    return ins


def load_stage(nc, E, name, ffn, square, small, x_dram=None):
    with ExitStack() as ctx:
        def sb(n, shape, dt):
            return ctx.enter_context(nc.sbuf_tensor(f"{name}_{n}", shape, dt))

        s = semaphores(nc, E, name, "x", "small", "cast", "hi", "lo", "st", "scaled")
        jobs = ffn + square
        landed = [new_semaphore(nc, E, f"{name}_w{i}") for i in range(len(jobs))]
        raw = [sb(f"raw{i}", [P, k, n], I32 if whole else F32) for i, (_, _, k, n, whole) in enumerate(jobs)]
        val = [sb(f"val{i}", [P, k, n], F32) if whole else raw[i] for i, (_, _, k, n, whole) in enumerate(jobs)]
        casts = sum(j[4] for j in jobs)
        block = ctx.enter_context(nc.Block())

        @block.sync
        def _(sp):
            for i, (_, src, k, n, _) in enumerate(jobs):
                sp.dma_start(raw[i][:, :, :], src.rearrange("(k p) n -> p k n", p=P)).then_inc(landed[i], 16)
            for tile, src in small:
                sp.dma_start(tile, src).then_inc(s["small"], 16)
            if x_dram is not None:
                for c in range(CHUNKS):
                    sp.dma_start(E.x[:, c * CT:(c + 1) * CT, :],
                                 x_dram[c * CHUNK:(c + 1) * CHUNK, :].rearrange("(t p) f -> p t f", p=P)).then_inc(s["x"], 16)
                sp.wait_ge(s["x"], 16 * CHUNKS)
            sp.wait_ge(s["small"], 16 * len(small))

        @block.vector
        def _(v):
            cast = 0
            for i, (parts, _, k, n, whole) in enumerate(jobs):
                v.wait_ge(landed[i], 16)
                if whole:
                    v.tensor_copy(val[i][:, :, :], raw[i][:, :, :]).then_inc(s["cast"], 1)
                    cast += 1
                    v.wait_ge(s["cast"], cast)
                v.tensor_copy(parts[0][:, :, :], val[i][:, :, :]).then_inc(s["hi"], 1)
            if x_dram is not None:
                v.wait_ge(s["x"], 16 * CHUNKS)
                for c in range(CHUNKS):
                    statistics(v, E, c)
            E.scale_small(v, s)

        @block.gpsimd
        def _(p):
            for i, (parts, _, k, n, whole) in enumerate(jobs):
                p.wait_ge(s["hi"], i + 1)
                p.tensor_tensor(parts[1][:, :, :], val[i][:, :, :], parts[0][:, :, :].bitcast(F32),
                                ALU.subtract).then_inc(s["lo"], 1)


def ffn_stage(nc, E, name, gated, out_dram=None):
    F = (HID0 if gated else HID1) // P
    with ExitStack() as ctx:
        def sb(n, shape, dt):
            return ctx.enter_context(nc.sbuf_tensor(f"{name}_{n}", shape, dt))

        alloc_norm(E, sb)
        alloc_front(E, sb)
        h = sb("h", [P, 2, CHUNK], F32)
        h_parts = [sb(f"h_{n}", [P, 2, CHUNK], F32R) for n in ("hi", "lo")]
        gate_act = sb("gate_act", [P, 2, CHUNK], F32) if gated else None
        xb = None if gated else sb("xb", [P, 2, CT, D], F32)
        up_ps = ctx.enter_context(nc.psum_tensor(f"{name}_up", [P, 2, 2 if gated else 1, CHUNK], F32))
        acc = ctx.enter_context(nc.psum_tensor(f"{name}_acc", [P, CT, D], F32))
        T = ctx.enter_context(nc.psum_tensor(f"{name}_T", [P, KD, CHUNK], F32))
        s = semaphores(nc, E, name, "ln_step", "ln_var", "ln_std", "xn_ready", "turned", "hi_ready", "lo_ready",
                       "up_ready", "gate_ready", "h_ready", "h_hi", "h_lo", "down_done", "x_new", "xb_ready",
                       "stored")
        block = ctx.enter_context(nc.Block())
        used = s["h_ready"]

        @block.tensor
        def _(pe):
            def up(c, par, f, first):
                if f == 0:
                    pe.wait_ge(s["hi_ready"], c * KD + KD)
                    pe.wait_ge(s["lo_ready"], c * KD + KD)
                if not first or f >= 2:
                    pe.wait_ge(used, c * F + f - 1)
                cols = slice(f * P, (f + 1) * P)
                for g, w in enumerate(E.w_up):
                    for k in range(KD):
                        mm = three_pass(pe, up_ps[:, f % 2, g, :], pair(w, slice(None), k, cols),
                                        pair(E.xt, slice(None), par, k, slice(None)), k == 0, k == KD - 1)
                mm.then_inc(s["up_ready"], 1)

            def down(c, f, first):
                pe.wait_ge(s["h_hi"], c * F + f + 1)
                pe.wait_ge(s["h_lo"], c * F + f + 1)
                if f == 0 and not first:
                    pe.wait_ge(s["x_new"], c * 2)
                for t in range(CT):
                    mm = three_pass(pe, acc[:, t, :], pair(h_parts, slice(None), f % 2, slice(t * P, (t + 1) * P)),
                                    pair(E.w_down, slice(None), f, slice(None)), f == 0 and t % 2 == 0, f == F - 1, True)
                mm.then_inc(s["down_done"], 1)

            turn(pe, E, T, 0, 0, s, True)

            def body(c, par, use, first, last):
                for f in range(F):
                    up(c, par, f, first)
                    if f > 0:
                        down(c, f - 1, first)
                    elif not first:
                        down(c - 1, F - 1, False)
                    if f == 2 and not last:
                        turn(pe, E, T, c + 1, 1 - par, s)

            each_chunk(pe, body)
            down(CHUNKS - 1, F - 1, False)

        @block.scalar
        def _(act):
            norm_scales_scalar(act, E, s["ln_var"], s["ln_std"])
            part_hi(act, E, T, 0, 0, s)

            def body(c, par, use, first, last):
                for f in range(F):
                    act.wait_ge(s["up_ready"], c * F + f + 1)
                    if gated:
                        if not first or f >= 2:
                            act.wait_ge(s["h_ready"], c * F + f - 1)
                        act.activation(gate_act[:, f % 2, :], up_ps[:, f % 2, 0, :], ACT.Silu,
                                       scale=DEQ).then_inc(s["gate_ready"], 1)
                    else:
                        if not first or f >= 2:
                            act.wait_ge(s["h_lo"], c * F + f - 1)
                        act.activation(h[:, f % 2, :], up_ps[:, f % 2, 0, :], ACT.Gelu,
                                       bias=E.b1[:, f:f + 1]).then_inc(s["h_ready"], 1)
                    if f == 3 and not last:
                        part_hi(act, E, T, c + 1, 1 - par, s)

            each_chunk(act, body)

        @block.gpsimd
        def _(p):
            def add_bias(c, par):
                for t in range(CT):
                    ins = p.tensor_tensor(xb[:, par, t:t + 1, :], E.x[:, bass.ds(c * CT + t, 1), :],
                                          E.b2_half[:, :].unsqueeze(1), ALU.add)
                ins.then_inc(s["xb_ready"], 1)

            if not gated:
                add_bias(0, 0)

            def body(c, par, use, first, last):
                for f in range(F):
                    if f == F - 1 and not (gated or first or last):
                        p.wait_ge(s["x_new"], c * 2)
                    p.wait_ge(s["h_hi"], c * F + f + 1)
                    if not first or f >= 2:
                        p.wait_ge(s["down_done"], c * F + f - 1)
                    p.tensor_tensor(h_parts[1][:, f % 2, :], h[:, f % 2, :], h_parts[0][:, f % 2, :].bitcast(F32),
                                    ALU.subtract).then_inc(s["h_lo"], 1)
                if not (gated or last):
                    add_bias(c + 1, 1 - par)

            each_chunk(p, body)

        @block.vector
        def _(v):
            norm_scales_vector(v, E, s["ln_step"], s["ln_var"], s["ln_std"])
            normalise(v, E, 0, 0, s)
            part_lo(v, E, T, 0, 0, s)

            def finish(c, par):
                v.wait_ge(s["down_done"], c * F + F)
                if not gated:
                    v.wait_ge(s["xb_ready"], c + 1)
                for q in range(2):
                    at = bass.ds(c * CT + 2 * q, 2)
                    v.scalar_tensor_tensor(out=E.x[:, at, :], in0=acc[:, 2 * q:2 * q + 2, :],
                                           scalar=0.5 * DEQ if gated else 0.5,
                                           in1=E.x[:, at, :] if gated else xb[:, par, 2 * q:2 * q + 2, :],
                                           op0=ALU.mult, op1=ALU.add).then_inc(s["x_new"], 1)
                if out_dram is None:
                    v.wait_ge(s["x_new"], c * 2 + 2)
                    statistics(v, E, c)

            def body(c, par, use, first, last):
                if not last:
                    if not first:
                        v.wait_ge(s["turned"], c * KD)
                    normalise(v, E, c + 1, 1 - par, s)
                for f in range(F):
                    if gated:
                        v.wait_ge(s["gate_ready"], c * F + f + 1)
                        if not first or f >= 2:
                            v.wait_ge(s["h_lo"], c * F + f - 1)
                        v.scalar_tensor_tensor(out=h[:, f % 2, :], in0=up_ps[:, f % 2, 1, :], scalar=DEQ,
                                               in1=gate_act[:, f % 2, :], op0=ALU.mult, op1=ALU.mult).then_inc(s["h_ready"], 1)
                    v.wait_ge(s["h_ready"], c * F + f + 1)
                    if not first or f >= 2:
                        v.wait_ge(s["down_done"], c * F + f - 1)
                    v.tensor_copy(h_parts[0][:, f % 2, :], h[:, f % 2, :]).then_inc(s["h_hi"], 1)
                    if f == 1 and not first:
                        finish(c - 1, 1 - par)
                    if f == 3 and not last:
                        part_lo(v, E, T, c + 1, 1 - par, s)

            each_chunk(v, body)
            finish(CHUNKS - 1, (CHUNKS - 1) % 2)

        if out_dram is not None:
            @block.sync
            def _(sp):
                def body(c, par, use, first, last):
                    sp.wait_ge(s["x_new"], c * 2 + 2)
                    sp.dma_start(out_dram[bass.ds(c * CHUNK, CHUNK), :].rearrange("(t p) f -> p t f", p=P),
                                 E.x[:, bass.ds(c * CT, CT), :]).then_inc(s["stored"], 16)

                each_chunk(sp, body)
                sp.wait_ge(s["stored"], 16 * CHUNKS)


def qkv_stage(nc, E, name, rope):
    QK = 2 * KD
    with ExitStack() as ctx:
        def sb(n, shape, dt):
            return ctx.enter_context(nc.sbuf_tensor(f"{name}_{n}", shape, dt))

        alloc_norm(E, sb)
        alloc_front(E, sb)
        qf = sb("qf", [P, QK, CHUNK], F32)
        raw = sb("raw", [P, QK, CHUNK], F32) if rope else qf
        swapped = sb("swapped", [P, CHUNK], F32) if rope else None
        cos_part = sb("cos_part", [P, CHUNK], F32) if rope else None
        rest = sb("rest", [P, QK, CHUNK], F32)
        parts = sb("parts", [P, 2, QK, 3, CHUNK], BF16)
        vt = sb("vt", [P, 2, CT, D], F32)
        T = ctx.enter_context(nc.psum_tensor(f"{name}_T", [P, KD, CHUNK], F32))
        qk_ps = ctx.enter_context(nc.psum_tensor(f"{name}_qk", [P, QK, CHUNK], F32))
        v_ps = ctx.enter_context(nc.psum_tensor(f"{name}_v", [P, CT, D], F32))
        s = semaphores(nc, E, name, "ln_step", "ln_var", "ln_std", "xn_ready", "turned", "hi_ready", "lo_ready",
                       "qk_ready", "raw_ready", "swap_ready", "cos_ready", "sin_ready", "rope_ready", "p1_ready",
                       "r_ready", "p2_ready", "p3_ready", "v_ready", "vt_ready")
        parts_out = [new_semaphore(nc, E, f"{name}_parts_out{i}") for i in range(2)]
        v_out = [new_semaphore(nc, E, f"{name}_v_out{i}") for i in range(2)]
        q_ready = s["rope_ready"] if rope else s["raw_ready"]
        block = ctx.enter_context(nc.Block())

        @block.tensor
        def _(pe):
            turn(pe, E, T, 0, 0, s, True)

            def body(c, par, use, fresh, last):
                first = fresh and par == 0
                pe.wait_ge(s["hi_ready"], c * KD + KD)
                pe.wait_ge(s["lo_ready"], c * KD + KD)
                for i in range(QK):
                    w, half = (E.wq, E.wk)[i // KD], i % KD
                    if not first:
                        pe.wait_ge(s["raw_ready"], c * QK + i + 1 - QK)
                    for k in range(KD):
                        mm = three_pass(pe, qk_ps[:, i, :], pair(w, slice(None), k, slice(half * P, (half + 1) * P)),
                                        pair(E.xt, slice(None), par, k, slice(None)), k == 0, k == KD - 1)
                    mm.then_inc(s["qk_ready"], 1)
                if not last:
                    turn(pe, E, T, c + 1, 1 - par, s)
                for t in range(CT):
                    if t % 2 == 0 and not first:
                        pe.wait_ge(s["vt_ready"], c * 2 - 1 + t // 2)
                    for k in range(KD):
                        mm = three_pass(pe, v_ps[:, t, :], pair(E.xt, slice(None), par, k, slice(t * P, (t + 1) * P)),
                                        pair(E.wv, slice(None), k, slice(None)), k == 0, k == KD - 1)
                    if t % 2:
                        mm.then_inc(s["v_ready"], 1)

            each_chunk_of_pairs(pe, body)

        @block.scalar
        def _(act):
            norm_scales_scalar(act, E, s["ln_var"], s["ln_std"])
            part_hi(act, E, T, 0, 0, s)

            def body(c, par, use, fresh, last):
                first = fresh and par == 0
                for i in range(QK):
                    act.wait_ge(s["qk_ready"], c * QK + i + 1)
                    if not first:
                        act.wait_ge(s["rope_ready"] if rope else s["r_ready"], c * QK + i + 1 - QK)
                    scale = (1.0 / HD if rope else 0.25) if i < KD else 1.0
                    if rope:
                        ins = act.activation(raw[:, i, :], qk_ps[:, i, :], ACT.Copy, scale=scale)
                    else:
                        ins = act.activation(raw[:, i, :], qk_ps[:, i, :], ACT.Identity, scale=scale,
                                             bias=E.b_qk[:, i:i + 1])
                    ins.then_inc(s["raw_ready"], 1)
                if not last:
                    part_hi(act, E, T, c + 1, 1 - par, s)

            each_chunk_of_pairs(act, body)

        @block.gpsimd
        def _(p):
            def body(c, par, use, fresh, last):
                first = fresh and par == 0
                def times_cos(i):
                    n = c * QK + i
                    p.wait_ge(s["raw_ready"], n + 1)
                    if not first or i > 0:
                        p.wait_ge(s["rope_ready"], n)
                    p.tensor_tensor(cos_part[:, :], raw[:, i, :], E.cos[:, par, :], ALU.mult).then_inc(s["cos_ready"], 1)

                if rope:
                    times_cos(0)
                for i in range(QK):
                    n = c * QK + i
                    p.wait_ge(s["p1_ready"], n + 1)
                    if not first:
                        p.wait_ge(s["p3_ready"], n + 1 - QK)
                    p.tensor_tensor(rest[:, i, :], qf[:, i, :], parts[:, par, i, 0, :], ALU.subtract).then_inc(s["r_ready"], 1)
                    if rope and i + 1 < QK:
                        times_cos(i + 1)
                    p.wait_ge(s["p2_ready"], n + 1)
                    p.tensor_tensor(parts[:, par, i, 2, :], rest[:, i, :], parts[:, par, i, 1, :],
                                    ALU.subtract).then_inc(s["p3_ready"], 1)

            each_chunk_of_pairs(p, body)

        @block.vector
        def _(v):
            norm_scales_vector(v, E, s["ln_step"], s["ln_var"], s["ln_std"])
            normalise(v, E, 0, 0, s)
            part_lo(v, E, T, 0, 0, s)

            def body(c, par, use, fresh, last):
                first = fresh and par == 0
                if not fresh:
                    v.wait_ge(parts_out[par], use * (16 * QK))
                if not last:
                    if not first:
                        v.wait_ge(s["turned"], c * KD)
                    if rope:
                        v.wait_ge(s["raw_ready"], c * QK + 1)
                    normalise(v, E, c + 1, 1 - par, s)
                elif rope:
                    v.wait_ge(s["raw_ready"], c * QK + 1)

                def rotate(i):
                    n = c * QK + i
                    v.stream_shuffle(swapped[:, :], raw[:, i, :], [j ^ 1 for j in range(32)]).then_inc(s["swap_ready"], 1)
                    v.wait_ge(s["swap_ready"], n + 1)
                    v.tensor_tensor(swapped[:, :], swapped[:, :], E.sin[:, par, :], ALU.mult).then_inc(s["sin_ready"], 1)
                    v.wait_ge(s["sin_ready"], n + 1)
                    v.wait_ge(s["cos_ready"], n + 1)
                    if not first:
                        v.wait_ge(s["r_ready"], n + 1 - QK)
                    v.tensor_tensor(qf[:, i, :], swapped[:, :], cos_part[:, :], ALU.add).then_inc(s["rope_ready"], 1)

                def second(i):
                    v.wait_ge(s["r_ready"], c * QK + i + 1)
                    v.tensor_copy(parts[:, par, i, 1, :], rest[:, i, :]).then_inc(s["p2_ready"], 1)

                for i in range(QK):
                    if rope:
                        rotate(i)
                    if rope and i + 1 < QK:
                        v.wait_ge(s["raw_ready"], c * QK + i + 2)
                    v.wait_ge(q_ready, c * QK + i + 1)
                    v.tensor_copy(parts[:, par, i, 0, :], qf[:, i, :]).then_inc(s["p1_ready"], 1)
                    if i >= 1:
                        second(i - 1)
                second(QK - 1)
                if not last:
                    part_lo(v, E, T, c + 1, 1 - par, s)
                if not fresh:
                    v.wait_ge(v_out[par], use * 16)
                for q in range(2):
                    v.wait_ge(s["v_ready"], c * 2 + q + 1)
                    dst, src = vt[:, par, 2 * q:2 * q + 2, :], v_ps[:, 2 * q:2 * q + 2, :]
                    if rope:
                        ins = v.tensor_copy(dst, src)
                    else:
                        ins = v.tensor_tensor(dst, src, E.bv[:, :].unsqueeze(1).to_broadcast([P, 2, D]), ALU.add)
                    ins.then_inc(s["vt_ready"], 1)

            each_chunk_of_pairs(v, body)

        @block.sync
        def _(sp):
            def body(c, par, use, fresh, last):
                first = fresh and par == 0
                for i in range(QK):
                    sp.wait_ge(s["p3_ready"], c * QK + i + 1)
                    half = i % KD
                    dst = (E.q_dram, E.k_dram)[i // KD][:, half * P:(half + 1) * P, bass.ds(c * CHUNK, CHUNK)]
                    sp.dma_start(dst.rearrange("g p n -> p g n"), parts[:, par, i, :, :]).then_inc(parts_out[par], 16)
                sp.wait_ge(s["vt_ready"], c * 2 + 2)
                sp.dma_start(E.v_dram[bass.ds(c * CHUNK, CHUNK), :].rearrange("(t p) f -> p t f", p=P),
                             vt[:, par, :, :]).then_inc(v_out[par], 16)

            each_chunk_of_pairs(sp, body)
            for par in range(2):
                sp.wait_ge(parts_out[par], 16 * QK * CHUNKS // 2)
                sp.wait_ge(v_out[par], 16 * CHUNKS // 2)


def attention_stage(nc, E, name, causal):
    NORM_R = 1 if causal else 2
    with ExitStack() as ctx:
        def sb(n, shape, dt):
            return ctx.enter_context(nc.sbuf_tensor(f"{name}_{n}", shape, dt))

        def ps(n, shape):
            return ctx.enter_context(nc.psum_tensor(f"{name}_{n}", shape, F32))

        q_st = sb("q_st", [P, SETS, GH, S], BF16)
        k_st = sb("k_st", [P, SETS, GH, S], BF16)
        v_raw = sb("v_raw", [P, 2, QT, GH * HD], F32)
        v_st = sb("v_st", [P, 2, QT, GH, VW], F32)
        probs = sb("probs", [P, 2, GH, 512], F32)
        maxes = sb("maxes", [P, GH * QT, KC], F32)
        neg_max = sb("neg_max", [P, GH * QT], F32)
        m_rest = sb("m_rest", [GH * QT, P], F32)
        m_parts = sb("m_parts", [GH * QT, 2, 3, P], BF16)
        o_t = sb("o_t", [P, 512], F32)
        o_n = sb("o_n", [P, 4, GH, VW], F32)
        small = sb("small", [P, 8, 4, GH], F32)
        o_first = sb("o_first", [P, 4, GH, HD], F32)
        o_rest = sb("o_rest", [P, 4, GH, HD], F32)
        o_out = sb("o_out", [P, 4, GH, HD], F32)
        v_first = None if causal else sb("v_first", [P, 2, GH * HD], F32)
        key_mask = sb("key_mask", [P, QT, GH], F32)
        half = sb("half", [P, 4, GH], F32)
        s_max = ps("s_max", [P, 2, 512])
        s_exp = ps("s_exp", [P, 2, 2, 512])
        o_ps = ps("o_ps", [P, 512])
        t_ps = ps("t_ps", [P, 4, GH, VW])
        t_max = t_ps[0:GH * QT, 0, :, :].rearrange("p j r -> p (j r)")
        s = semaphores(nc, E, name, "v_ready", "sa_ready", "max_done", "nm_ready", "mt_done",
                       "mt_read", "m_step", "m_ready", "st_ready", "exp_done", "pv_done", "o_read", "o_turned",
                       "t_read", "z_ready", "z_inv", "o_step", "o_done", "constants", "clipped", "o_stored")
        staged = [new_semaphore(nc, E, f"{name}_staged{i}") for i in range(SETS)]
        v_in = [new_semaphore(nc, E, f"{name}_v_in{i}") for i in range(2)]
        f_in = [new_semaphore(nc, E, f"{name}_f_in{i}") for i in range(2)]
        m_in = [new_semaphore(nc, E, f"{name}_m_in{i}") for i in range(2)]
        block = ctx.enter_context(nc.Block())
        STAGE_DMAS = len(PARTS_Q) + len(PARTS_K)

        def pieces(step):
            return range(min(PACE * step, MAXES), min(PACE * (step + 1), MAXES))

        @block.sync
        def _(sp):
            def stage(it):
                for g, (pq, pk) in enumerate(zip(PARTS_Q, PARTS_K)):
                    for st, dram, part in ((q_st, E.q_dram, pq), (k_st, E.k_dram, pk)):
                        src = dram[part, it.hg * GH * HD:(it.hg + 1) * GH * HD, bass.ds(it.b * S, S)]
                        sp.dma_start(st[g * HD:(g + 1) * HD, it.set, :, :],
                                     src.rearrange("(j d) n -> d j n", d=HD)).then_inc(staged[it.set], 16)

            def stage_v(it):
                src = E.v_dram[bass.ds(it.b * S, S), it.hg * GH * HD:(it.hg + 1) * GH * HD]
                sp.dma_start(v_raw[:, it.par, :, :], src.rearrange("(t p) f -> p t f", p=P)).then_inc(v_in[it.par], 16)

            def stage_first(it):
                src = E.v_dram[bass.ds(it.b * S, 1), it.hg * GH * HD:(it.hg + 1) * GH * HD]
                sp.dma_start(v_first[:, it.par, :], src.to_broadcast([P, GH * HD])).then_inc(f_in[it.par], 16)

            def put_max(it):
                sp.wait_ge(s["m_ready"], it.n(1, 1))
                for part in range(MROWS):
                    dst = q_st[SROWS + part:SROWS + part + 1, it.set, :, :].rearrange("o j (t q) -> o (j t) q", q=P)
                    sp.dma_start(dst, m_parts[:, it.par, part, :]).then_inc(m_in[it.par], 16)

            def store(it, qc):
                sp.wait_ge(s["o_done"], it.n(2, qc + 1))
                rows = E.ao_dram[bass.ds(it.b * S + qc * 512, 512), it.hg * GH * HD:(it.hg + 1) * GH * HD]
                sp.dma_start(rows.rearrange("(t p) f -> p t f", p=P),
                             o_out[:, :, :, :].rearrange("p t j d -> p t (j d)")).then_inc(s["o_stored"], 16)

            start = It(0, 0)
            stage(start)
            stage_v(start)
            stage(start.ahead(1))
            stage_v(start.ahead(1))
            if not causal:
                stage_first(start)
                stage_first(start.ahead(1))
            stage(start.ahead(2))
            put_max(start)

            def body(it, first, last):
                left = ITERS - 1 - it.r if isinstance(it.k, int) else SETS
                if left >= 3:
                    if not first:
                        sp.wait_ge(s["st_ready"], it.n(2 * STEPS, 0))
                    stage(it.ahead(3))
                if left >= 2:
                    sp.wait_ge(s["v_ready"], it.n(1, 1))
                    stage_v(it.ahead(2))
                if not first:
                    store(it.ahead(-1), 1)
                    if not (causal or last):
                        stage_first(it.ahead(1))
                if not last:
                    put_max(it.ahead(1))
                store(it, 0)

            each_iteration(sp, body)
            store(It(0, ITERS - 1), 1)
            sp.wait_ge(s["o_stored"], 2 * 16 * ITERS)

        @block.tensor
        def _(pe):
            def max_piece(it, a, free):
                j, rest = divmod(a, QT * KC)
                qt, kc = divmod(rest, KC)
                if a == 0:
                    pe.wait_ge(staged[it.set], it.b * (16 * STAGE_DMAS) + 16 * STAGE_DMAS)
                if not free:
                    pe.wait_ge(s["max_done"], it.n(MAXES, a - 1))
                masked = causal and kc * 512 + 511 > qt * P
                mm = pe.matmul(s_max[:, a % 2, :], q_st[0:SROWS, it.set, j, qt * P:(qt + 1) * P],
                               k_st[0:SROWS, it.set, j, kc * 512:(kc + 1) * 512], start=True, stop=not masked)
                if masked:
                    at = S + kc * 512 - qt * P
                    mm = pe.matmul(s_max[:, a % 2, :], E.ident16[:, :], E.mask_q[:, at:at + 512], start=False, stop=True)
                mm.then_inc(s["sa_ready"], 1)

            def turn_max(it, first=False):
                pe.wait_ge(s["nm_ready"], it.n(1, 1))
                if not first:
                    pe.wait_ge(s["t_read"], it.n(2, -1))
                pe.transpose(t_max, neg_max[:, :], E.ident[:, :]).then_inc(s["mt_done"], 1)

            def scores(it, step, first):
                qc, kt = divmod(step, QT)
                for jp in range(2):
                    u = 2 * step + jp
                    if step == 0 and jp == 0:
                        pe.wait_ge(m_in[it.par], it.pair * (16 * MROWS) + 16 * MROWS)
                        pe.wait_ge(s["constants"], 1)
                    if not first or u >= 2:
                        pe.wait_ge(s["exp_done"], it.n(2 * STEPS, u - 1))
                    for jj in range(2):
                        j = 2 * jp + jj
                        masked = causal and kt * P + P - 1 > qc * 512
                        mm = pe.matmul(s_exp[:, jp, jj, :], k_st[0:SROWS + MROWS, it.set, j, kt * P:(kt + 1) * P],
                                       q_st[0:SROWS + MROWS, it.set, j, qc * 512:(qc + 1) * 512],
                                       start=True, stop=not masked)
                        if masked:
                            at = S + qc * 512 - kt * P
                            mm = pe.matmul(s_exp[:, jp, jj, :], E.ident16[:, :], E.mask_k[:, at:at + 512],
                                           start=False, stop=True)
                    mm.then_inc(s["st_ready"], 1)

            def values(it, step, first):
                qc, kt = divmod(step, QT)
                if step == 0:
                    pe.wait_ge(s["v_ready"], it.n(1, 1))
                pe.wait_ge(s["exp_done"], it.n(2 * STEPS, 2 * step + 2))
                if kt == 0 and not (first and qc == 0):
                    pe.wait_ge(s["o_read"], it.n(2, qc))
                for j in range(GH):
                    mm = pe.matmul(o_ps[j * VW:(j + 1) * VW, :], v_st[:, it.par, kt, j, :], probs[:, step % 2, j, :],
                                   start=kt == 0, stop=kt == QT - 1)
                mm.then_inc(s["pv_done"], 1)

            def turn_out(it, qc, first):
                pe.wait_ge(s["o_read"], it.n(2, qc + 1))
                pe.wait_ge(s["mt_read"], it.n(1, 1 + qc) if not (it.r == ITERS - 1 and qc) else ITERS)
                if not (first and qc == 0):
                    pe.wait_ge(s["t_read"], it.n(2, qc))
                for t in range(4):
                    mm = pe.transpose(t_ps[:, t, :, :].rearrange("p j r -> p (j r)"), o_t[:, t * P:(t + 1) * P],
                                      E.ident[:, :])
                mm.then_inc(s["o_turned"], 1)

            start = It(0, 0)
            for a in range(MAXES):
                max_piece(start, a, a < 2)
            turn_max(start, True)

            def body(it, first, last):
                for step in range(STEPS):
                    scores(it, step, first)
                    if not last:
                        for a in pieces(step):
                            max_piece(it.ahead(1), a, False)
                    if step > 0:
                        values(it, step - 1, first)
                    elif not first:
                        values(it.ahead(-1), STEPS - 1, False)
                    if step == 1 and not first:
                        turn_out(it.ahead(-1), 1, False)
                    if step == 9:
                        turn_out(it, 0, first)
                    if step == 14 and not last:
                        turn_max(it.ahead(1))

            each_iteration(pe, body)
            end = It(0, ITERS - 1)
            values(end, STEPS - 1, False)
            turn_out(end, 1, False)

        @block.scalar
        def _(act):
            def read_out(it, qc, first=False):
                act.wait_ge(s["pv_done"], it.n(STEPS, (qc + 1) * QT))
                if not (first and qc == 0):
                    act.wait_ge(s["o_turned"], it.n(2, qc))
                act.activation(o_t[:, :], o_ps[:, :], ACT.Copy).then_inc(s["o_read"], 1)

            def read_turned(it, qc, first=False):
                act.wait_ge(s["o_turned"], it.n(2, qc + 1))
                if not (first and qc == 0):
                    act.wait_ge(s["o_done"], it.n(2, qc))
                act.activation(o_n[:, :, :, :], t_ps[:, :, :, :], ACT.Copy).then_inc(s["t_read"], 1)

            def body(it, first, last):
                for step in range(STEPS):
                    for jp in range(2):
                        u = 2 * step + jp
                        act.wait_ge(s["st_ready"], it.n(2 * STEPS, u + 1))
                        if jp == 0 and (not first or step >= 2):
                            act.wait_ge(s["pv_done"], it.n(STEPS, step - 1))
                        act.activation(probs[:, step % 2, 2 * jp:2 * jp + 2, :], s_exp[:, jp, :, :],
                                       ACT.Exp).then_inc(s["exp_done"], 1)
                    if step == 0 and not first:
                        read_out(it.ahead(-1), 1)
                    if step == 2 and not first:
                        read_turned(it.ahead(-1), 1)
                    if step == 8:
                        read_out(it, 0, first)
                    if step == 10:
                        read_turned(it, 0, first)

            each_iteration(act, body)
            end = It(0, ITERS - 1)
            read_out(end, 1)
            read_turned(end, 1)

        @block.vector
        def _(v):
            def max_piece(it, a):
                v.wait_ge(s["sa_ready"], it.n(MAXES, a + 1))
                v.tensor_reduce(maxes[:, a // KC, a % KC:a % KC + 1], s_max[:, a % 2, :], AX.X,
                                ALU.max).then_inc(s["max_done"], 1)

            def whole_max(it):
                v.wait_ge(s["max_done"], it.n(MAXES, MAXES))
                v.tensor_reduce(neg_max[:, :], maxes[:, :, :], AX.X, ALU.max, negate=True).then_inc(s["nm_ready"], 1)

            def split_max(it, wait_slot):
                v.wait_ge(s["mt_done"], it.n(1, 1))
                if wait_slot:
                    v.wait_ge(m_in[it.par], it.pair * (16 * MROWS))
                p1, p2, p3 = (m_parts[:, it.par, i, :] for i in range(3))
                v.tensor_copy(p1, t_max).then_inc(s["m_step"], 1)
                v.wait_ge(s["m_step"], it.n(2, 1))
                v.tensor_tensor(m_rest[:, :], t_max, p1, ALU.subtract).then_inc(s["mt_read"], 1)
                v.wait_ge(s["mt_read"], it.n(1, 1))
                v.tensor_copy(p2, m_rest[:, :]).then_inc(s["m_step"], 1)
                v.wait_ge(s["m_step"], it.n(2, 2))
                v.tensor_tensor(p3, m_rest[:, :], p2, ALU.subtract).then_inc(s["m_ready"], 1)

            def invert(it, qc, i):
                if causal:
                    v.wait_ge(s["t_read"], it.n(2, qc + 1))
                else:
                    v.wait_ge(s["z_ready"], it.n(4, 2 * qc + i + 1))
                src = o_n[:, :, :, HD] if causal else small[:, 2 * i, :, :]
                if i == 1:
                    v.tensor_scalar(src, src, CLIP, None, ALU.max).then_inc(s["clipped"], 1)
                    v.wait_ge(s["clipped"], it.n(2, qc + 1))
                v.reciprocal(small[:, 2 * i + 1, :, :], src).then_inc(s["z_inv"], 1)

            start = It(0, 0)
            for a in range(MAXES):
                max_piece(start, a)
            whole_max(start)
            split_max(start, False)

            def body(it, first, last):
                nxt = it.ahead(1)
                for step in range(STEPS):
                    if not last:
                        for a in pieces(step):
                            max_piece(nxt, a)
                    if step in (4, 6)[:NORM_R] and not first:
                        invert(it.ahead(-1), 1, step // 2 - 2)
                if not last:
                    whole_max(nxt)
                    split_max(nxt, not first)
                for i in range(NORM_R):
                    invert(it, 0, i)

            each_iteration(v, body)
            for i in range(NORM_R):
                invert(It(0, ITERS - 1), 1, i)

        @block.gpsimd
        def _(p):
            fills = [(k_st[SROWS:SROWS + MROWS, :, :, :], 1.0), (v_st[:, :, :, :, :], 0.0), (key_mask[:, :, :], 1.0),
                     (half[:, :, :], 0.5), (v_st[:, :, :, :, HD:HD + 1], 1.0)]
            if not causal:
                fills += [(key_mask[0:1, 0, :], 0.0), (v_st[0:1, :, 0, :, HD:HD + 1], 0.0),
                          (v_st[0:1, :, 0, :, HD + 1:HD + 2], 1.0)]
            for n, (tile, value) in enumerate(fills):
                p.memset(tile, value).then_inc(s["constants"], 1)
                p.wait_ge(s["constants"], n + 1)

            def put_values(it, used):
                p.wait_ge(v_in[it.par], it.pair * 16 + 16)
                if used:
                    p.wait_ge(s["pv_done"], it.n(STEPS, -STEPS))
                p.tensor_tensor(v_st[:, it.par, :, :, 0:HD], v_raw[:, it.par, :, :].rearrange("p t (j d) -> p t j d", d=HD),
                                key_mask[:, :, :].unsqueeze(3).to_broadcast([P, QT, GH, HD]), ALU.mult).then_inc(s["v_ready"], 1)

            def normalise_out(it, qc, wait_slot):
                u = qc
                p.wait_ge(s["t_read"], it.n(2, u + 1))
                if wait_slot:
                    p.wait_ge(s["o_stored"], it.n(32, 16 * qc))
                rest, ones, one = o_n[:, :, :, 0:HD], o_n[:, :, :, HD], o_n[:, :, :, HD + 1]
                out = o_out[:, :, :, :]

                def wide(x):
                    return x.unsqueeze(3).to_broadcast([P, 4, GH, HD])

                if causal:
                    p.wait_ge(s["z_inv"], it.n(2, u + 1))
                    p.tensor_tensor(out, rest, wide(small[:, 1, :, :]), ALU.mult).then_inc(s["o_done"], 1)
                    return
                n = 0
                PER = 6

                def chain(ins):
                    nonlocal n
                    n += 1
                    ins.then_inc(s["o_step"], 1)
                    p.wait_ge(s["o_step"], it.n(2 * PER, u * PER + n))

                z, z_inv, share, share_inv, w_all, w_one, w_add, w_rest = (small[:, i, :, :] for i in range(8))
                p.tensor_tensor(z, ones, one, ALU.add).then_inc(s["z_ready"], 1)
                p.wait_ge(s["z_inv"], it.n(4, 2 * u + 1))
                p.tensor_tensor(share, ones, z_inv, ALU.mult).then_inc(s["z_ready"], 1)
                chain(p.tensor_tensor(w_all, z_inv, half[:, :, :], ALU.mult))
                chain(p.tensor_tensor(w_one, w_all, one, ALU.mult))
                if qc == 0:
                    p.wait_ge(f_in[it.par], it.pair * 16 + 16)
                fv = v_first[:, it.par, :].rearrange("p (j d) -> p j d", d=HD).unsqueeze(1).to_broadcast([P, 4, GH, HD])
                chain(p.tensor_tensor(o_first[:, :, :, :], fv, wide(w_one), ALU.mult))
                p.wait_ge(s["z_inv"], it.n(4, 2 * u + 2))
                chain(p.tensor_tensor(w_add, share_inv, w_all, ALU.mult))
                chain(p.tensor_tensor(w_rest, w_add, w_all, ALU.add))
                chain(p.tensor_tensor(o_rest[:, :, :, :], rest, wide(w_rest), ALU.mult))
                p.tensor_tensor(out, o_rest[:, :, :, :], o_first[:, :, :, :], ALU.add).then_inc(s["o_done"], 1)

            put_values(It(0, 0), False)

            def body(it, first, last):
                if not last:
                    put_values(it.ahead(1), not first)
                if not first:
                    normalise_out(it.ahead(-1), 1, True)
                normalise_out(it, 0, not first)

            each_iteration(p, body)
            normalise_out(It(0, ITERS - 1), 1, True)


def out_stage(nc, E, name):
    with ExitStack() as ctx:
        def sb(n, shape, dt):
            return ctx.enter_context(nc.sbuf_tensor(f"{name}_{n}", shape, dt))

        alloc_front(E, sb)
        acc = ctx.enter_context(nc.psum_tensor(f"{name}_acc", [P, 2, CT, D], F32))
        T = ctx.enter_context(nc.psum_tensor(f"{name}_T", [P, KD, CHUNK], F32))
        s = semaphores(nc, E, name, "turned", "hi_ready", "lo_ready", "out_done", "x_new", "x_sum")
        loaded = [new_semaphore(nc, E, f"{name}_in{i}") for i in range(2)]
        block = ctx.enter_context(nc.Block())

        @block.sync
        def _(sp):
            def body(c, par, use, fresh):
                if not fresh:
                    sp.wait_ge(s["turned"], c * KD - KD)
                sp.dma_start(E.xn[:, par, :, :], E.ao_dram[bass.ds(c * CHUNK, CHUNK), :].rearrange("(t p) f -> p t f", p=P))\
                    .then_inc(loaded[par], 16)

            each_chunk_of_two(sp, body)

        @block.tensor
        def _(pe):
            def turn_rows(c, par, use, first):
                pe.wait_ge(loaded[par], use * 16 + 16)
                if not first:
                    pe.wait_ge(s["hi_ready"], c * KD)
                    pe.wait_ge(s["lo_ready"], c * KD)
                for k in range(KD):
                    for t in range(CT):
                        mm = pe.transpose(T[:, k, t * P:(t + 1) * P], E.xn[:, par, t, k * P:(k + 1) * P], E.ident[:, :])
                    mm.then_inc(s["turned"], 1)

            def product(c, par, fresh):
                pe.wait_ge(s["hi_ready"], c * KD + KD)
                pe.wait_ge(s["lo_ready"], c * KD + KD)
                if not fresh:
                    pe.wait_ge(s["x_new"], c * 2 - 2)
                for t in range(CT):
                    for k in range(KD):
                        mm = three_pass(pe, acc[:, par, t, :], pair(E.xt, slice(None), par, k, slice(t * P, (t + 1) * P)),
                                        pair(E.wo, slice(None), k, slice(None)), k == 0, k == KD - 1)
                mm.then_inc(s["out_done"], 1)

            def body(c, par, use, fresh):
                turn_rows(c, par, use, fresh and par == 0)
                if not (fresh and par == 0):
                    product(c - 1, 1 - par, fresh)

            each_chunk_of_two(pe, body)
            product(CHUNKS - 1, 1, False)

        @block.scalar
        def _(act):
            def body(c, par, use, fresh):
                if not fresh:
                    act.wait_ge(s["out_done"], c - 1)
                part_hi(act, E, T, c, par, s)

            each_chunk_of_two(act, body)

        @block.vector
        def _(v):
            def finish(c, par):
                v.wait_ge(s["out_done"], c + 1)
                for q in range(2):
                    at = bass.ds(c * CT + 2 * q, 2)
                    v.tensor_tensor(E.x[:, at, :], acc[:, par, 2 * q:2 * q + 2, :], E.x[:, at, :], ALU.add).then_inc(s["x_sum"], 1)
                for q in range(2):
                    at = bass.ds(c * CT + 2 * q, 2)
                    v.wait_ge(s["x_sum"], c * 2 + q + 1)
                    v.tensor_tensor(E.x[:, at, :], E.x[:, at, :], E.bo[:, :].unsqueeze(1).to_broadcast([P, 2, D]),
                                    ALU.add).then_inc(s["x_new"], 1)
                v.wait_ge(s["x_new"], c * 2 + 2)
                statistics(v, E, c)

            def body(c, par, use, fresh):
                part_lo(v, E, T, c, par, s)
                if not (fresh and par == 0):
                    finish(c - 1, 1 - par)

            each_chunk_of_two(v, body)
            finish(CHUNKS - 1, 1)


def program(nc, io, out_dram):
    E = Env()
    E.semaphores = []
    with ExitStack() as ctx:
        def sb(n, shape, dt):
            return ctx.enter_context(nc.sbuf_tensor(n, shape, dt))

        E.q_dram = nc.dram_tensor("q_parts", [3, D, B * S], BF16)
        E.k_dram = nc.dram_tensor("k_parts", [3, D, B * S], BF16)
        E.v_dram = nc.dram_tensor("v_rows", [B * S, D], F32)
        E.ao_dram = nc.dram_tensor("attention_rows", [B * S, D], F32)
        E.x = sb("x", [P, TILES, D], F32)
        E.stats = sb("stats", [P, TILES, 6], F32)
        E.ident = sb("ident", [P, P], F32)

        def parts(stack, n, k, cols):
            return [stack.enter_context(nc.sbuf_tensor(f"{n}_{x}", [P, k, cols], F32R)) for x in ("hi", "lo")]

        with ExitStack() as layer:
            gate, up = parts(layer, "w_gate", KD, HID0), parts(layer, "w_up", KD, HID0)
            E.w_up, E.w_down = (gate, up), parts(layer, "w_down", HID0 // P, D)
            E.wq, E.wk, E.wv, E.wo = (parts(layer, f"w0{n}", KD, D) for n in "qkvo")
            b_raw = layer.enter_context(nc.sbuf_tensor("b_raw", [P, 2 * KD], F32))
            E.b_qk = layer.enter_context(nc.sbuf_tensor("b_qk", [P, 2 * KD], F32))
            E.bv = layer.enter_context(nc.sbuf_tensor("bv", [P, D], F32))
            E.bo = layer.enter_context(nc.sbuf_tensor("bo", [P, D], F32))

            def scale_small(v, s):
                v.wait_ge(s["small"], 16 * 5)
                v.tensor_scalar(E.b_qk[:, 0:KD], b_raw[:, 0:KD], 0.25, None, ALU.mult)
                v.tensor_copy(E.b_qk[:, KD:2 * KD], b_raw[:, KD:2 * KD])

            E.scale_small = scale_small
            load_stage(nc, E, "load0",
                       [(gate, io["gate_t"], KD, HID0, True), (up, io["up_t"], KD, HID0, True),
                        (E.w_down, io["down_t"], HID0 // P, D, True)],
                       [(w, io[f"w0{n}_t"], KD, D, False) for w, n in zip((E.wq, E.wk, E.wv, E.wo), "qkvo")],
                       [(E.ident[:, :], io["ident"]), (b_raw[:, 0:KD], io["bq"]), (b_raw[:, KD:2 * KD], io["bk"]),
                        (E.bv[:, :], io["bv"].partition_broadcast(P)), (E.bo[:, :], io["bo0"].partition_broadcast(P))],
                       io["x"])
            ffn_stage(nc, E, "ffn0a", True)
            qkv_stage(nc, E, "qkv0", False)
            attention_stage(nc, E, "att0", False)
            out_stage(nc, E, "out0")
            ffn_stage(nc, E, "ffn0b", True)
        clear_semaphores(nc, E)

        with ExitStack() as layer:
            E.w_up = (parts(layer, "w1", KD, HID1),)
            E.w_down = parts(layer, "w2", HID1 // P, D)
            E.wq, E.wk, E.wv, E.wo = (parts(layer, f"w1{n}", KD, D) for n in "qkvo")
            E.b1 = layer.enter_context(nc.sbuf_tensor("b1", [P, HID1 // P], F32))
            E.b2_half = layer.enter_context(nc.sbuf_tensor("b2_half", [P, D], F32))
            E.bo = layer.enter_context(nc.sbuf_tensor("bo1", [P, D], F32))
            b2 = layer.enter_context(nc.sbuf_tensor("b2", [P, D], F32))
            E.cos = layer.enter_context(nc.sbuf_tensor("cos", [P, S // CHUNK, CHUNK], F32))
            E.sin = layer.enter_context(nc.sbuf_tensor("sin", [P, S // CHUNK, CHUNK], F32))
            E.mask_q = layer.enter_context(nc.sbuf_tensor("mask_q", [P, 2 * S], F16))
            E.mask_k = layer.enter_context(nc.sbuf_tensor("mask_k", [P, 2 * S], F16))
            E.ident16 = layer.enter_context(nc.sbuf_tensor("ident16", [P, P], F16))

            def scale_small(v, s):
                v.wait_ge(s["small"], 16 * 8)
                v.tensor_scalar(E.b2_half[:, :], b2[:, :], 0.5, None, ALU.mult)

            E.scale_small = scale_small
            load_stage(nc, E, "load1",
                       [(E.w_up[0], io["w1"], KD, HID1, False), (E.w_down, io["w2"], HID1 // P, D, False)],
                       [(w, io[f"w1{n}_t"], KD, D, False) for w, n in zip((E.wq, E.wk, E.wv, E.wo), "qkvo")],
                       [(E.b1[:, :], io["b1"]), (b2[:, :], io["b2"].partition_broadcast(P)),
                        (E.bo[:, :], io["bo1"].partition_broadcast(P)), (E.cos[:, :, :], io["cos"]),
                        (E.sin[:, :, :], io["sin"]), (E.mask_q[:, :], io["mask_q"]), (E.mask_k[:, :], io["mask_k"]),
                        (E.ident16[:, :], io["ident16"])])
            ffn_stage(nc, E, "ffn1a", False)
            qkv_stage(nc, E, "qkv1", True)
            attention_stage(nc, E, "att1", True)
            out_stage(nc, E, "out1")
            ffn_stage(nc, E, "ffn1b", False, out_dram)


def shape_constants():
    import numpy as np

    p, c = np.arange(P)[:, None], np.arange(2 * S)[None, :] - S
    neg = np.float16(-10000.0)
    inv_freq = (np.float32(1.0) / np.float32(10000.0) ** (np.arange(0, HD, 2, dtype=np.float32) / np.float32(HD)))
    ang = (np.arange(S, dtype=np.float32)[:, None] * inv_freq.astype(np.float32)[None, :]).astype(np.float32)
    d = np.arange(P) % HD
    cos = np.cos(ang).astype(np.float32)[:, d // 2].T
    sin = np.sin(ang).astype(np.float32)[:, d // 2].T * np.where(d % 2, 1.0, -1.0).astype(np.float32)[:, None]
    return {
        "ident": np.eye(P, dtype=np.float32),
        "ident16": np.eye(P, dtype=np.float16),
        "mask_q": np.where(c > p, neg, np.float16(0)),
        "mask_k": np.where(c < p, neg, np.float16(0)),
        "cos": np.ascontiguousarray(cos.reshape(P, S // CHUNK, CHUNK)),
        "sin": np.ascontiguousarray(sin.astype(np.float32).reshape(P, S // CHUNK, CHUNK)),
    }


def kernel(**inputs):
    import numpy as np
    import concourse.bacc as bacc
    from concourse.bass_utils import run_bass_kernel_spmd

    a = {k: np.asarray(v) for k, v in inputs.items()}

    def columns(v):
        return np.ascontiguousarray(v.reshape(-1, P).T)

    arrays = {
        "x": np.ascontiguousarray(a["L0_attn_x"].reshape(B * S, D)),
        "gate_t": np.ascontiguousarray(a["L0_ffn_w_gate"].T),
        "up_t": np.ascontiguousarray(a["L0_ffn_w_up"].T),
        "down_t": np.ascontiguousarray(a["L0_ffn_w_down"].T),
        "bq": columns(a["L0_attn_bq"]), "bk": columns(a["L0_attn_bk"]),
        "bv": a["L0_attn_bv"], "bo0": a["L0_attn_bo"],
        "w1": a["L1_ffn_w1"], "w2": a["L1_ffn_w2"],
        "b1": columns(a["L1_ffn_b1"]), "b2": a["L1_ffn_b2"], "bo1": a["L1_attn_bo"],
    }
    for n in "qkvo":
        arrays[f"w0{n}_t"] = np.ascontiguousarray(a[f"L0_attn_W{n}"].T)
        arrays[f"w1{n}_t"] = np.ascontiguousarray(a[f"L1_attn_W{n}"].T)
    arrays.update(shape_constants())

    nc = bacc.Bacc("TRN2", target_bir_lowering=False, num_devices=1)
    io = {n: nc.dram_tensor(f"in_{n}", v.shape, mybir.dt.from_np(v.dtype), kind="ExternalInput").ap()
          for n, v in arrays.items()}
    out = nc.dram_tensor("out", (B * S, D), F32, kind="ExternalOutput").ap()
    program(nc, io, out)
    r = run_bass_kernel_spmd(nc, [{f"in_{n}": v for n, v in arrays.items()}], core_ids=[0])
    return r.results[0]["out"].reshape(B, S, D)
```

```python
from contextlib import ExitStack

import concourse.bass as bass
from concourse import mybir

F32 = mybir.dt.float32
F32R = mybir.dt.float32r
BF16 = mybir.dt.bfloat16
F16 = mybir.dt.float16
I32 = mybir.dt.int32
ALU = mybir.AluOpType
ACT = mybir.ActivationFunctionType
AX = mybir.AxisListType

P = 128
B, S, D = 4, 1024, 256
H, HD = 16, 16
TILES = B * S // P
CT = 4
CHUNK = CT * P
CHUNKS = TILES // CT
KD = D // P
HID0, HID1 = 768, 1024
EPS = 1e-5
DEQ = 1.0 / 127.0
LAMBDA = 0.5
CLIP = 1e-9
MASK = 10000.0
UNDERFLOW = 200.0
GH = 4
GROUPS = H // GH
ITERS = B * GROUPS
SETS = 4
PARTS_Q = (0, 0, 0, 1, 1, 2)
PARTS_K = (0, 1, 2, 0, 1, 0)
SROWS = HD * len(PARTS_Q)
MROWS = 3
QT = S // P
KC = S // 512
VW = 32


def each_chunk(eng, body):
    body(0, 0, 0, True, False)
    with eng.Fori(0, (CHUNKS - 2) // 2) as k:
        body(k * 2 + 1, 1, k, False, False)
        body(k * 2 + 2, 0, k + 1, False, False)
    body(CHUNKS - 1, 1, (CHUNKS - 1) // 2, False, True)


def each_chunk_of_two(eng, body):
    body(0, 0, 0, True)
    body(1, 1, 0, True)
    with eng.Fori(0, (CHUNKS - 2) // 2) as k:
        body(k * 2 + 2, 0, k + 1, False)
        body(k * 2 + 3, 1, k + 1, False)


def each_chunk_of_pairs(eng, body):
    body(0, 0, 0, True, False)
    body(1, 1, 0, True, False)
    with eng.Fori(0, (CHUNKS - 4) // 2) as k:
        body(k * 2 + 2, 0, k + 1, False, False)
        body(k * 2 + 3, 1, k + 1, False, False)
    body(CHUNKS - 2, 0, (CHUNKS - 2) // 2, False, False)
    body(CHUNKS - 1, 1, (CHUNKS - 2) // 2, False, True)


class It:

    def __init__(self, k, r):
        self.k, self.r = k, r
        self.b = k + r // GROUPS
        self.hg = r % GROUPS
        self.set = r % SETS
        self.par = r % 2
        self.pair = k * 2 + r // 2

    def n(self, mult, plus):
        return self.k * (4 * mult) + (self.r * mult + plus)

    def ahead(self, d):
        return It(self.k, self.r + d)

    @property
    def start(self):
        return isinstance(self.k, int) and self.r == 0

    @property
    def exists(self):
        return not isinstance(self.k, int) or 0 <= self.r < ITERS


def each_iteration(eng, body):
    body(It(0, 0), True, False)
    with eng.Fori(0, 3) as k:
        for r in range(1, 5):
            body(It(k, r), False, False)
    for n in range(13, ITERS):
        body(It(0, n), False, n == ITERS - 1)


class Env:
    pass


def three_pass(pe, out, left, right, first, last, skip=False):
    pe.matmul(out, left[0], right[1], start=first, stop=False, skip_group_check=skip)
    pe.matmul(out, left[1], right[0], start=False, stop=False, skip_group_check=skip)
    return pe.matmul(out, left[0], right[0], start=False, stop=last, skip_group_check=skip)


def pair(parts, *index):
    return parts[0][index], parts[1][index]


def alloc_norm(E, sb):
    E.mean, E.rstd = sb("ln_mean", [P, TILES], F32), sb("ln_rstd", [P, TILES], F32)
    E.ln_a, E.ln_b, E.ln_c = (sb(f"ln_{n}", [P, TILES], F32) for n in "abc")
    E.std = sb("ln_std", [P, TILES], F32)


def norm_scales_vector(v, E, ln_step, ln_var, ln_std):
    me, ve, mo, vo = (E.stats[:, :, i] for i in (1, 2, 4, 5))
    a, b, c = E.ln_a[:, :], E.ln_b[:, :], E.ln_c[:, :]
    n = 0

    def chain(ins):
        nonlocal n
        n += 1
        ins.then_inc(ln_step, 1)
        v.wait_ge(ln_step, n)

    chain(v.tensor_tensor(a, me, mo, ALU.add))
    chain(v.tensor_scalar(E.mean[:, :], a, 0.5, None, ALU.mult))
    chain(v.tensor_tensor(b, me, mo, ALU.subtract))
    chain(v.tensor_tensor(c, b, b, ALU.mult))
    chain(v.tensor_tensor(b, ve, vo, ALU.add))
    chain(v.tensor_scalar(a, b, 1.0 / D, EPS, ALU.mult, ALU.add))
    v.scalar_tensor_tensor(out=b, in0=c, scalar=0.25, in1=a, op0=ALU.mult, op1=ALU.add).then_inc(ln_var, 1)
    v.wait_ge(ln_std, 1)
    chain(v.reciprocal(a, E.std[:, :]))
    chain(v.tensor_tensor(c, b, a, ALU.mult))
    chain(v.tensor_tensor(a, c, E.std[:, :], ALU.add))
    chain(v.tensor_scalar(c, a, 0.5, None, ALU.mult))
    chain(v.reciprocal(E.rstd[:, :], c))


def norm_scales_scalar(act, E, ln_var, ln_std):
    act.wait_ge(ln_var, 1)
    act.activation(E.std[:, :], E.ln_b[:, :], ACT.Sqrt).then_inc(ln_std, 1)


def alloc_front(E, sb):
    E.xn = sb("xn", [P, 2, CT, D], F32)
    E.xt = [sb(f"xt_{n}", [P, 2, KD, CHUNK], F32R) for n in ("hi", "lo")]


def normalise(v, E, c, par, s):
    for t in range(CT):
        at = bass.ds(c * CT + t, 1)
        ins = v.tensor_scalar(E.xn[:, par, t:t + 1, :], E.x[:, at, :], E.mean[:, at], E.rstd[:, at],
                              ALU.subtract, ALU.mult)
    ins.then_inc(s["xn_ready"], 1)


def turn(pe, E, T, c, par, s, first=False):
    pe.wait_ge(s["xn_ready"], c + 1)
    if not first:
        pe.wait_ge(s["hi_ready"], c * KD)
        pe.wait_ge(s["lo_ready"], c * KD)
    for k in range(KD):
        for t in range(CT):
            mm = pe.transpose(T[:, k, t * P:(t + 1) * P], E.xn[:, par, t, k * P:(k + 1) * P], E.ident[:, :])
        mm.then_inc(s["turned"], 1)


def part_hi(act, E, T, c, par, s):
    for k in range(KD):
        act.wait_ge(s["turned"], c * KD + k + 1)
        act.activation(E.xt[0][:, par, k, :], T[:, k, :], ACT.Copy).then_inc(s["hi_ready"], 1)


def part_lo(v, E, T, c, par, s):
    for k in range(KD):
        v.wait_ge(s["hi_ready"], c * KD + k + 1)
        v.tensor_tensor(E.xt[1][:, par, k, :], T[:, k, :], E.xt[0][:, par, k, :].bitcast(F32),
                        ALU.subtract).then_inc(s["lo_ready"], 1)


def new_semaphore(nc, E, name):
    sem = nc.alloc_semaphore(name)
    E.semaphores.append(sem)
    return sem


def semaphores(nc, E, name, *names):
    return {n: new_semaphore(nc, E, f"{name}_{n}") for n in names}


def clear_semaphores(nc, E):
    nc.clear_and_free_semaphores(E.semaphores)
    nc.all_engine_barrier()
    E.semaphores = []


def statistics(v, E, c):
    for t in range(CT):
        ins = v.bn_stats(E.stats[:, bass.ds(c * CT + t, 1), :], E.x[:, bass.ds(c * CT + t, 1), :])
    return ins


def load_stage(nc, E, name, ffn, square, small, x_dram=None):
    with ExitStack() as ctx:
        def sb(n, shape, dt):
            return ctx.enter_context(nc.sbuf_tensor(f"{name}_{n}", shape, dt))

        s = semaphores(nc, E, name, "x", "small", "cast", "hi", "lo", "st", "scaled")
        jobs = ffn + square
        landed = [new_semaphore(nc, E, f"{name}_w{i}") for i in range(len(jobs))]
        raw = [sb(f"raw{i}", [P, k, n], I32 if whole else F32) for i, (_, _, k, n, whole) in enumerate(jobs)]
        val = [sb(f"val{i}", [P, k, n], F32) if whole else raw[i] for i, (_, _, k, n, whole) in enumerate(jobs)]
        casts = sum(j[4] for j in jobs)
        block = ctx.enter_context(nc.Block())

        @block.sync
        def _(sp):
            for i, (_, src, k, n, _) in enumerate(jobs):
                sp.dma_start(raw[i][:, :, :], src.rearrange("(k p) n -> p k n", p=P)).then_inc(landed[i], 16)
            for tile, src in small:
                sp.dma_start(tile, src).then_inc(s["small"], 16)
            if x_dram is not None:
                for c in range(CHUNKS):
                    sp.dma_start(E.x[:, c * CT:(c + 1) * CT, :],
                                 x_dram[c * CHUNK:(c + 1) * CHUNK, :].rearrange("(t p) f -> p t f", p=P)).then_inc(s["x"], 16)
                sp.wait_ge(s["x"], 16 * CHUNKS)
            sp.wait_ge(s["small"], 16 * len(small))

        @block.vector
        def _(v):
            cast = 0
            for i, (parts, _, k, n, whole) in enumerate(jobs):
                v.wait_ge(landed[i], 16)
                if whole:
                    v.tensor_copy(val[i][:, :, :], raw[i][:, :, :]).then_inc(s["cast"], 1)
                    cast += 1
                    v.wait_ge(s["cast"], cast)
                v.tensor_copy(parts[0][:, :, :], val[i][:, :, :]).then_inc(s["hi"], 1)
            if x_dram is not None:
                v.wait_ge(s["x"], 16 * CHUNKS)
                for c in range(CHUNKS):
                    statistics(v, E, c)
            E.scale_small(v, s)

        @block.gpsimd
        def _(p):
            for i, (parts, _, k, n, whole) in enumerate(jobs):
                p.wait_ge(s["hi"], i + 1)
                p.tensor_tensor(parts[1][:, :, :], val[i][:, :, :], parts[0][:, :, :].bitcast(F32),
                                ALU.subtract).then_inc(s["lo"], 1)


def ffn_stage(nc, E, name, gated, out_dram=None):
    F = (HID0 if gated else HID1) // P
    with ExitStack() as ctx:
        def sb(n, shape, dt):
            return ctx.enter_context(nc.sbuf_tensor(f"{name}_{n}", shape, dt))

        alloc_norm(E, sb)
        alloc_front(E, sb)
        h = sb("h", [P, 2, CHUNK], F32)
        h_parts = [sb(f"h_{n}", [P, 2, CHUNK], F32R) for n in ("hi", "lo")]
        gate_act = sb("gate_act", [P, 2, CHUNK], F32) if gated else None
        xb = None if gated else sb("xb", [P, 2, CT, D], F32)
        up_ps = ctx.enter_context(nc.psum_tensor(f"{name}_up", [P, 2, 2 if gated else 1, CHUNK], F32))
        acc = ctx.enter_context(nc.psum_tensor(f"{name}_acc", [P, CT, D], F32))
        T = ctx.enter_context(nc.psum_tensor(f"{name}_T", [P, KD, CHUNK], F32))
        s = semaphores(nc, E, name, "ln_step", "ln_var", "ln_std", "xn_ready", "turned", "hi_ready", "lo_ready",
                       "up_ready", "gate_ready", "h_ready", "h_hi", "h_lo", "down_done", "x_new", "xb_ready",
                       "stored")
        block = ctx.enter_context(nc.Block())
        used = s["h_ready"]

        @block.tensor
        def _(pe):
            def up(c, par, f, first):
                if f == 0:
                    pe.wait_ge(s["hi_ready"], c * KD + KD)
                    pe.wait_ge(s["lo_ready"], c * KD + KD)
                if not first or f >= 2:
                    pe.wait_ge(used, c * F + f - 1)
                cols = slice(f * P, (f + 1) * P)
                for g, w in enumerate(E.w_up):
                    for k in range(KD):
                        mm = three_pass(pe, up_ps[:, f % 2, g, :], pair(w, slice(None), k, cols),
                                        pair(E.xt, slice(None), par, k, slice(None)), k == 0, k == KD - 1)
                mm.then_inc(s["up_ready"], 1)

            def down(c, f, first):
                pe.wait_ge(s["h_hi"], c * F + f + 1)
                pe.wait_ge(s["h_lo"], c * F + f + 1)
                if f == 0 and not first:
                    pe.wait_ge(s["x_new"], c * 2)
                for t in range(CT):
                    mm = three_pass(pe, acc[:, t, :], pair(h_parts, slice(None), f % 2, slice(t * P, (t + 1) * P)),
                                    pair(E.w_down, slice(None), f, slice(None)), f == 0 and t % 2 == 0, f == F - 1, True)
                mm.then_inc(s["down_done"], 1)

            turn(pe, E, T, 0, 0, s, True)

            def body(c, par, use, first, last):
                for f in range(F):
                    up(c, par, f, first)
                    if f > 0:
                        down(c, f - 1, first)
                    elif not first:
                        down(c - 1, F - 1, False)
                    if f == 2 and not last:
                        turn(pe, E, T, c + 1, 1 - par, s)

            each_chunk(pe, body)
            down(CHUNKS - 1, F - 1, False)

        @block.scalar
        def _(act):
            norm_scales_scalar(act, E, s["ln_var"], s["ln_std"])
            part_hi(act, E, T, 0, 0, s)

            def body(c, par, use, first, last):
                for f in range(F):
                    act.wait_ge(s["up_ready"], c * F + f + 1)
                    if gated:
                        if not first or f >= 2:
                            act.wait_ge(s["h_ready"], c * F + f - 1)
                        act.activation(gate_act[:, f % 2, :], up_ps[:, f % 2, 0, :], ACT.Silu,
                                       scale=DEQ).then_inc(s["gate_ready"], 1)
                    else:
                        if not first or f >= 2:
                            act.wait_ge(s["h_lo"], c * F + f - 1)
                        act.activation(h[:, f % 2, :], up_ps[:, f % 2, 0, :], ACT.Gelu,
                                       bias=E.b1[:, f:f + 1]).then_inc(s["h_ready"], 1)
                    if f == 3 and not last:
                        part_hi(act, E, T, c + 1, 1 - par, s)

            each_chunk(act, body)

        @block.gpsimd
        def _(p):
            def add_bias(c, par):
                for t in range(CT):
                    ins = p.tensor_tensor(xb[:, par, t:t + 1, :], E.x[:, bass.ds(c * CT + t, 1), :],
                                          E.b2_half[:, :].unsqueeze(1), ALU.add)
                ins.then_inc(s["xb_ready"], 1)

            if not gated:
                add_bias(0, 0)

            def body(c, par, use, first, last):
                for f in range(F):
                    if f == F - 1 and not (gated or first or last):
                        p.wait_ge(s["x_new"], c * 2)
                    p.wait_ge(s["h_hi"], c * F + f + 1)
                    if not first or f >= 2:
                        p.wait_ge(s["down_done"], c * F + f - 1)
                    p.tensor_tensor(h_parts[1][:, f % 2, :], h[:, f % 2, :], h_parts[0][:, f % 2, :].bitcast(F32),
                                    ALU.subtract).then_inc(s["h_lo"], 1)
                if not (gated or last):
                    add_bias(c + 1, 1 - par)

            each_chunk(p, body)

        @block.vector
        def _(v):
            norm_scales_vector(v, E, s["ln_step"], s["ln_var"], s["ln_std"])
            normalise(v, E, 0, 0, s)
            part_lo(v, E, T, 0, 0, s)

            def finish(c, par):
                v.wait_ge(s["down_done"], c * F + F)
                if not gated:
                    v.wait_ge(s["xb_ready"], c + 1)
                for q in range(2):
                    at = bass.ds(c * CT + 2 * q, 2)
                    v.scalar_tensor_tensor(out=E.x[:, at, :], in0=acc[:, 2 * q:2 * q + 2, :],
                                           scalar=0.5 * DEQ if gated else 0.5,
                                           in1=E.x[:, at, :] if gated else xb[:, par, 2 * q:2 * q + 2, :],
                                           op0=ALU.mult, op1=ALU.add).then_inc(s["x_new"], 1)
                if out_dram is None:
                    v.wait_ge(s["x_new"], c * 2 + 2)
                    statistics(v, E, c)

            def body(c, par, use, first, last):
                if not last:
                    if not first:
                        v.wait_ge(s["turned"], c * KD)
                    normalise(v, E, c + 1, 1 - par, s)
                for f in range(F):
                    if gated:
                        v.wait_ge(s["gate_ready"], c * F + f + 1)
                        if not first or f >= 2:
                            v.wait_ge(s["h_lo"], c * F + f - 1)
                        v.scalar_tensor_tensor(out=h[:, f % 2, :], in0=up_ps[:, f % 2, 1, :], scalar=DEQ,
                                               in1=gate_act[:, f % 2, :], op0=ALU.mult, op1=ALU.mult).then_inc(s["h_ready"], 1)
                    v.wait_ge(s["h_ready"], c * F + f + 1)
                    if not first or f >= 2:
                        v.wait_ge(s["down_done"], c * F + f - 1)
                    v.tensor_copy(h_parts[0][:, f % 2, :], h[:, f % 2, :]).then_inc(s["h_hi"], 1)
                    if f == 1 and not first:
                        finish(c - 1, 1 - par)
                    if f == 3 and not last:
                        part_lo(v, E, T, c + 1, 1 - par, s)

            each_chunk(v, body)
            finish(CHUNKS - 1, (CHUNKS - 1) % 2)

        if out_dram is not None:
            @block.sync
            def _(sp):
                def body(c, par, use, first, last):
                    sp.wait_ge(s["x_new"], c * 2 + 2)
                    sp.dma_start(out_dram[bass.ds(c * CHUNK, CHUNK), :].rearrange("(t p) f -> p t f", p=P),
                                 E.x[:, bass.ds(c * CT, CT), :]).then_inc(s["stored"], 16)

                each_chunk(sp, body)
                sp.wait_ge(s["stored"], 16 * CHUNKS)


def qkv_stage(nc, E, name, rope):
    QK = 2 * KD
    with ExitStack() as ctx:
        def sb(n, shape, dt):
            return ctx.enter_context(nc.sbuf_tensor(f"{name}_{n}", shape, dt))

        alloc_norm(E, sb)
        alloc_front(E, sb)
        qf = sb("qf", [P, QK, CHUNK], F32)
        raw = sb("raw", [P, QK, CHUNK], F32) if rope else qf
        swapped = sb("swapped", [P, CHUNK], F32) if rope else None
        cos_part = sb("cos_part", [P, CHUNK], F32) if rope else None
        rest = sb("rest", [P, QK, CHUNK], F32)
        parts = sb("parts", [P, 2, QK, 3, CHUNK], BF16)
        vt = sb("vt", [P, 2, CT, D], F32)
        if rope:
            peaks = sb("peaks", [P, QK, CHUNKS], F32)
            peak = sb("peak", [P, 2], F32)
            peak_all = sb("peak_all", [P, 2], F32)
            peak_product = sb("peak_product", [1, 1], F32)
        T = ctx.enter_context(nc.psum_tensor(f"{name}_T", [P, KD, CHUNK], F32))
        qk_ps = ctx.enter_context(nc.psum_tensor(f"{name}_qk", [P, QK, CHUNK], F32))
        v_ps = ctx.enter_context(nc.psum_tensor(f"{name}_v", [P, CT, D], F32))
        s = semaphores(nc, E, name, "ln_step", "ln_var", "ln_std", "xn_ready", "turned", "hi_ready", "lo_ready",
                       "qk_ready", "raw_ready", "swap_ready", "cos_ready", "sin_ready", "rope_ready", "p1_ready",
                       "r_ready", "p2_ready", "p3_ready", "v_ready", "vt_ready", "peaks_ready", "peak_ready", "peak_all",
                       "peak_product")
        parts_out = [new_semaphore(nc, E, f"{name}_parts_out{i}") for i in range(2)]
        v_out = [new_semaphore(nc, E, f"{name}_v_out{i}") for i in range(2)]
        q_ready = s["rope_ready"] if rope else s["raw_ready"]
        block = ctx.enter_context(nc.Block())

        @block.tensor
        def _(pe):
            turn(pe, E, T, 0, 0, s, True)

            def body(c, par, use, fresh, last):
                first = fresh and par == 0
                pe.wait_ge(s["hi_ready"], c * KD + KD)
                pe.wait_ge(s["lo_ready"], c * KD + KD)
                for i in range(QK):
                    w, half = (E.wq, E.wk)[i // KD], i % KD
                    if not first:
                        pe.wait_ge(s["raw_ready"], c * QK + i + 1 - QK)
                    for k in range(KD):
                        mm = three_pass(pe, qk_ps[:, i, :], pair(w, slice(None), k, slice(half * P, (half + 1) * P)),
                                        pair(E.xt, slice(None), par, k, slice(None)), k == 0, k == KD - 1)
                    mm.then_inc(s["qk_ready"], 1)
                if not last:
                    turn(pe, E, T, c + 1, 1 - par, s)
                for t in range(CT):
                    if t % 2 == 0 and not first:
                        pe.wait_ge(s["vt_ready"], c * 2 - 1 + t // 2)
                    for k in range(KD):
                        mm = three_pass(pe, v_ps[:, t, :], pair(E.xt, slice(None), par, k, slice(t * P, (t + 1) * P)),
                                        pair(E.wv, slice(None), k, slice(None)), k == 0, k == KD - 1)
                    if t % 2:
                        mm.then_inc(s["v_ready"], 1)

            each_chunk_of_pairs(pe, body)

        @block.scalar
        def _(act):
            norm_scales_scalar(act, E, s["ln_var"], s["ln_std"])
            part_hi(act, E, T, 0, 0, s)

            def body(c, par, use, fresh, last):
                first = fresh and par == 0
                for i in range(QK):
                    act.wait_ge(s["qk_ready"], c * QK + i + 1)
                    if not first:
                        act.wait_ge(s["rope_ready"] if rope else s["r_ready"], c * QK + i + 1 - QK)
                    scale = (1.0 / HD if rope else 0.25) if i < KD else 1.0
                    if rope:
                        ins = act.activation(raw[:, i, :], qk_ps[:, i, :], ACT.Copy, scale=scale)
                    else:
                        ins = act.activation(raw[:, i, :], qk_ps[:, i, :], ACT.Identity, scale=scale,
                                             bias=E.b_qk[:, i:i + 1])
                    ins.then_inc(s["raw_ready"], 1)
                if not last:
                    part_hi(act, E, T, c + 1, 1 - par, s)

            each_chunk_of_pairs(act, body)

        @block.gpsimd
        def _(p):
            def body(c, par, use, fresh, last):
                first = fresh and par == 0
                def times_cos(i):
                    n = c * QK + i
                    p.wait_ge(s["raw_ready"], n + 1)
                    if not first or i > 0:
                        p.wait_ge(s["rope_ready"], n)
                    p.tensor_tensor(cos_part[:, :], raw[:, i, :], E.cos[:, par, :], ALU.mult).then_inc(s["cos_ready"], 1)

                if rope:
                    times_cos(0)
                for i in range(QK):
                    n = c * QK + i
                    p.wait_ge(s["p1_ready"], n + 1)
                    if not first:
                        p.wait_ge(s["p3_ready"], n + 1 - QK)
                    p.tensor_tensor(rest[:, i, :], qf[:, i, :], parts[:, par, i, 0, :], ALU.subtract).then_inc(s["r_ready"], 1)
                    if rope and i + 1 < QK:
                        times_cos(i + 1)
                    p.wait_ge(s["p2_ready"], n + 1)
                    p.tensor_tensor(parts[:, par, i, 2, :], rest[:, i, :], parts[:, par, i, 1, :],
                                    ALU.subtract).then_inc(s["p3_ready"], 1)

            each_chunk_of_pairs(p, body)
            if rope:
                p.wait_ge(s["peak_ready"], 1)
                p.partition_all_reduce(peak_all[:, :], peak[:, :], P, bass.bass_isa.ReduceOp.max).then_inc(s["peak_all"], 1)

        @block.vector
        def _(v):
            norm_scales_vector(v, E, s["ln_step"], s["ln_var"], s["ln_std"])
            normalise(v, E, 0, 0, s)
            part_lo(v, E, T, 0, 0, s)

            def body(c, par, use, fresh, last):
                first = fresh and par == 0
                if not fresh:
                    v.wait_ge(parts_out[par], use * (16 * QK))
                if not last:
                    if not first:
                        v.wait_ge(s["turned"], c * KD)
                    if rope:
                        v.wait_ge(s["raw_ready"], c * QK + 1)
                    normalise(v, E, c + 1, 1 - par, s)
                elif rope:
                    v.wait_ge(s["raw_ready"], c * QK + 1)

                def rotate(i):
                    n = c * QK + i
                    v.stream_shuffle(swapped[:, :], raw[:, i, :], [j ^ 1 for j in range(32)]).then_inc(s["swap_ready"], 1)
                    v.wait_ge(s["swap_ready"], n + 1)
                    v.tensor_tensor(swapped[:, :], swapped[:, :], E.sin[:, par, :], ALU.mult).then_inc(s["sin_ready"], 1)
                    v.wait_ge(s["sin_ready"], n + 1)
                    v.wait_ge(s["cos_ready"], n + 1)
                    if not first:
                        v.wait_ge(s["r_ready"], n + 1 - QK)
                    v.tensor_tensor(qf[:, i, :], swapped[:, :], cos_part[:, :], ALU.add).then_inc(s["rope_ready"], 1)

                def second(i):
                    v.wait_ge(s["r_ready"], c * QK + i + 1)
                    v.tensor_copy(parts[:, par, i, 1, :], rest[:, i, :]).then_inc(s["p2_ready"], 1)

                for i in range(QK):
                    if rope:
                        rotate(i)
                    if rope and i + 1 < QK:
                        v.wait_ge(s["raw_ready"], c * QK + i + 2)
                    v.wait_ge(q_ready, c * QK + i + 1)
                    v.tensor_copy(parts[:, par, i, 0, :], qf[:, i, :]).then_inc(s["p1_ready"], 1)
                    if rope:
                        v.tensor_reduce(peaks[:, i, bass.ds(c, 1)], qf[:, i, :], AX.X, ALU.max,
                                        apply_absolute_value=True).then_inc(s["peaks_ready"], 1)
                    if i >= 1:
                        second(i - 1)
                second(QK - 1)
                if not last:
                    part_lo(v, E, T, c + 1, 1 - par, s)
                if not fresh:
                    v.wait_ge(v_out[par], use * 16)
                for q in range(2):
                    v.wait_ge(s["v_ready"], c * 2 + q + 1)
                    dst, src = vt[:, par, 2 * q:2 * q + 2, :], v_ps[:, 2 * q:2 * q + 2, :]
                    if rope:
                        ins = v.tensor_copy(dst, src)
                    else:
                        ins = v.tensor_tensor(dst, src, E.bv[:, :].unsqueeze(1).to_broadcast([P, 2, D]), ALU.add)
                    ins.then_inc(s["vt_ready"], 1)

            each_chunk_of_pairs(v, body)
            if rope:
                v.wait_ge(s["peaks_ready"], QK * CHUNKS)
                v.tensor_reduce(peak[:, :], peaks[:, :, :].rearrange("p (a k) c -> p a (k c)", a=2), AX.X,
                                ALU.max).then_inc(s["peak_ready"], 1)
                v.wait_ge(s["peak_all"], 1)
                v.tensor_tensor(peak_product[:, :], peak_all[0:1, 0:1], peak_all[0:1, 1:2], ALU.mult).then_inc(s["peak_product"], 1)
                v.wait_ge(s["peak_product"], 1)
                v.tensor_scalar(E.outweighed[:, :], peak_product[:, :], (MASK - UNDERFLOW) / (2 * HD), None, ALU.is_lt)

        @block.sync
        def _(sp):
            def body(c, par, use, fresh, last):
                first = fresh and par == 0
                for i in range(QK):
                    sp.wait_ge(s["p3_ready"], c * QK + i + 1)
                    half = i % KD
                    dst = (E.q_dram, E.k_dram)[i // KD][:, half * P:(half + 1) * P, bass.ds(c * CHUNK, CHUNK)]
                    sp.dma_start(dst.rearrange("g p n -> p g n"), parts[:, par, i, :, :]).then_inc(parts_out[par], 16)
                sp.wait_ge(s["vt_ready"], c * 2 + 2)
                sp.dma_start(E.v_dram[bass.ds(c * CHUNK, CHUNK), :].rearrange("(t p) f -> p t f", p=P),
                             vt[:, par, :, :]).then_inc(v_out[par], 16)

            each_chunk_of_pairs(sp, body)
            for par in range(2):
                sp.wait_ge(parts_out[par], 16 * QK * CHUNKS // 2)
                sp.wait_ge(v_out[par], 16 * CHUNKS // 2)


SLOTS = 4
TURN_AFTER = 2


class Plan:

    def __init__(self, masked, below, slack):
        self.masked, self.below = masked, below
        self.steps, units = [], []
        for qc in range(KC):
            unit = []
            for j in range(GH):
                for qt in range(4 * qc, 4 * qc + 4):
                    for kc in range(KC):
                        keys = min(512, (qt + 1) * P - kc * 512) if below else 512
                        if keys > 0:
                            unit.append((qc, j, qt, kc, keys))
            units.append(unit)
            for kt in range(QT):
                q0 = max(0, kt * P - qc * 512) if below else 0
                if q0 < 512:
                    self.steps.append((qc, kt, q0))
        n = len(units[0])
        self.pieces = units[0] + units[1][:TURN_AFTER] + [(0, None)] + units[1][TURN_AFTER:] + [(1, None)]
        self.end = [n - 1, len(self.pieces) - 2]
        self.turn = [n + TURN_AFTER, len(self.pieces) - 1]
        self.NS, self.NP = len(self.steps), len(self.pieces)
        self.begin = [next(i for i, x in enumerate(self.steps) if x[0] == qc) for qc in range(KC)] + [self.NS]
        cost_s = [512 - q0 for _, _, q0 in self.steps]
        cost_p = [x[4] + 64 if x[1] is not None else (256, 768)[x[0]] for x in self.pieces]
        all_s, all_p = sum(cost_s), sum(cost_p)
        total = all_s * all_p * SLOTS
        at_s = [sum(cost_s[:i]) * all_p * SLOTS for i in range(self.NS + 1)]
        at_p = [sum(cost_p[:i + 1]) * all_s * SLOTS for i in range(self.NP)]
        lead = max(at_p[self.turn[qc]] - at_s[self.begin[qc]] for qc in range(KC)) + int(slack * total)

        def between(low, high):
            return [(d, a) for d in range(3) for a in range(self.NP) if low < at_p[a] + d * total <= high]

        self.start = between(-1, lead)
        self.feed = [between(lead + at_s[i] + (at_s[i + 1] - at_s[i]) * n // SLOTS,
                             lead + at_s[i] + (at_s[i + 1] - at_s[i]) * (n + 1) // SLOTS)
                     for i in range(self.NS) for n in range(SLOTS)]

    def later(self, a, by):
        return [(qc, (self.turn[qc] + by) // self.NP) for qc in range(KC) if (self.turn[qc] + by) % self.NP == a]


def attention_stage(nc, E, name, causal):
    NORM_R = 1 if causal else 2
    UROWS = GH * 4
    with ExitStack() as ctx:
        def sb(n, shape, dt):
            return ctx.enter_context(nc.sbuf_tensor(f"{name}_{n}", shape, dt))

        def ps(n, shape):
            return ctx.enter_context(nc.psum_tensor(f"{name}_{n}", shape, F32))

        q_st = sb("q_st", [P, SETS, KC, GH, 512], BF16)
        k_st = sb("k_st", [P, SETS, GH, S], BF16)
        v_raw = sb("v_raw", [P, 2, QT, GH * HD], F32)
        v_st = sb("v_st", [P, 2, QT, GH, VW], F32)
        probs = sb("probs", [P, 2, GH, 512], F32)
        maxes = sb("maxes", [P, KC * UROWS, KC], F32)
        neg_max = sb("neg_max", [P, KC * UROWS], F32)
        m_turned = sb("m_turned", [KC * UROWS, P], F32)
        m_rest = sb("m_rest", [KC * UROWS, P], F32)
        m_parts = sb("m_parts", [KC * UROWS, KC, 3, P], BF16)
        o_t = sb("o_t", [P, 512], F32)
        o_n = sb("o_n", [P, 4, GH, VW], F32)
        small = sb("small", [P, 8, 4, GH], F32)
        o_first = sb("o_first", [P, 4, GH, HD], F32)
        o_rest = sb("o_rest", [P, 4, GH, HD], F32)
        o_out = sb("o_out", [P, 4, GH, HD], F32)
        v_first = None if causal else sb("v_first", [P, 2, GH * HD], F32)
        key_mask = sb("key_mask", [P, QT, GH], F32)
        half = sb("half", [P, 4, GH], F32)
        s_max = ps("s_max", [P, 2, 512])
        s_exp = ps("s_exp", [P, 2, 2, 512])
        o_ps = ps("o_ps", [P, 512])
        t_ps = ps("t_ps", [P, 4, GH, VW])
        s = semaphores(nc, E, name, "v_ready", "sa_ready", "max_done", "nm_ready", "m_step", "m_ready", "st_ready", "exp_done", "pv_done", "o_read", "o_turned",
                       "t_read", "z_ready", "z_inv", "o_step", "o_done", "constants", "nm_zero", "clipped", "o_stored")
        staged = [new_semaphore(nc, E, f"{name}_staged{i}") for i in range(SETS)]
        v_in = [new_semaphore(nc, E, f"{name}_v_in{i}") for i in range(2)]
        f_in = [new_semaphore(nc, E, f"{name}_f_in{i}") for i in range(2)]
        m_in = [new_semaphore(nc, E, f"{name}_m_in{i}") for i in range(KC)]
        block = ctx.enter_context(nc.Block())
        STAGE_DMAS = len(PARTS_Q) * KC + len(PARTS_K)
        general = Plan(causal, False, 3 / 16)
        below = Plan(True, True, 4 / 16) if causal else None

        def choose(eng, path):
            if not causal:
                path(general)
                return
            outweighed = eng.value_load(E.outweighed[0:1, 0:1])
            with eng.If(outweighed > 0):
                path(below)
            with eng.Else():
                path(general)

        @block.sync
        def _(sp):
            def path(plan):
                NS, NP = plan.NS, plan.NP

                def stage(it):
                    for g, (pq, pk) in enumerate(zip(PARTS_Q, PARTS_K)):
                        heads = slice(it.hg * GH * HD, (it.hg + 1) * GH * HD)
                        for qc in range(KC):
                            src = E.q_dram[pq, heads, bass.ds(it.b * S + qc * 512, 512)]
                            sp.dma_start(q_st[g * HD:(g + 1) * HD, it.set, qc, :, :],
                                         src.rearrange("(j d) n -> d j n", d=HD)).then_inc(staged[it.set], 16)
                        src = E.k_dram[pk, heads, bass.ds(it.b * S, S)]
                        sp.dma_start(k_st[g * HD:(g + 1) * HD, it.set, :, :],
                                     src.rearrange("(j d) n -> d j n", d=HD)).then_inc(staged[it.set], 16)

                def stage_v(it):
                    src = E.v_dram[bass.ds(it.b * S, S), it.hg * GH * HD:(it.hg + 1) * GH * HD]
                    sp.dma_start(v_raw[:, it.par, :, :], src.rearrange("(t p) f -> p t f", p=P)).then_inc(v_in[it.par], 16)

                def stage_first(it):
                    src = E.v_dram[bass.ds(it.b * S, 1), it.hg * GH * HD:(it.hg + 1) * GH * HD]
                    sp.dma_start(v_first[:, it.par, :], src.to_broadcast([P, GH * HD])).then_inc(f_in[it.par], 16)

                def put_max(it, qc):
                    sp.wait_ge(s["m_ready"], it.n(2, qc + 1))
                    for part in range(MROWS):
                        dst = q_st[SROWS + part:SROWS + part + 1, it.set, qc, :, :].rearrange("o j (t q) -> o (j t) q", q=P)
                        sp.dma_start(dst, m_parts[qc * UROWS:(qc + 1) * UROWS, qc, part, :]).then_inc(m_in[qc], 16)

                def store(it, qc):
                    sp.wait_ge(s["o_done"], it.n(2, qc + 1))
                    rows = E.ao_dram[bass.ds(it.b * S + qc * 512, 512), it.hg * GH * HD:(it.hg + 1) * GH * HD]
                    sp.dma_start(rows.rearrange("(t p) f -> p t f", p=P),
                                 o_out[:, :, :, :].rearrange("p t j d -> p t (j d)")).then_inc(s["o_stored"], 16)

                start = It(0, 0)
                stage(start)
                stage_v(start)
                stage(start.ahead(1))
                stage_v(start.ahead(1))
                if not causal:
                    stage_first(start)
                    stage_first(start.ahead(1))
                stage(start.ahead(2))
                put_max(start, 0)

                def body(it, first, last):
                    left = ITERS - 1 - it.r if isinstance(it.k, int) else SETS
                    if left >= 3:
                        if not first:
                            sp.wait_ge(s["st_ready"], it.n(2 * NS, 0))
                        stage(it.ahead(3))
                    if left >= 2:
                        sp.wait_ge(s["v_ready"], it.n(1, 1))
                        stage_v(it.ahead(2))
                    put_max(it, 1)
                    if not first:
                        store(it.ahead(-1), 1)
                        if not (causal or last):
                            stage_first(it.ahead(1))
                    store(it, 0)
                    if not last:
                        put_max(it.ahead(1), 0)

                each_iteration(sp, body)
                store(It(0, ITERS - 1), 1)
                sp.wait_ge(s["o_stored"], 2 * 16 * ITERS)

            choose(sp, path)

        @block.tensor
        def _(pe):
            def path(plan):
                NS, NP = plan.NS, plan.NP

                def max_piece(it, a, free):
                    if a == 0:
                        pe.wait_ge(staged[it.set], it.b * (16 * STAGE_DMAS) + 16 * STAGE_DMAS)
                    if not free:
                        pe.wait_ge(s["max_done"], it.n(NP, a - 1))
                    if a in plan.turn:
                        turn_max(it, plan.pieces[a][0], a)
                        return
                    qc, j, qt, kc, keys = plan.pieces[a]
                    masked = plan.masked and kc * 512 + keys - 1 > qt * P
                    row = (qt - 4 * qc) * P
                    mm = pe.matmul(s_max[:, a % 2, 0:keys], q_st[0:SROWS, it.set, qc, j, row:row + P],
                                   k_st[0:SROWS, it.set, j, kc * 512:kc * 512 + keys], start=True, stop=not masked)
                    if masked:
                        k0 = keys - P if plan.below else 0
                        at = S + kc * 512 + k0 - qt * P
                        mm = pe.matmul(s_max[:, a % 2, k0:keys], E.ident16[:, :], E.mask_q[:, at:at + keys - k0],
                                       start=False, stop=True)
                    mm.then_inc(s["sa_ready"], 1)

                def turn_max(it, qc, a):
                    pe.wait_ge(s["nm_ready"], it.n(2, qc + 1))
                    if it.start and qc == 0:
                        pe.wait_ge(s["nm_zero"], 1)
                    pe.transpose(s_max[0:KC * UROWS, a % 2, 0:P], neg_max[:, :], E.ident[:, :]).then_inc(s["sa_ready"], 1)

                def feed(it, pieces):
                    for d, a in pieces:
                        if it.ahead(d).exists:
                            max_piece(it.ahead(d), a, it.ahead(d).start and a < 2)

                def scores(it, step, jp, first):
                    qc, kt, q0 = plan.steps[step]
                    u = 2 * step + jp
                    if step in plan.begin and jp == 0:
                        pe.wait_ge(m_in[qc], it.n(16 * MROWS, 16 * MROWS))
                        pe.wait_ge(s["constants"], 1)
                    if not first or u >= 2:
                        pe.wait_ge(s["exp_done"], it.n(2 * NS, u - 1))
                    masked = plan.masked and kt * P + P - 1 > qc * 512 + q0
                    for jj in range(2):
                        j = 2 * jp + jj
                        mm = pe.matmul(s_exp[:, jp, jj, q0:512], k_st[0:SROWS + MROWS, it.set, j, kt * P:(kt + 1) * P],
                                       q_st[0:SROWS + MROWS, it.set, qc, j, q0:512], start=True, stop=not masked)
                        if masked:
                            q1 = q0 + P if plan.below else 512
                            at = S + qc * 512 + q0 - kt * P
                            mm = pe.matmul(s_exp[:, jp, jj, q0:q1], E.ident16[:, :], E.mask_k[:, at:at + q1 - q0],
                                           start=False, stop=True)
                    mm.then_inc(s["st_ready"], 1)

                def values(it, step, first):
                    qc, kt, q0 = plan.steps[step]
                    if step == 0:
                        pe.wait_ge(s["v_ready"], it.n(1, 1))
                    pe.wait_ge(s["exp_done"], it.n(2 * NS, 2 * step + 2))
                    if kt == 0 and not (first and qc == 0):
                        pe.wait_ge(s["o_read"], it.n(2, qc))
                    for j in range(GH):
                        mm = pe.matmul(o_ps[j * VW:(j + 1) * VW, q0:512], v_st[:, it.par, kt, j, :], probs[:, step % 2, j, q0:512],
                                       start=kt == 0, stop=step + 1 in plan.begin, skip_group_check=True)
                    mm.then_inc(s["pv_done"], 1)

                def turn_out(it, qc, first):
                    pe.wait_ge(s["o_read"], it.n(2, qc + 1))
                    if not (first and qc == 0):
                        pe.wait_ge(s["t_read"], it.n(2, qc))
                    for t in range(4):
                        mm = pe.transpose(t_ps[:, t, :, :].rearrange("p j r -> p (j r)"), o_t[:, t * P:(t + 1) * P],
                                          E.ident[:, :])
                    mm.then_inc(s["o_turned"], 1)

                feed(It(0, 0), plan.start)

                def body(it, first, last):
                    for step in range(NS):
                        slots = plan.feed[step * SLOTS:(step + 1) * SLOTS]
                        feed(it, slots[0])
                        scores(it, step, 0, first)
                        feed(it, slots[1])
                        scores(it, step, 1, first)
                        feed(it, slots[2])
                        if step > 0:
                            values(it, step - 1, first)
                        elif not first:
                            values(it.ahead(-1), NS - 1, False)
                        if step == 1 and not first:
                            turn_out(it.ahead(-1), 1, False)
                        if step == plan.begin[1] + 1:
                            turn_out(it, 0, first)
                        feed(it, slots[3])

                each_iteration(pe, body)
                end = It(0, ITERS - 1)
                values(end, NS - 1, False)
                turn_out(end, 1, False)

            choose(pe, path)

        @block.scalar
        def _(act):
            def path(plan):
                NS, NP = plan.NS, plan.NP

                def read_out(it, qc, first=False):
                    act.wait_ge(s["pv_done"], it.n(NS, plan.begin[qc + 1]))
                    if not (first and qc == 0):
                        act.wait_ge(s["o_turned"], it.n(2, qc))
                    act.activation(o_t[:, :], o_ps[:, :], ACT.Copy).then_inc(s["o_read"], 1)

                def read_turned(it, qc, first=False):
                    act.wait_ge(s["o_turned"], it.n(2, qc + 1))
                    if not (first and qc == 0):
                        act.wait_ge(s["o_done"], it.n(2, qc))
                    act.activation(o_n[:, :, :, :], t_ps[:, :, :, :], ACT.Copy).then_inc(s["t_read"], 1)

                def body(it, first, last):
                    for step in range(NS):
                        q0 = plan.steps[step][2]
                        for jp in range(2):
                            u = 2 * step + jp
                            act.wait_ge(s["st_ready"], it.n(2 * NS, u + 1))
                            if jp == 0 and (not first or step >= 2):
                                act.wait_ge(s["pv_done"], it.n(NS, step - 1))
                            act.activation(probs[:, step % 2, 2 * jp:2 * jp + 2, q0:512], s_exp[:, jp, :, q0:512],
                                           ACT.Exp).then_inc(s["exp_done"], 1)
                        if step == 0 and not first:
                            read_out(it.ahead(-1), 1)
                        if step == 2 and not first:
                            read_turned(it.ahead(-1), 1)
                        if step == plan.begin[1]:
                            read_out(it, 0, first)
                        if step == plan.begin[1] + 2:
                            read_turned(it, 0, first)

                each_iteration(act, body)
                end = It(0, ITERS - 1)
                read_out(end, 1)
                read_turned(end, 1)

            choose(act, path)

        @block.vector
        def _(v):
            v.memset(neg_max[:, :], 0.0).then_inc(s["nm_zero"], 1)
            v.wait_ge(s["nm_zero"], 1)

            def path(plan):
                NS, NP = plan.NS, plan.NP

                def max_piece(it, a):
                    v.wait_ge(s["sa_ready"], it.n(NP, a + 1))
                    if a in plan.turn:
                        v.tensor_copy(m_turned[:, :], s_max[0:KC * UROWS, a % 2, 0:P]).then_inc(s["max_done"], 1)
                        return
                    qc, j, qt, kc, keys = plan.pieces[a]
                    row = qc * UROWS + j * 4 + qt - 4 * qc
                    v.tensor_reduce(maxes[:, row, kc:kc + 1], s_max[:, a % 2, 0:keys], AX.X,
                                    ALU.max).then_inc(s["max_done"], 1)
                    if a == plan.end[qc]:
                        v.wait_ge(s["max_done"], it.n(NP, a + 1))
                        rows = slice(qc * UROWS, (qc + 1) * UROWS)
                        chunks = qc + 1 if plan.below else KC
                        v.tensor_reduce(neg_max[:, rows], maxes[:, rows, 0:chunks], AX.X, ALU.max,
                                        negate=True).then_inc(s["nm_ready"], 1)

                def split_max(it, qc, i):
                    p1, p2, p3 = (m_parts[:, qc, part, :] for part in range(3))
                    if i == 0:
                        v.wait_ge(s["max_done"], it.n(NP, plan.turn[qc] + 1))
                        if not it.start:
                            v.wait_ge(m_in[qc], it.n(16 * MROWS, 0))
                        v.tensor_copy(p1, m_turned[:, :]).then_inc(s["m_step"], 1)
                    elif i == 1:
                        v.wait_ge(s["m_step"], it.n(6, 3 * qc + 1))
                        v.tensor_tensor(m_rest[:, :], m_turned[:, :], p1, ALU.subtract).then_inc(s["m_step"], 1)
                    elif i == 2:
                        v.wait_ge(s["m_step"], it.n(6, 3 * qc + 2))
                        v.tensor_copy(p2, m_rest[:, :]).then_inc(s["m_step"], 1)
                    else:
                        v.wait_ge(s["m_step"], it.n(6, 3 * qc + 3))
                        v.tensor_tensor(p3, m_rest[:, :], p2, ALU.subtract).then_inc(s["m_ready"], 1)

                def feed(it, pieces):
                    for d, a in pieces:
                        if it.ahead(d).exists:
                            max_piece(it.ahead(d), a)
                        for i in range(4):
                            for qc, back in plan.later(a, i):
                                if it.ahead(d - back).exists:
                                    split_max(it.ahead(d - back), qc, i)

                def invert(it, qc, i):
                    if causal:
                        v.wait_ge(s["t_read"], it.n(2, qc + 1))
                    else:
                        v.wait_ge(s["z_ready"], it.n(4, 2 * qc + i + 1))
                    src = o_n[:, :, :, HD] if causal else small[:, 2 * i, :, :]
                    if i == 1:
                        v.tensor_scalar(src, src, CLIP, None, ALU.max).then_inc(s["clipped"], 1)
                        v.wait_ge(s["clipped"], it.n(2, qc + 1))
                    v.reciprocal(small[:, 2 * i + 1, :, :], src).then_inc(s["z_inv"], 1)

                feed(It(0, 0), plan.start)

                def body(it, first, last):
                    for step in range(NS):
                        for slot in plan.feed[step * SLOTS:(step + 1) * SLOTS]:
                            feed(it, slot)
                        for i in range(NORM_R):
                            if step == 3 + 2 * i and not first:
                                invert(it.ahead(-1), 1, i)
                            if step == plan.begin[1] + 3 + 2 * i:
                                invert(it, 0, i)

                each_iteration(v, body)
                for i in range(NORM_R):
                    invert(It(0, ITERS - 1), 1, i)

            choose(v, path)

        @block.gpsimd
        def _(p):
            fills = [(k_st[SROWS:SROWS + MROWS, :, :, :], 1.0), (v_st[:, :, :, :, :], 0.0), (key_mask[:, :, :], 1.0),
                     (half[:, :, :], 0.5), (v_st[:, :, :, :, HD:HD + 1], 1.0)]
            if not causal:
                fills += [(key_mask[0:1, 0, :], 0.0), (v_st[0:1, :, 0, :, HD:HD + 1], 0.0),
                          (v_st[0:1, :, 0, :, HD + 1:HD + 2], 1.0)]
            for n, (tile, value) in enumerate(fills):
                p.memset(tile, value).then_inc(s["constants"], 1)
                p.wait_ge(s["constants"], n + 1)

            def path(plan):
                NS, NP = plan.NS, plan.NP

                def put_values(it, used):
                    p.wait_ge(v_in[it.par], it.pair * 16 + 16)
                    if used:
                        p.wait_ge(s["pv_done"], it.n(NS, -NS))
                    p.tensor_tensor(v_st[:, it.par, :, :, 0:HD], v_raw[:, it.par, :, :].rearrange("p t (j d) -> p t j d", d=HD),
                                    key_mask[:, :, :].unsqueeze(3).to_broadcast([P, QT, GH, HD]), ALU.mult).then_inc(s["v_ready"], 1)

                def normalise_out(it, qc, wait_slot):
                    u = qc
                    p.wait_ge(s["t_read"], it.n(2, u + 1))
                    if wait_slot:
                        p.wait_ge(s["o_stored"], it.n(32, 16 * qc))
                    rest, ones, one = o_n[:, :, :, 0:HD], o_n[:, :, :, HD], o_n[:, :, :, HD + 1]
                    out = o_out[:, :, :, :]

                    def wide(x):
                        return x.unsqueeze(3).to_broadcast([P, 4, GH, HD])

                    if causal:
                        p.wait_ge(s["z_inv"], it.n(2, u + 1))
                        p.tensor_tensor(out, rest, wide(small[:, 1, :, :]), ALU.mult).then_inc(s["o_done"], 1)
                        return
                    n = 0
                    PER = 6

                    def chain(ins):
                        nonlocal n
                        n += 1
                        ins.then_inc(s["o_step"], 1)
                        p.wait_ge(s["o_step"], it.n(2 * PER, u * PER + n))

                    z, z_inv, share, share_inv, w_all, w_one, w_add, w_rest = (small[:, i, :, :] for i in range(8))
                    p.tensor_tensor(z, ones, one, ALU.add).then_inc(s["z_ready"], 1)
                    p.wait_ge(s["z_inv"], it.n(4, 2 * u + 1))
                    p.tensor_tensor(share, ones, z_inv, ALU.mult).then_inc(s["z_ready"], 1)
                    chain(p.tensor_tensor(w_all, z_inv, half[:, :, :], ALU.mult))
                    chain(p.tensor_tensor(w_one, w_all, one, ALU.mult))
                    if qc == 0:
                        p.wait_ge(f_in[it.par], it.pair * 16 + 16)
                    fv = v_first[:, it.par, :].rearrange("p (j d) -> p j d", d=HD).unsqueeze(1).to_broadcast([P, 4, GH, HD])
                    chain(p.tensor_tensor(o_first[:, :, :, :], fv, wide(w_one), ALU.mult))
                    p.wait_ge(s["z_inv"], it.n(4, 2 * u + 2))
                    chain(p.tensor_tensor(w_add, share_inv, w_all, ALU.mult))
                    chain(p.tensor_tensor(w_rest, w_add, w_all, ALU.add))
                    chain(p.tensor_tensor(o_rest[:, :, :, :], rest, wide(w_rest), ALU.mult))
                    p.tensor_tensor(out, o_rest[:, :, :, :], o_first[:, :, :, :], ALU.add).then_inc(s["o_done"], 1)

                put_values(It(0, 0), False)

                def body(it, first, last):
                    if not last:
                        put_values(it.ahead(1), not first)
                    if not first:
                        normalise_out(it.ahead(-1), 1, True)
                    normalise_out(it, 0, not first)

                each_iteration(p, body)
                normalise_out(It(0, ITERS - 1), 1, True)

            choose(p, path)


def out_stage(nc, E, name):
    with ExitStack() as ctx:
        def sb(n, shape, dt):
            return ctx.enter_context(nc.sbuf_tensor(f"{name}_{n}", shape, dt))

        alloc_front(E, sb)
        acc = ctx.enter_context(nc.psum_tensor(f"{name}_acc", [P, 2, CT, D], F32))
        T = ctx.enter_context(nc.psum_tensor(f"{name}_T", [P, KD, CHUNK], F32))
        s = semaphores(nc, E, name, "turned", "hi_ready", "lo_ready", "out_done", "x_new", "x_sum")
        loaded = [new_semaphore(nc, E, f"{name}_in{i}") for i in range(2)]
        block = ctx.enter_context(nc.Block())

        @block.sync
        def _(sp):
            def body(c, par, use, fresh):
                if not fresh:
                    sp.wait_ge(s["turned"], c * KD - KD)
                sp.dma_start(E.xn[:, par, :, :], E.ao_dram[bass.ds(c * CHUNK, CHUNK), :].rearrange("(t p) f -> p t f", p=P))\
                    .then_inc(loaded[par], 16)

            each_chunk_of_two(sp, body)

        @block.tensor
        def _(pe):
            def turn_rows(c, par, use, first):
                pe.wait_ge(loaded[par], use * 16 + 16)
                if not first:
                    pe.wait_ge(s["hi_ready"], c * KD)
                    pe.wait_ge(s["lo_ready"], c * KD)
                for k in range(KD):
                    for t in range(CT):
                        mm = pe.transpose(T[:, k, t * P:(t + 1) * P], E.xn[:, par, t, k * P:(k + 1) * P], E.ident[:, :])
                    mm.then_inc(s["turned"], 1)

            def product(c, par, fresh):
                pe.wait_ge(s["hi_ready"], c * KD + KD)
                pe.wait_ge(s["lo_ready"], c * KD + KD)
                if not fresh:
                    pe.wait_ge(s["x_new"], c * 2 - 2)
                for t in range(CT):
                    for k in range(KD):
                        mm = three_pass(pe, acc[:, par, t, :], pair(E.xt, slice(None), par, k, slice(t * P, (t + 1) * P)),
                                        pair(E.wo, slice(None), k, slice(None)), k == 0, k == KD - 1)
                mm.then_inc(s["out_done"], 1)

            def body(c, par, use, fresh):
                turn_rows(c, par, use, fresh and par == 0)
                if not (fresh and par == 0):
                    product(c - 1, 1 - par, fresh)

            each_chunk_of_two(pe, body)
            product(CHUNKS - 1, 1, False)

        @block.scalar
        def _(act):
            def body(c, par, use, fresh):
                if not fresh:
                    act.wait_ge(s["out_done"], c - 1)
                part_hi(act, E, T, c, par, s)

            each_chunk_of_two(act, body)

        @block.vector
        def _(v):
            def finish(c, par):
                v.wait_ge(s["out_done"], c + 1)
                for q in range(2):
                    at = bass.ds(c * CT + 2 * q, 2)
                    v.tensor_tensor(E.x[:, at, :], acc[:, par, 2 * q:2 * q + 2, :], E.x[:, at, :], ALU.add).then_inc(s["x_sum"], 1)
                for q in range(2):
                    at = bass.ds(c * CT + 2 * q, 2)
                    v.wait_ge(s["x_sum"], c * 2 + q + 1)
                    v.tensor_tensor(E.x[:, at, :], E.x[:, at, :], E.bo[:, :].unsqueeze(1).to_broadcast([P, 2, D]),
                                    ALU.add).then_inc(s["x_new"], 1)
                v.wait_ge(s["x_new"], c * 2 + 2)
                statistics(v, E, c)

            def body(c, par, use, fresh):
                part_lo(v, E, T, c, par, s)
                if not (fresh and par == 0):
                    finish(c - 1, 1 - par)

            each_chunk_of_two(v, body)
            finish(CHUNKS - 1, 1)


def program(nc, io, out_dram):
    E = Env()
    E.semaphores = []
    with ExitStack() as ctx:
        def sb(n, shape, dt):
            return ctx.enter_context(nc.sbuf_tensor(n, shape, dt))

        E.q_dram = nc.dram_tensor("q_parts", [3, D, B * S], BF16)
        E.k_dram = nc.dram_tensor("k_parts", [3, D, B * S], BF16)
        E.v_dram = nc.dram_tensor("v_rows", [B * S, D], F32)
        E.ao_dram = nc.dram_tensor("attention_rows", [B * S, D], F32)
        E.x = sb("x", [P, TILES, D], F32)
        E.stats = sb("stats", [P, TILES, 6], F32)
        E.ident = sb("ident", [P, P], F32)

        def parts(stack, n, k, cols):
            return [stack.enter_context(nc.sbuf_tensor(f"{n}_{x}", [P, k, cols], F32R)) for x in ("hi", "lo")]

        with ExitStack() as layer:
            gate, up = parts(layer, "w_gate", KD, HID0), parts(layer, "w_up", KD, HID0)
            E.w_up, E.w_down = (gate, up), parts(layer, "w_down", HID0 // P, D)
            E.wq, E.wk, E.wv, E.wo = (parts(layer, f"w0{n}", KD, D) for n in "qkvo")
            b_raw = layer.enter_context(nc.sbuf_tensor("b_raw", [P, 2 * KD], F32))
            E.b_qk = layer.enter_context(nc.sbuf_tensor("b_qk", [P, 2 * KD], F32))
            E.bv = layer.enter_context(nc.sbuf_tensor("bv", [P, D], F32))
            E.bo = layer.enter_context(nc.sbuf_tensor("bo", [P, D], F32))

            def scale_small(v, s):
                v.wait_ge(s["small"], 16 * 5)
                v.tensor_scalar(E.b_qk[:, 0:KD], b_raw[:, 0:KD], 0.25, None, ALU.mult)
                v.tensor_copy(E.b_qk[:, KD:2 * KD], b_raw[:, KD:2 * KD])

            E.scale_small = scale_small
            load_stage(nc, E, "load0",
                       [(gate, io["gate_t"], KD, HID0, True), (up, io["up_t"], KD, HID0, True),
                        (E.w_down, io["down_t"], HID0 // P, D, True)],
                       [(w, io[f"w0{n}_t"], KD, D, False) for w, n in zip((E.wq, E.wk, E.wv, E.wo), "qkvo")],
                       [(E.ident[:, :], io["ident"]), (b_raw[:, 0:KD], io["bq"]), (b_raw[:, KD:2 * KD], io["bk"]),
                        (E.bv[:, :], io["bv"].partition_broadcast(P)), (E.bo[:, :], io["bo0"].partition_broadcast(P))],
                       io["x"])
            ffn_stage(nc, E, "ffn0a", True)
            qkv_stage(nc, E, "qkv0", False)
            attention_stage(nc, E, "att0", False)
            out_stage(nc, E, "out0")
            ffn_stage(nc, E, "ffn0b", True)
        clear_semaphores(nc, E)

        with ExitStack() as layer:
            E.w_up = (parts(layer, "w1", KD, HID1),)
            E.w_down = parts(layer, "w2", HID1 // P, D)
            E.wq, E.wk, E.wv, E.wo = (parts(layer, f"w1{n}", KD, D) for n in "qkvo")
            E.b1 = layer.enter_context(nc.sbuf_tensor("b1", [P, HID1 // P], F32))
            E.b2_half = layer.enter_context(nc.sbuf_tensor("b2_half", [P, D], F32))
            E.bo = layer.enter_context(nc.sbuf_tensor("bo1", [P, D], F32))
            b2 = layer.enter_context(nc.sbuf_tensor("b2", [P, D], F32))
            E.cos = layer.enter_context(nc.sbuf_tensor("cos", [P, S // CHUNK, CHUNK], F32))
            E.sin = layer.enter_context(nc.sbuf_tensor("sin", [P, S // CHUNK, CHUNK], F32))
            E.mask_q = layer.enter_context(nc.sbuf_tensor("mask_q", [P, 2 * S], F16))
            E.mask_k = layer.enter_context(nc.sbuf_tensor("mask_k", [P, 2 * S], F16))
            E.outweighed = layer.enter_context(nc.sbuf_tensor("outweighed", [1, 1], I32))
            E.ident16 = layer.enter_context(nc.sbuf_tensor("ident16", [P, P], F16))

            def scale_small(v, s):
                v.wait_ge(s["small"], 16 * 8)
                v.tensor_scalar(E.b2_half[:, :], b2[:, :], 0.5, None, ALU.mult)

            E.scale_small = scale_small
            load_stage(nc, E, "load1",
                       [(E.w_up[0], io["w1"], KD, HID1, False), (E.w_down, io["w2"], HID1 // P, D, False)],
                       [(w, io[f"w1{n}_t"], KD, D, False) for w, n in zip((E.wq, E.wk, E.wv, E.wo), "qkvo")],
                       [(E.b1[:, :], io["b1"]), (b2[:, :], io["b2"].partition_broadcast(P)),
                        (E.bo[:, :], io["bo1"].partition_broadcast(P)), (E.cos[:, :, :], io["cos"]),
                        (E.sin[:, :, :], io["sin"]), (E.mask_q[:, :], io["mask_q"]), (E.mask_k[:, :], io["mask_k"]),
                        (E.ident16[:, :], io["ident16"])])
            ffn_stage(nc, E, "ffn1a", False)
            qkv_stage(nc, E, "qkv1", True)
            attention_stage(nc, E, "att1", True)
            out_stage(nc, E, "out1")
            ffn_stage(nc, E, "ffn1b", False, out_dram)


def shape_constants():
    import numpy as np

    p, c = np.arange(P)[:, None], np.arange(2 * S)[None, :] - S
    neg = np.float16(-MASK)
    inv_freq = (np.float32(1.0) / np.float32(10000.0) ** (np.arange(0, HD, 2, dtype=np.float32) / np.float32(HD)))
    ang = (np.arange(S, dtype=np.float32)[:, None] * inv_freq.astype(np.float32)[None, :]).astype(np.float32)
    d = np.arange(P) % HD
    cos = np.cos(ang).astype(np.float32)[:, d // 2].T
    sin = np.sin(ang).astype(np.float32)[:, d // 2].T * np.where(d % 2, 1.0, -1.0).astype(np.float32)[:, None]
    return {
        "ident": np.eye(P, dtype=np.float32),
        "ident16": np.eye(P, dtype=np.float16),
        "mask_q": np.where(c > p, neg, np.float16(0)),
        "mask_k": np.where(c < p, neg, np.float16(0)),
        "cos": np.ascontiguousarray(cos.reshape(P, S // CHUNK, CHUNK)),
        "sin": np.ascontiguousarray(sin.astype(np.float32).reshape(P, S // CHUNK, CHUNK)),
    }


def kernel(**inputs):
    import numpy as np
    import concourse.bacc as bacc
    from concourse.bass_utils import run_bass_kernel_spmd

    a = {k: np.asarray(v) for k, v in inputs.items()}

    def columns(v):
        return np.ascontiguousarray(v.reshape(-1, P).T)

    arrays = {
        "x": np.ascontiguousarray(a["L0_attn_x"].reshape(B * S, D)),
        "gate_t": np.ascontiguousarray(a["L0_ffn_w_gate"].T),
        "up_t": np.ascontiguousarray(a["L0_ffn_w_up"].T),
        "down_t": np.ascontiguousarray(a["L0_ffn_w_down"].T),
        "bq": columns(a["L0_attn_bq"]), "bk": columns(a["L0_attn_bk"]),
        "bv": a["L0_attn_bv"], "bo0": a["L0_attn_bo"],
        "w1": a["L1_ffn_w1"], "w2": a["L1_ffn_w2"],
        "b1": columns(a["L1_ffn_b1"]), "b2": a["L1_ffn_b2"], "bo1": a["L1_attn_bo"],
    }
    for n in "qkvo":
        arrays[f"w0{n}_t"] = np.ascontiguousarray(a[f"L0_attn_W{n}"].T)
        arrays[f"w1{n}_t"] = np.ascontiguousarray(a[f"L1_attn_W{n}"].T)
    arrays.update(shape_constants())

    nc = bacc.Bacc("TRN2", target_bir_lowering=False, num_devices=1)
    io = {n: nc.dram_tensor(f"in_{n}", v.shape, mybir.dt.from_np(v.dtype), kind="ExternalInput").ap()
          for n, v in arrays.items()}
    out = nc.dram_tensor("out", (B * S, D), F32, kind="ExternalOutput").ap()
    program(nc, io, out)
    r = run_bass_kernel_spmd(nc, [{f"in_{n}": v for n, v in arrays.items()}], core_ids=[0])
    return r.results[0]["out"].reshape(B, S, D)
```

```python
from contextlib import ExitStack

import concourse.bass as bass
from concourse import mybir

F32 = mybir.dt.float32
F32R = mybir.dt.float32r
BF16 = mybir.dt.bfloat16
F16 = mybir.dt.float16
I32 = mybir.dt.int32
ALU = mybir.AluOpType
ACT = mybir.ActivationFunctionType
AX = mybir.AxisListType

P = 128
B, S, D = 4, 1024, 256
H, HD = 16, 16
TILES = B * S // P
CT = 4
CHUNK = CT * P
CHUNKS = TILES // CT
KD = D // P
HID0, HID1 = 768, 1024
EPS = 1e-5
DEQ = 1.0 / 127.0
LAMBDA = 0.5
CLIP = 1e-9
MASK = 10000.0
UNDERFLOW = 200.0
GH = 4
GROUPS = H // GH
ITERS = B * GROUPS
SETS = 4
PARTS_Q = (0, 0, 0, 1, 1, 2)
PARTS_K = (0, 1, 2, 0, 1, 0)
SROWS = HD * len(PARTS_Q)
MROWS = 3
QT = S // P
KC = S // 512
VW = 32


def each_chunk(eng, body):
    body(0, 0, 0, True, False)
    with eng.Fori(0, (CHUNKS - 2) // 2) as k:
        body(k * 2 + 1, 1, k, False, False)
        body(k * 2 + 2, 0, k + 1, False, False)
    body(CHUNKS - 1, 1, (CHUNKS - 1) // 2, False, True)


def each_chunk_of_two(eng, body):
    body(0, 0, 0, True)
    body(1, 1, 0, True)
    with eng.Fori(0, (CHUNKS - 2) // 2) as k:
        body(k * 2 + 2, 0, k + 1, False)
        body(k * 2 + 3, 1, k + 1, False)


def each_chunk_lagged(eng, body):
    for c in range(3):
        body(c, c % 2, c // 2, False)
    with eng.Fori(0, (CHUNKS - 4) // 2) as k:
        body(k * 2 + 3, 1, k + 1, False)
        body(k * 2 + 4, 0, k + 2, False)
    body(CHUNKS - 1, 1, (CHUNKS - 1) // 2, True)


class It:

    def __init__(self, k, r):
        self.k, self.r = k, r
        self.b = k + r // GROUPS
        self.hg = r % GROUPS
        self.set = r % SETS
        self.par = r % 2
        self.pair = k * 2 + r // 2

    def n(self, mult, plus):
        return self.k * (4 * mult) + (self.r * mult + plus)

    def ahead(self, d):
        return It(self.k, self.r + d)

    @property
    def start(self):
        return isinstance(self.k, int) and self.r == 0

    @property
    def exists(self):
        return not isinstance(self.k, int) or 0 <= self.r < ITERS


def each_iteration(eng, body):
    body(It(0, 0), True, False)
    with eng.Fori(0, 3) as k:
        for r in range(1, 5):
            body(It(k, r), False, False)
    for n in range(13, ITERS):
        body(It(0, n), False, n == ITERS - 1)


class Env:
    pass


def three_pass(pe, out, left, right, first, last, skip=False, whole=None):
    if whole != 1:
        pe.matmul(out, left[0], right[1], start=first, stop=False, skip_group_check=skip)
    if whole != 0:
        pe.matmul(out, left[1], right[0], start=first and whole == 1, stop=False, skip_group_check=skip)
    return pe.matmul(out, left[0], right[0], start=False, stop=last, skip_group_check=skip)


def pair(parts, *index):
    return parts[0][index], parts[1][index]


def alloc_front(nc, E, ctx, name):
    def sb(n, shape, dt):
        return ctx.enter_context(nc.sbuf_tensor(f"{name}_{n}", shape, dt))

    E.mean, E.rstd = sb("ln_mean", [P, TILES], F32), sb("ln_rstd", [P, TILES], F32)
    E.ln_a, E.ln_b, E.ln_c = (sb(f"ln_{n}", [P, TILES], F32) for n in "abc")
    E.std = sb("ln_std", [P, TILES], F32)
    E.xn = sb("xn", [P, 2, CT, D], F32)
    E.xt = [sb(f"xt_{n}", [P, 2, KD, CHUNK], F32R) for n in ("hi", "lo")]
    E.counts = sb("counts", [1, 4], F32)


ALL = slice(0, TILES)
NORM_STEPS = 6
NEXT = slice(0, CT)


def norm_variance(v, E, step, var, at, n=0):
    me, ve, mo, vo = (E.stats[:, at, i] for i in (1, 2, 4, 5))
    a, b, c = E.ln_a[:, at], E.ln_b[:, at], E.ln_c[:, at]
    before = n

    def chain(ins):
        nonlocal n
        n += 1
        ins.then_inc(step, 1)
        v.wait_ge(step, n)

    chain(v.tensor_tensor(b, me, mo, ALU.subtract))
    chain(v.tensor_tensor(c, b, b, ALU.mult))
    chain(v.tensor_tensor(b, ve, vo, ALU.add))
    chain(v.tensor_scalar(a, b, 1.0 / D, EPS, ALU.mult, ALU.add))
    v.scalar_tensor_tensor(out=b, in0=c, scalar=0.25, in1=a, op0=ALU.mult, op1=ALU.add).then_inc(var, 1)
    v.wait_ge(var, 1)
    chain(v.tensor_tensor(c, me, mo, ALU.add))
    chain(v.tensor_scalar(E.mean[:, at], c, 0.5, None, ALU.mult))
    assert n - before == NORM_STEPS
    return n


def norm_rstd(v, E, step, std, at, n):
    a, b, c = E.ln_a[:, at], E.ln_b[:, at], E.ln_c[:, at]

    def chain(ins):
        nonlocal n
        n += 1
        ins.then_inc(step, 1)
        v.wait_ge(step, n)

    v.wait_ge(std, 1)
    chain(v.reciprocal(a, E.std[:, at]))
    chain(v.tensor_tensor(c, b, a, ALU.mult))
    chain(v.tensor_tensor(a, c, E.std[:, at], ALU.add))
    chain(v.tensor_scalar(c, a, 0.5, None, ALU.mult))
    chain(v.reciprocal(E.rstd[:, at], c))


def norm_root(act, E, var, std, at):
    act.wait_ge(var, 1)
    act.activation(E.std[:, at], E.ln_b[:, at], ACT.Sqrt).then_inc(std, 1)


def count_front(v, E, s):
    for i, (n, times) in enumerate((("xn_ready", 1), ("turned", KD), ("hi_ready", KD), ("lo_ready", KD))):
        v.memset(E.counts[:, i:i + 1], 0.0).then_inc(s[n], times)


def normalise(v, E, c, par, s, rows=None):
    for t in range(CT):
        at = bass.ds((c if rows is None else rows) * CT + t, 1)
        ins = v.tensor_scalar(E.xn[:, par, t:t + 1, :], E.x[:, at, :], E.mean[:, at], E.rstd[:, at],
                              ALU.subtract, ALU.mult)
    ins.then_inc(s["xn_ready"], 1)


def turn(pe, E, T, c, par, s, first=False, ready=None):
    pe.wait_ge(s["xn_ready"], c + 1 if ready is None else ready)
    if not first:
        pe.wait_ge(s["hi_ready"], c * KD)
        pe.wait_ge(s["lo_ready"], c * KD)
    for k in range(KD):
        for t in range(CT):
            mm = pe.transpose(T[:, k, t * P:(t + 1) * P], E.xn[:, par, t, k * P:(k + 1) * P], E.ident[:, :])
        mm.then_inc(s["turned"], 1)


def part_hi(act, E, T, c, par, s):
    for k in range(KD):
        act.wait_ge(s["turned"], c * KD + k + 1)
        act.activation(E.xt[0][:, par, k, :], T[:, k, :], ACT.Copy).then_inc(s["hi_ready"], 1)


def part_lo(v, E, T, c, par, s):
    for k in range(KD):
        v.wait_ge(s["hi_ready"], c * KD + k + 1)
        v.tensor_tensor(E.xt[1][:, par, k, :], T[:, k, :], E.xt[0][:, par, k, :].bitcast(F32),
                        ALU.subtract).then_inc(s["lo_ready"], 1)


def new_semaphore(nc, E, name):
    sem = nc.alloc_semaphore(name)
    E.semaphores.append(sem)
    return sem


def semaphores(nc, E, name, *names):
    return {n: new_semaphore(nc, E, f"{name}_{n}") for n in names}


def clear_semaphores(nc, E):
    nc.clear_and_free_semaphores(E.semaphores)
    nc.all_engine_barrier()
    E.semaphores = []


def statistics(v, E, c):
    for t in range(CT):
        ins = v.bn_stats(E.stats[:, bass.ds(c * CT + t, 1), :], E.x[:, bass.ds(c * CT + t, 1), :])
    return ins


class Split:

    def __init__(self, nc, E, ctx, name, jobs, tables=()):
        self.jobs, self.name, self.tables = jobs, name, tables
        self.tables_in = new_semaphore(nc, E, f"{name}_tables_in")
        self.landed = [new_semaphore(nc, E, f"{name}_in{i}") for i in range(len(jobs))]
        self.raw, self.value = [], []
        for i, (_, _, k, n, whole) in enumerate(jobs):
            self.raw.append(ctx.enter_context(nc.sbuf_tensor(f"{name}_raw{i}", [P, k, n], I32 if whole else F32)))
            self.value.append(ctx.enter_context(nc.sbuf_tensor(f"{name}_value{i}", [P, k, n], F32)) if whole else self.raw[i])

    def load(self, sp, i):
        _, src, k, n, _ = self.jobs[i]
        sp.dma_start(self.raw[i][:, :, :], src.rearrange("(k p) n -> p k n", p=P)).then_inc(self.landed[i], 16)

    def hi(self, eng, i):
        return eng.tensor_copy(self.jobs[i][0][0][:, :, :], self.value[i][:, :, :])

    def lo(self, eng, i, at=slice(None)):
        hi, lo = self.jobs[i][0]
        return eng.tensor_tensor(lo[:, at, :], self.value[i][:, at, :], hi[:, at, :].bitcast(F32), ALU.subtract)


def load_stage(nc, E, name, jobs, late, small, x_dram=None, ident=None):
    with ExitStack() as ctx:
        s = semaphores(nc, E, name, "x", "small", "cast", "hi", "hi_scalar", "peaks", "peak", "peak_all", "next_step", "next_var",
                       "next_std", "ident", "xn_ready", "turned", "hi_ready", "lo_ready")
        split = Split(nc, E, ctx, name, jobs)
        peaks = ctx.enter_context(nc.sbuf_tensor(f"{name}_peaks", [P, len(jobs)], F32))
        peak = ctx.enter_context(nc.sbuf_tensor(f"{name}_peak", [P, 1], F32))
        peak_all = ctx.enter_context(nc.sbuf_tensor(f"{name}_peak_all", [P, 1], F32))
        x_in = [new_semaphore(nc, E, f"{name}_x{c}") for c in range(CHUNKS)] if x_dram is not None else []
        integer = jobs[0][4]
        T = ctx.enter_context(nc.psum_tensor(f"{name}_T", [P, KD, CHUNK], F32))
        block = ctx.enter_context(nc.Block())

        @block.sync
        def _(sp):
            if ident is not None:
                sp.dma_start(E.ident[:, :], ident).then_inc(s["ident"], 16)
            for i in range(len(jobs)):
                split.load(sp, i)
            for tile, src in small:
                sp.dma_start(tile, src).then_inc(s["small"], 16)
            for c, landed in enumerate(x_in):
                sp.dma_start(E.x[:, c * CT:(c + 1) * CT, :],
                             x_dram[c * CHUNK:(c + 1) * CHUNK, :].rearrange("(t p) f -> p t f", p=P)).then_inc(landed, 16)
            for i in range(len(late.jobs)):
                late.load(sp, i)
            for tile, src in late.tables:
                sp.dma_start(tile, src).then_inc(late.tables_in, 16)
            sp.wait_ge(s["small"], 16 * len(small))

        @block.tensor
        def _(pe):
            if ident is not None:
                pe.wait_ge(s["ident"], 16)
            turn(pe, E, T, 0, 0, s, True)

        @block.scalar
        def _(act):
            def front():
                norm_root(act, E, s["next_var"], s["next_std"], NEXT)
                part_hi(act, E, T, 0, 0, s)

            if not integer:
                front()
            for i in range(len(jobs)):
                act.wait_ge(split.landed[i], 16)
                if integer:
                    act.activation(split.value[i][:, :, :], split.raw[i][:, :, :], ACT.Copy).then_inc(s["cast"], 1)
                elif i == 1:
                    act.activation(jobs[i][0][0][:, :, :], split.value[i][:, :, :], ACT.Copy).then_inc(s["hi_scalar"], 1)
            if integer:
                front()

        @block.vector
        def _(v):
            def front():
                n = norm_variance(v, E, s["next_step"], s["next_var"], NEXT, 1 if x_in else 0)
                norm_rstd(v, E, s["next_step"], s["next_std"], NEXT, n)
                normalise(v, E, 0, 0, s)

            if not integer:
                front()
                part_lo(v, E, T, 0, 0, s)
                v.wait_ge(split.landed[0], 16)
                split.hi(v, 0).then_inc(s["hi"], 1)
                v.wait_ge(s["hi"], 1)
                split.lo(v, 0)
                v.wait_ge(s["hi_scalar"], 1)
                split.lo(v, 1, slice(jobs[1][2] // 2, jobs[1][2]))
            else:
                for i in range(len(jobs)):
                    v.wait_ge(s["cast"], i + 1)
                    split.hi(v, i).then_inc(s["hi"], 1)
                    v.tensor_reduce(peaks[:, i:i + 1], split.value[i][:, :, :], AX.XY, ALU.max,
                                    apply_absolute_value=True).then_inc(s["peaks"], 1)
                v.wait_ge(s["peaks"], len(jobs))
                v.tensor_reduce(peak[:, :], peaks[:, :], AX.X, ALU.max).then_inc(s["peak"], 1)
            for c, landed in enumerate(x_in):
                v.wait_ge(landed, 16)
                last = statistics(v, E, c)
                if c == 0:
                    last.then_inc(s["next_step"], 1)
                    v.wait_ge(s["next_step"], 1)
                    front()
                if c == 3:
                    part_lo(v, E, T, 0, 0, s)
            if integer:
                v.wait_ge(s["peak_all"], 1)
                v.tensor_scalar(E.whole[:, :], peak_all[0:1, :], 2048.5, None, ALU.is_lt)
            E.scale_small(v, s)

        @block.gpsimd
        def _(p):
            for i in range(0 if integer else 1, len(jobs)):
                if integer:
                    p.wait_ge(s["hi"], i + 1)
                else:
                    p.wait_ge(s["hi_scalar"], 1)
                split.lo(p, i, slice(None) if integer else slice(0, jobs[i][2] // 2))
            if integer:
                p.wait_ge(s["peak"], 1)
                p.partition_all_reduce(peak_all[:, :], peak[:, :], P, bass.bass_isa.ReduceOp.max).then_inc(s["peak_all"], 1)


def ffn_stage(nc, E, name, gated, out_dram=None, late=None, follow=False):
    F = (HID0 if gated else HID1) // P
    with ExitStack() as ctx:
        def sb(n, shape, dt):
            return ctx.enter_context(nc.sbuf_tensor(f"{name}_{n}", shape, dt))

        h = sb("h", [P, 2, CHUNK], F32)
        h_parts = [sb(f"h_{n}", [P, 2, CHUNK], F32R) for n in ("hi", "lo")]
        gate_act = sb("gate_act", [P, 2, CHUNK], F32) if gated else None
        xb = None if gated else sb("xb", [P, 2, CT, D], F32)
        up_ps = ctx.enter_context(nc.psum_tensor(f"{name}_up", [P, 2, 2 if gated else 1, CHUNK], F32))
        acc = ctx.enter_context(nc.psum_tensor(f"{name}_acc", [P, CT, D], F32))
        T = ctx.enter_context(nc.psum_tensor(f"{name}_T", [P, KD, CHUNK], F32))
        s = semaphores(nc, E, name, "ln_step", "ln_var", "ln_std", "next_step", "next_var", "next_std", "xn_ready", "turned", "hi_ready", "lo_ready",
                       "up_ready", "gate_done", "gate_ready", "h_ready", "h_hi", "h_lo", "down_done", "x_new", "xb_ready",
                       "stored", "late_hi", "late_lo")
        block = ctx.enter_context(nc.Block())
        used = s["h_ready"]

        @block.tensor
        def _(pe):
            def path(whole):
                def up(c, par, f, first):
                    if f == 0:
                        pe.wait_ge(s["hi_ready"], c * KD + KD)
                        pe.wait_ge(s["lo_ready"], c * KD + KD)
                    if not first or f >= 2:
                        pe.wait_ge(used, c * F + f - 1)
                    cols = slice(f * P, (f + 1) * P)
                    for g, w in enumerate(E.w_up):
                        for k in range(KD):
                            mm = three_pass(pe, up_ps[:, f % 2, g, :], pair(w, slice(None), k, cols),
                                            pair(E.xt, slice(None), par, k, slice(None)), k == 0, k == KD - 1,
                                            whole=0 if whole else None)
                        mm.then_inc(s["up_ready"] if g == len(E.w_up) - 1 else s["gate_done"], 1)

                def down(c, f, first):
                    pe.wait_ge(s["h_hi"], c * F + f + 1)
                    pe.wait_ge(s["h_lo"], c * F + f + 1)
                    for t in range(CT):
                        if f == 0 and t % 2 == 0 and not first:
                            pe.wait_ge(s["x_new"], c * 2 - 1 + t // 2)
                        mm = three_pass(pe, acc[:, t, :], pair(h_parts, slice(None), f % 2, slice(t * P, (t + 1) * P)),
                                        pair(E.w_down, slice(None), f, slice(None)), f == 0 and t % 2 == 0, f == F - 1,
                                        True, whole=1 if whole else None)
                    mm.then_inc(s["down_done"], 1)

                def body(c, par, use, first, last):
                    for f in range(F):
                        up(c, par, f, first)
                        if f > 0:
                            down(c, f - 1, first)
                        elif not first:
                            down(c - 1, F - 1, False)
                        if f == 2 and (follow or not last):
                            turn(pe, E, T, c + 1, 1 - par, s)

                each_chunk(pe, body)
                down(CHUNKS - 1, F - 1, False)

            if not gated:
                path(False)
                return
            whole = pe.value_load(E.whole[0:1, 0:1])
            with pe.If(whole > 0):
                path(True)
            with pe.Else():
                path(False)

        @block.scalar
        def _(act):
            norm_root(act, E, s["ln_var"], s["ln_std"], ALL)

            def body(c, par, use, first, last):
                for f in range(F):
                    act.wait_ge(s["gate_done"] if gated else s["up_ready"], c * F + f + 1)
                    if gated:
                        if not first or f >= 2:
                            act.wait_ge(s["h_ready"], c * F + f - 1)
                        act.activation(gate_act[:, f % 2, :], up_ps[:, f % 2, 0, :], ACT.Silu,
                                       scale=DEQ).then_inc(s["gate_ready"], 1)
                    else:
                        if not first or f >= 2:
                            act.wait_ge(s["h_lo"], c * F + f - 1)
                        act.activation(h[:, f % 2, :], up_ps[:, f % 2, 0, :], ACT.Gelu,
                                       bias=E.b1[:, f:f + 1]).then_inc(s["h_ready"], 1)
                    act.wait_ge(s["h_ready"], c * F + f + 1)
                    if not first or f >= 2:
                        act.wait_ge(s["down_done"], c * F + f - 1)
                    act.activation(h_parts[0][:, f % 2, :], h[:, f % 2, :], ACT.Copy).then_inc(s["h_hi"], 1)
                    if f == 1 and follow and last:
                        norm_root(act, E, s["next_var"], s["next_std"], NEXT)
                    if f == 3 and (follow or not last):
                        part_hi(act, E, T, c + 1, 1 - par, s)

            each_chunk(act, body)

        @block.gpsimd
        def _(p):
            def add_bias(c, par):
                for t in range(CT):
                    ins = p.tensor_tensor(xb[:, par, t:t + 1, :], E.x[:, bass.ds(c * CT + t, 1), :],
                                          E.b2_half[:, :].unsqueeze(1), ALU.add)
                ins.then_inc(s["xb_ready"], 1)

            if not gated:
                add_bias(0, 0)

            def body(c, par, use, first, last):
                if not (gated or last):
                    if not first:
                        p.wait_ge(s["x_new"], c * 2)
                    add_bias(c + 1, 1 - par)

            if late is not None:
                for i in range(len(late.jobs)):
                    p.wait_ge(late.landed[i], 16)
                    late.hi(p, i).then_inc(s["late_hi"], 1)
                    p.wait_ge(s["late_hi"], i + 1)
                    late.lo(p, i).then_inc(s["late_lo"], 1)
                    p.wait_ge(s["late_lo"], i + 1)
            if not gated:
                each_chunk(p, body)

        @block.vector
        def _(v):
            count_front(v, E, s)
            n = norm_variance(v, E, s["ln_step"], s["ln_var"], ALL)
            norm_rstd(v, E, s["ln_step"], s["ln_std"], ALL, n)

            def finish(c, par, halves=(0, 1)):
                for q in halves:
                    if q == 0:
                        v.wait_ge(s["down_done"], c * F + F)
                        if not gated:
                            v.wait_ge(s["xb_ready"], c + 1)
                    at = bass.ds(c * CT + 2 * q, 2)
                    v.scalar_tensor_tensor(out=E.x[:, at, :], in0=acc[:, 2 * q:2 * q + 2, :],
                                           scalar=0.5 * DEQ if gated else 0.5,
                                           in1=E.x[:, at, :] if gated else xb[:, par, 2 * q:2 * q + 2, :],
                                           op0=ALU.mult, op1=ALU.add).then_inc(s["x_new"], 1)

            def measure(c):
                if out_dram is None:
                    v.wait_ge(s["x_new"], c * 2 + 2)
                    statistics(v, E, c)

            def body(c, par, use, first, last):
                if not last:
                    if not first:
                        v.wait_ge(s["turned"], c * KD)
                    normalise(v, E, c + 1, 1 - par, s)
                for f in range(F):
                    if gated:
                        v.wait_ge(s["up_ready"], c * F + f + 1)
                        v.wait_ge(s["gate_ready"], c * F + f + 1)
                        if not first or f >= 2:
                            v.wait_ge(s["h_lo"], c * F + f - 1)
                        v.scalar_tensor_tensor(out=h[:, f % 2, :], in0=up_ps[:, f % 2, 1, :], scalar=DEQ,
                                               in1=gate_act[:, f % 2, :], op0=ALU.mult, op1=ALU.mult).then_inc(s["h_ready"], 1)
                    if f == 0 and not first:
                        finish(c - 1, 1 - par, (0,))
                    v.wait_ge(s["h_hi"], c * F + f + 1)
                    if not first or f >= 2:
                        v.wait_ge(s["down_done"], c * F + f - 1)
                    v.tensor_tensor(h_parts[1][:, f % 2, :], h[:, f % 2, :], h_parts[0][:, f % 2, :].bitcast(F32),
                                    ALU.subtract).then_inc(s["h_lo"], 1)
                    if f == 0 and not first:
                        finish(c - 1, 1 - par, (1,))
                    if f == 1 and not first:
                        measure(c - 1)
                    if f == 0 and follow and last:
                        n = norm_variance(v, E, s["next_step"], s["next_var"], NEXT)
                    if f == 1 and follow and last:
                        norm_rstd(v, E, s["next_step"], s["next_std"], NEXT, n)
                        v.wait_ge(s["turned"], c * KD)
                        normalise(v, E, c + 1, 1 - par, s, rows=0)
                    if f == 3 and (follow or not last):
                        part_lo(v, E, T, c + 1, 1 - par, s)

            each_chunk(v, body)
            finish(CHUNKS - 1, (CHUNKS - 1) % 2)
            measure(CHUNKS - 1)

        if late is not None and late.tables:
            @block.sync
            def _(sp):
                sp.wait_ge(late.tables_in, 16 * len(late.tables))

        if out_dram is not None:
            @block.sync
            def _(sp):
                def body(c, par, use, first, last):
                    sp.wait_ge(s["x_new"], c * 2 + 2)
                    sp.dma_start(out_dram[bass.ds(c * CHUNK, CHUNK), :].rearrange("(t p) f -> p t f", p=P),
                                 E.x[:, bass.ds(c * CT, CT), :]).then_inc(s["stored"], 16)

                each_chunk(sp, body)
                sp.wait_ge(s["stored"], 16 * CHUNKS)


def qkv_stage(nc, E, name, rope):
    QK = 2 * KD
    with ExitStack() as ctx:
        def sb(n, shape, dt):
            return ctx.enter_context(nc.sbuf_tensor(f"{name}_{n}", shape, dt))

        qf = sb("qf", [P, QK, CHUNK], F32)
        raw = sb("raw", [P, QK, CHUNK], F32) if rope else qf
        swapped = sb("swapped", [P, CHUNK], F32) if rope else None
        cos_part = sb("cos_part", [P, 2, CHUNK], F32) if rope else None
        rest = sb("rest", [P, QK, CHUNK], F32)
        parts = sb("parts", [P, 2, QK, 3, CHUNK], BF16)
        vt = sb("vt", [P, 2, CT, D], F32)
        if rope:
            peaks = sb("peaks", [P, 2, QK], F32)
            top = sb("top", [P, QK], F32)
            peak = sb("peak", [P, 2], F32)
            peak_all = sb("peak_all", [P, 2], F32)
            peak_product = sb("peak_product", [1, 1], F32)
        T = ctx.enter_context(nc.psum_tensor(f"{name}_T", [P, KD, CHUNK], F32))
        qk_ps = ctx.enter_context(nc.psum_tensor(f"{name}_qk", [P, QK, CHUNK], F32))
        v_ps = ctx.enter_context(nc.psum_tensor(f"{name}_v", [P, CT, D], F32))
        s = semaphores(nc, E, name, "ln_step", "ln_var", "ln_std", "xn_ready", "turned", "hi_ready", "lo_ready",
                       "qk_ready", "raw_ready", "swap_ready", "cos_ready", "sin_ready", "rope_ready", "p1_ready",
                       "r_ready", "p2_ready", "p3_vector", "p3_pool", "v_ready", "vt_ready", "peaks_ready", "top_ready",
                       "peak_ready", "peak_all", "peak_product")
        parts_out = [new_semaphore(nc, E, f"{name}_parts_out{i}") for i in range(2)]
        v_out = [new_semaphore(nc, E, f"{name}_v_out{i}") for i in range(2)]
        q_ready = s["rope_ready"] if rope else s["raw_ready"]
        block = ctx.enter_context(nc.Block())

        def opening(c):
            return isinstance(c, int) and c == 0

        @block.tensor
        def _(pe):
            def body(c, par, use, last):
                first = opening(c)
                pe.wait_ge(s["hi_ready"], c * KD + KD)
                pe.wait_ge(s["lo_ready"], c * KD + KD)
                for i in range(QK):
                    w, half = (E.wq, E.wk)[i // KD], i % KD
                    if not first:
                        pe.wait_ge(s["raw_ready"], c * QK + i + 1 - QK)
                    for k in range(KD):
                        mm = three_pass(pe, qk_ps[:, i, :], pair(w, slice(None), k, slice(half * P, (half + 1) * P)),
                                        pair(E.xt, slice(None), par, k, slice(None)), k == 0, k == KD - 1)
                    mm.then_inc(s["qk_ready"], 1)
                if not last:
                    turn(pe, E, T, c + 1, 1 - par, s)
                for t in range(CT):
                    if t % 2 == 0 and not first:
                        pe.wait_ge(s["vt_ready"], c * 2 - 1 + t // 2)
                    for k in range(KD):
                        mm = three_pass(pe, v_ps[:, t, :], pair(E.xt, slice(None), par, k, slice(t * P, (t + 1) * P)),
                                        pair(E.wv, slice(None), k, slice(None)), k == 0, k == KD - 1)
                    if t % 2:
                        mm.then_inc(s["v_ready"], 1)

            each_chunk_lagged(pe, body)

        def before(c, par, use, i, back):
            if i >= back:
                return c, par, use, i - back
            return None if opening(c) else (c - 1, 1 - par, use - 1 + par, i - back + QK)

        def each_tile(eng, step, start=None, middle=None, middle_at=QK, finish=None):
            def body(c, par, use, last):
                if start:
                    start(c, par, use, last)
                for i in range(QK + 1):
                    if i == middle_at and middle:
                        middle(c, par, use, last)
                    if i < QK:
                        step((c, par, use, i), before(c, par, use, i, 1), before(c, par, use, i, 2))
                    if i == 1 and finish and not opening(c):
                        finish(c - 1, 1 - par, use - 1 + par)

            each_chunk_lagged(eng, body)
            end = (CHUNKS - 1, 1, (CHUNKS - 2) // 2)
            step(None, (*end, QK - 1), (*end, QK - 2))
            step(None, None, (*end, QK - 1))
            if finish:
                finish(*end)

        def store_v(eng, c, par, use):
            if not (isinstance(use, int) and use == 0):
                eng.wait_ge(v_out[par], use * 16)
            for q in range(2):
                eng.wait_ge(s["v_ready"], c * 2 + q + 1)
                dst, src = vt[:, par, 2 * q:2 * q + 2, :], v_ps[:, 2 * q:2 * q + 2, :]
                if rope:
                    ins = eng.activation(dst, src, ACT.Copy)
                else:
                    ins = eng.tensor_tensor(dst, src, E.bv[:, :].unsqueeze(1).to_broadcast([P, 2, D]), ALU.add)
                ins.then_inc(s["vt_ready"], 1)

        def third_part(eng, c, par, use, i, done):
            eng.wait_ge(s["p2_ready"], c * QK + i + 1)
            eng.tensor_tensor(parts[:, par, i, 2, :], rest[:, i, :], parts[:, par, i, 1, :],
                              ALU.subtract).then_inc(done, 1)

        @block.scalar
        def _(act):
            norm_root(act, E, s["ln_var"], s["ln_std"], ALL)

            def read(c, par, use, i):
                n = c * QK + i
                act.wait_ge(s["qk_ready"], n + 1)
                if not opening(c):
                    act.wait_ge(s["rope_ready"] if rope else s["r_ready"], n + 1 - QK)
                scale = (1.0 / HD if rope else 0.25) if i < KD else 1.0
                if rope:
                    ins = act.activation(raw[:, i, :], qk_ps[:, i, :], ACT.Copy, scale=scale)
                else:
                    ins = act.activation(raw[:, i, :], qk_ps[:, i, :], ACT.Identity, scale=scale,
                                         bias=E.b_qk[:, i:i + 1])
                ins.then_inc(s["raw_ready"], 1)

            def first_part(c, par, use, i):
                if i == 0 and not (isinstance(use, int) and use == 0):
                    act.wait_ge(parts_out[par], use * (16 * QK))
                act.wait_ge(q_ready, c * QK + i + 1)
                act.activation(parts[:, par, i, 0, :], qf[:, i, :], ACT.Copy).then_inc(s["p1_ready"], 1)

            def second_part(c, par, use, i):
                act.wait_ge(s["r_ready"], c * QK + i + 1)
                act.activation(parts[:, par, i, 1, :], rest[:, i, :], ACT.Copy).then_inc(s["p2_ready"], 1)

            def step(tile, one, two):
                if tile:
                    read(*tile)
                    c, par, _, i = tile
                    if i == QK - 1 and not (isinstance(c, int) and c == CHUNKS - 1):
                        part_hi(act, E, T, c + 1, 1 - par, s)
                if one:
                    first_part(*one)
                if two:
                    second_part(*two)

            def finish(c, par, use):
                if rope:
                    store_v(act, c, par, use)

            each_tile(act, step, finish=finish)

        @block.gpsimd
        def _(p):
            def times_cos(c, par, use, i):
                n = c * QK + i
                p.wait_ge(s["raw_ready"], n + 1)
                if not (opening(c) and i < 2):
                    p.wait_ge(s["rope_ready"], n - 1)
                p.tensor_tensor(cos_part[:, i % 2, :], raw[:, i, :], E.cos[:, par, :], ALU.mult).then_inc(s["cos_ready"], 1)

            def leave(c, par, use, i):
                n = c * QK + i
                p.wait_ge(s["p1_ready"], n + 1)
                if not opening(c):
                    if i % 2:
                        p.wait_ge(s["p3_pool"], c * 2 + i // 2 - 1)
                    else:
                        p.wait_ge(s["p3_vector"], c * 2 + i // 2 - 1)
                p.tensor_tensor(rest[:, i, :], qf[:, i, :], parts[:, par, i, 0, :], ALU.subtract).then_inc(s["r_ready"], 1)

            def step(tile, one, two):
                if tile and rope:
                    times_cos(*tile)
                if one:
                    leave(*one)
                if two and two[3] % 2:
                    third_part(p, *two, s["p3_pool"])

            each_tile(p, step)
            if rope:
                p.wait_ge(s["peak_ready"], 1)
                p.partition_all_reduce(peak_all[:, :], peak[:, :], P, bass.bass_isa.ReduceOp.max).then_inc(s["peak_all"], 1)

        @block.vector
        def _(v):
            count_front(v, E, s)
            n = norm_variance(v, E, s["ln_step"], s["ln_var"], ALL)
            norm_rstd(v, E, s["ln_step"], s["ln_std"], ALL, n)

            def rotate(tile, one):
                if tile:
                    c, par, use, i = tile
                    n = c * QK + i
                    v.wait_ge(s["raw_ready"], n + 1)
                if one:
                    v.wait_ge(s["rope_ready"], one[0] * QK + one[3] + 1)
                    v.tensor_reduce(peaks[:, one[1], one[3]:one[3] + 1], qf[:, one[3], :], AX.X, ALU.max,
                                    apply_absolute_value=True).then_inc(s["peaks_ready"], 1)
                if tile:
                    v.stream_shuffle(swapped[:, :], raw[:, i, :], [j ^ 1 for j in range(32)]).then_inc(s["swap_ready"], 1)
                    v.wait_ge(s["swap_ready"], n + 1)
                    v.tensor_tensor(swapped[:, :], swapped[:, :], E.sin[:, par, :], ALU.mult).then_inc(s["sin_ready"], 1)
                    v.wait_ge(s["sin_ready"], n + 1)
                    if not opening(c):
                        v.wait_ge(s["r_ready"], n + 1 - QK)
                    v.wait_ge(s["cos_ready"], n + 1)
                    v.tensor_tensor(qf[:, i, :], swapped[:, :], cos_part[:, i % 2, :], ALU.add).then_inc(s["rope_ready"], 1)

            def step(tile, one, two):
                if rope:
                    rotate(tile, one)
                if two and two[3] % 2 == 0:
                    third_part(v, *two, s["p3_vector"])

            def start(c, par, use, last):
                if not last:
                    if not opening(c):
                        v.wait_ge(s["turned"], c * KD)
                    normalise(v, E, c + 1, 1 - par, s)

            def middle(c, par, use, last):
                if not last:
                    part_lo(v, E, T, c + 1, 1 - par, s)

            def finish(c, par, use):
                if rope:
                    v.wait_ge(s["peaks_ready"], c * QK + QK)
                    if opening(c):
                        v.tensor_copy(top[:, :], peaks[:, par, :]).then_inc(s["top_ready"], 1)
                    else:
                        v.wait_ge(s["top_ready"], c)
                        v.tensor_tensor(top[:, :], top[:, :], peaks[:, par, :], ALU.max).then_inc(s["top_ready"], 1)
                else:
                    store_v(v, c, par, use)

            each_tile(v, step, start=start, middle=middle, middle_at=QK - 1, finish=finish)
            if rope:
                v.wait_ge(s["top_ready"], CHUNKS)
                v.tensor_reduce(peak[:, :], top[:, :].rearrange("p (a k) -> p a k", a=2), AX.X,
                                ALU.max).then_inc(s["peak_ready"], 1)
                v.wait_ge(s["peak_all"], 1)
                v.tensor_tensor(peak_product[:, :], peak_all[0:1, 0:1], peak_all[0:1, 1:2], ALU.mult).then_inc(s["peak_product"], 1)
                v.wait_ge(s["peak_product"], 1)
                v.tensor_scalar(E.outweighed[:, :], peak_product[:, :], (MASK - UNDERFLOW) / (2 * HD), None, ALU.is_lt)

        @block.sync
        def _(sp):
            def body(c, par, use, last):
                for i in range(QK):
                    sp.wait_ge(s["p3_pool"] if i % 2 else s["p3_vector"], c * 2 + i // 2 + 1)
                    half = i % KD
                    dst = (E.q_dram, E.k_dram)[i // KD][:, half * P:(half + 1) * P, bass.ds(c * CHUNK, CHUNK)]
                    sp.dma_start(dst.rearrange("g p n -> p g n"), parts[:, par, i, :, :]).then_inc(parts_out[par], 16)
                sp.wait_ge(s["vt_ready"], c * 2 + 2)
                sp.dma_start(E.v_dram[bass.ds(c * CHUNK, CHUNK), :].rearrange("(t p) f -> p t f", p=P),
                             vt[:, par, :, :]).then_inc(v_out[par], 16)

            each_chunk_lagged(sp, body)
            for par in range(2):
                sp.wait_ge(parts_out[par], 16 * QK * CHUNKS // 2)
                sp.wait_ge(v_out[par], 16 * CHUNKS // 2)


RING = 3
SLOTS = 4
TURN_AFTER = 2


class Plan:

    def __init__(self, masked, below, slack):
        self.masked, self.below = masked, below
        self.steps, units = [], []
        for qc in range(KC):
            unit = []
            for j in range(GH):
                for qt in range(4 * qc, 4 * qc + 4):
                    for kc in range(KC):
                        keys = min(512, (qt + 1) * P - kc * 512) if below else 512
                        heads = 512 // keys if keys > 0 else 0
                        if below and qc == 0 and keys == 256:
                            heads = 1
                        if heads and j % heads == 0:
                            unit.append((qc, slice(j, j + heads), qt, kc, keys))
            units.append(unit)
            for kt in range(QT):
                q0 = max(0, kt * P - qc * 512) if below else 0
                if q0 < 512:
                    self.steps.append((qc, kt, q0))
        n = len(units[0])
        self.pieces = units[0] + units[1][:TURN_AFTER] + [(0, None)] + units[1][TURN_AFTER:] + [(1, None)]
        self.end = [n - 1, len(self.pieces) - 2]
        self.turn = [n + TURN_AFTER, len(self.pieces) - 1]
        self.NS, self.NP = len(self.steps), len(self.pieces)
        assert self.NP % RING == 0
        self.begin = [next(i for i, x in enumerate(self.steps) if x[0] == qc) for qc in range(KC)] + [self.NS]
        cost_s = [512 - q0 for _, _, q0 in self.steps]
        cost_p = [x[4] * (x[1].stop - x[1].start) + 64 if x[1] else (256, 1152)[x[0]] for x in self.pieces]
        all_s, all_p = sum(cost_s), sum(cost_p)
        total = all_s * all_p * SLOTS
        at_s = [sum(cost_s[:i]) * all_p * SLOTS for i in range(self.NS + 1)]
        at_p = [sum(cost_p[:i + 1]) * all_s * SLOTS for i in range(self.NP)]
        lead = max(at_p[self.turn[qc]] - at_s[self.begin[qc]] for qc in range(KC)) + int(slack * total)

        def between(low, high):
            return [(d, a) for d in range(3) for a in range(self.NP) if low < at_p[a] + d * total <= high]

        self.start = between(-1, lead)
        self.feed = [between(lead + at_s[i] + (at_s[i + 1] - at_s[i]) * n // SLOTS,
                             lead + at_s[i] + (at_s[i + 1] - at_s[i]) * (n + 1) // SLOTS)
                     for i in range(self.NS) for n in range(SLOTS)]

    def later(self, a, by):
        return [(qc, (self.turn[qc] + by) // self.NP) for qc in range(KC) if (self.turn[qc] + by) % self.NP == a]


def attention_stage(nc, E, name, causal):
    NORM_R = 1 if causal else 2
    BLOCKS = 512 // 32
    UROWS = GH * 4
    with ExitStack() as ctx:
        def sb(n, shape, dt):
            return ctx.enter_context(nc.sbuf_tensor(f"{name}_{n}", shape, dt))

        def ps(n, shape):
            return ctx.enter_context(nc.psum_tensor(f"{name}_{n}", shape, F32))

        q_st = sb("q_st", [P, SETS, KC, GH, 512], BF16)
        k_st = sb("k_st", [P, SETS, GH, S], BF16)
        v_raw = sb("v_raw", [P, 2, QT, GH * HD], F32)
        v_st = sb("v_st", [P, 2, QT, GH, VW], F32)
        probs = sb("probs", [P, 2, GH, 512], F32)
        maxes = sb("maxes", [P, KC, GH, 4, KC], F32)
        neg_max = sb("neg_max", [P, KC * UROWS], F32)
        m_turned = sb("m_turned", [KC * UROWS, P], F32)
        m_rest = sb("m_rest", [KC * UROWS, P], F32)
        m_parts = sb("m_parts", [KC * UROWS, KC, 3, P], BF16)
        o_n = sb("o_n", [P, BLOCKS, VW], F32)
        small = sb("small", [P, 8, BLOCKS], F32)
        o_first = sb("o_first", [P, BLOCKS, HD], F32)
        o_rest = sb("o_rest", [P, BLOCKS, HD], F32)
        o_out = sb("o_out", [P, BLOCKS, HD], F32)
        v_first = None if causal else sb("v_first", [P, 2, HD], F32)
        key_mask = sb("key_mask", [P, QT, GH], F32)
        half = sb("half", [P, BLOCKS], F32)
        s_max = ps("s_max", [P, RING, 512])
        s_exp = ps("s_exp", [P, 2, 2, 512])
        o_ps = ps("o_ps", [P, 512])
        s = semaphores(nc, E, name, "v_ready", "sa_ready", "max_done", "nm_ready", "m_step", "m_ready", "st_ready", "exp_done", "pv_done", "o_turned",
                       "z_ready", "z_inv", "o_step", "o_done", "constants", "nm_zero", "clipped", "o_stored")
        staged = [new_semaphore(nc, E, f"{name}_staged{i}") for i in range(SETS)]
        staged_second = [new_semaphore(nc, E, f"{name}_staged_second{i}") for i in range(SETS)]
        v_in = [new_semaphore(nc, E, f"{name}_v_in{i}") for i in range(2)]
        f_in = [new_semaphore(nc, E, f"{name}_f_in{i}") for i in range(2)]
        m_in = [new_semaphore(nc, E, f"{name}_m_in{i}") for i in range(KC)]
        block = ctx.enter_context(nc.Block())
        STAGE_DMAS = len(PARTS_Q) + len(PARTS_K)
        general = Plan(causal, False, 3 / 16)
        below = Plan(True, True, 6 / 16) if causal else None

        def choose(eng, path):
            if not causal:
                path(general)
                return
            outweighed = eng.value_load(E.outweighed[0:1, 0:1])
            with eng.If(outweighed > 0):
                path(below)
            with eng.Else():
                path(general)

        @block.sync
        def _(sp):
            def path(plan):
                NS, NP = plan.NS, plan.NP

                def stage(it):
                    heads = slice(it.hg * GH * HD, (it.hg + 1) * GH * HD)
                    for qc in range(KC):
                        for g, (pq, pk) in enumerate(zip(PARTS_Q, PARTS_K)):
                            rows = slice(g * HD, (g + 1) * HD)
                            src = E.q_dram[pq, heads, bass.ds(it.b * S + qc * 512, 512)]
                            sp.dma_start(q_st[rows, it.set, qc, :, :], src.rearrange("(j d) n -> d j n", d=HD))\
                                .then_inc((staged, staged_second)[qc][it.set], 16)
                            if qc == 0:
                                src = E.k_dram[pk, heads, bass.ds(it.b * S, S)]
                                sp.dma_start(k_st[rows, it.set, :, :], src.rearrange("(j d) n -> d j n", d=HD))\
                                    .then_inc(staged[it.set], 16)

                def stage_v(it):
                    src = E.v_dram[bass.ds(it.b * S, S), it.hg * GH * HD:(it.hg + 1) * GH * HD]
                    sp.dma_start(v_raw[:, it.par, :, :], src.rearrange("(t p) f -> p t f", p=P)).then_inc(v_in[it.par], 16)

                def stage_first(it):
                    src = E.v_dram[bass.ds(it.b * S, 1), it.hg * GH * HD:(it.hg + 1) * GH * HD]
                    sp.dma_start(v_first[:, it.par, :], src.rearrange("o (j d) -> j o d", d=HD).to_broadcast([GH, 32, HD]))\
                        .then_inc(f_in[it.par], 16)

                def put_max(it, qc):
                    sp.wait_ge(s["m_ready"], it.n(2, qc + 1))
                    for part in range(MROWS):
                        dst = q_st[SROWS + part:SROWS + part + 1, it.set, qc, :, :].rearrange("o j (t q) -> o (j t) q", q=P)
                        sp.dma_start(dst, m_parts[qc * UROWS:(qc + 1) * UROWS, qc, part, :]).then_inc(m_in[qc], 16)

                start = It(0, 0)
                stage(start)
                stage_v(start)
                stage(start.ahead(1))
                stage_v(start.ahead(1))
                if not causal:
                    stage_first(start)
                    stage_first(start.ahead(1))
                stage(start.ahead(2))
                put_max(start, 0)

                def body(it, first, last):
                    left = ITERS - 1 - it.r if isinstance(it.k, int) else SETS
                    put_max(it, 1)
                    if left >= 3:
                        if not first:
                            sp.wait_ge(s["st_ready"], it.n(2 * NS, 0))
                        stage(it.ahead(3))
                    if left >= 2:
                        sp.wait_ge(s["v_ready"], it.n(1, 1))
                        stage_v(it.ahead(2))
                    if not (causal or first or last):
                        sp.wait_ge(s["o_done"], it.n(2, 0))
                        stage_first(it.ahead(1))
                    if not last:
                        put_max(it.ahead(1), 0)

                each_iteration(sp, body)
                sp.wait_ge(s["o_stored"], 2 * 16 * GH * ITERS)

            choose(sp, path)

        @block.tensor
        def _(pe):
            def path(plan):
                NS, NP = plan.NS, plan.NP

                def max_piece(it, a, free):
                    if a == 0:
                        pe.wait_ge(staged[it.set], it.b * (16 * STAGE_DMAS) + 16 * STAGE_DMAS)
                    if a == plan.end[0] + 1:
                        pe.wait_ge(staged_second[it.set], it.b * (16 * len(PARTS_Q)) + 16 * len(PARTS_Q))
                    if not free:
                        pe.wait_ge(s["max_done"], it.n(NP, a + 1 - RING))
                    if a in plan.turn:
                        turn_max(it, plan.pieces[a][0], a)
                        return
                    qc, heads, qt, kc, keys = plan.pieces[a]
                    masked = plan.masked and kc * 512 + keys - 1 > qt * P
                    row = (qt - 4 * qc) * P
                    for j in range(heads.start, heads.stop):
                        begin = (j - heads.start) * keys
                        mm = pe.matmul(s_max[:, a % RING, begin:begin + keys], q_st[0:SROWS, it.set, qc, j, row:row + P],
                                       k_st[0:SROWS, it.set, j, kc * 512:kc * 512 + keys], start=True, stop=not masked)
                        if masked:
                            k0 = keys - P if plan.below else 0
                            at = S + kc * 512 + k0 - qt * P
                            mm = pe.matmul(s_max[:, a % RING, begin + k0:begin + keys], E.ident16[:, :],
                                           E.mask_q[:, at:at + keys - k0], start=False, stop=True)
                    mm.then_inc(s["sa_ready"], 1)

                def turn_max(it, qc, a):
                    pe.wait_ge(s["nm_ready"], it.n(2, qc + 1))
                    if it.start and qc == 0:
                        pe.wait_ge(s["nm_zero"], 1)
                    pe.transpose(s_max[0:KC * UROWS, a % RING, 0:P], neg_max[:, :], E.ident[:, :]).then_inc(s["sa_ready"], 1)

                def feed(it, pieces):
                    for d, a in pieces:
                        if it.ahead(d).exists:
                            max_piece(it.ahead(d), a, it.ahead(d).start and a < RING)

                def scores(it, step, jp, first):
                    qc, kt, q0 = plan.steps[step]
                    u = 2 * step + jp
                    if step in plan.begin and jp == 0:
                        pe.wait_ge(m_in[qc], it.n(16 * MROWS, 16 * MROWS))
                        pe.wait_ge(s["constants"], 1)
                    if not first or u >= 2:
                        pe.wait_ge(s["exp_done"], it.n(2 * NS, u - 1))
                    masked = plan.masked and kt * P + P - 1 > qc * 512 + q0
                    for jj in range(2):
                        j = 2 * jp + jj
                        mm = pe.matmul(s_exp[:, jp, jj, q0:512], k_st[0:SROWS + MROWS, it.set, j, kt * P:(kt + 1) * P],
                                       q_st[0:SROWS + MROWS, it.set, qc, j, q0:512], start=True, stop=not masked)
                        if masked:
                            q1 = q0 + P if plan.below else 512
                            at = S + qc * 512 + q0 - kt * P
                            mm = pe.matmul(s_exp[:, jp, jj, q0:q1], E.ident16[:, :], E.mask_k[:, at:at + q1 - q0],
                                           start=False, stop=True)
                    mm.then_inc(s["st_ready"], 1)

                def values(it, step, part, first):
                    qc, kt, q0 = plan.steps[step]
                    middle = q0 + (512 - q0) // (2 * P) * P
                    cols = (slice(q0, middle), slice(middle, 512))[part]
                    if step == 0 and part == 0:
                        pe.wait_ge(s["v_ready"], it.n(1, 1))
                    if part == 0:
                        pe.wait_ge(s["exp_done"], it.n(2 * NS, 2 * step + 2))
                        if kt == 0 and not (first and qc == 0):
                            pe.wait_ge(s["o_turned"], it.n(2, qc))
                    if cols.start == cols.stop:
                        return
                    for j in range(GH):
                        mm = pe.matmul(o_ps[j * VW:(j + 1) * VW, cols], v_st[:, it.par, kt, j, :], probs[:, step % 2, j, cols],
                                       start=kt == 0 and part == 0, stop=step + 1 in plan.begin, skip_group_check=True)
                    if part == 1:
                        mm.then_inc(s["pv_done"], 1)

                feed(It(0, 0), plan.start)

                def body(it, first, last):
                    for step in range(NS):
                        slots = plan.feed[step * SLOTS:(step + 1) * SLOTS]
                        feed(it, slots[0])
                        scores(it, step, 0, first)
                        feed(it, slots[1])
                        scores(it, step, 1, first)
                        feed(it, slots[2])
                        for part in range(2):
                            if step > 0:
                                values(it, step - 1, part, first)
                            elif not first:
                                values(it.ahead(-1), NS - 1, part, False)
                            if part == 0:
                                feed(it, slots[3])

                each_iteration(pe, body)
                end = It(0, ITERS - 1)
                values(end, NS - 1, 0, False)
                values(end, NS - 1, 1, False)

            choose(pe, path)

        @block.scalar
        def _(act):
            def path(plan):
                NS, NP = plan.NS, plan.NP

                def body(it, first, last):
                    for step in range(NS):
                        q0 = plan.steps[step][2]
                        for jp in range(2):
                            u = 2 * step + jp
                            act.wait_ge(s["st_ready"], it.n(2 * NS, u + 1))
                            if jp == 0 and (not first or step >= 2):
                                act.wait_ge(s["pv_done"], it.n(NS, step - 1))
                            act.activation(probs[:, step % 2, 2 * jp:2 * jp + 2, q0:512], s_exp[:, jp, :, q0:512],
                                           ACT.Exp).then_inc(s["exp_done"], 1)

                each_iteration(act, body)

            choose(act, path)

        @block.vector
        def _(v):
            v.memset(neg_max[:, :], 0.0).then_inc(s["nm_zero"], 1)
            v.wait_ge(s["nm_zero"], 1)

            def path(plan):
                NS, NP = plan.NS, plan.NP

                def max_piece(it, a):
                    v.wait_ge(s["sa_ready"], it.n(NP, a + 1))
                    if a in plan.turn:
                        v.tensor_copy(m_turned[:, :], s_max[0:KC * UROWS, a % RING, 0:P]).then_inc(s["max_done"], 1)
                        return
                    qc, heads, qt, kc, keys = plan.pieces[a]
                    banks = s_max[:, a % RING, 0:(heads.stop - heads.start) * keys].rearrange("p (j k) -> p j k", k=keys)
                    v.tensor_reduce(maxes[:, qc, heads, qt - 4 * qc, kc], banks, AX.X,
                                    ALU.max).then_inc(s["max_done"], 1)
                    if a == plan.end[qc]:
                        v.wait_ge(s["max_done"], it.n(NP, a + 1))
                        rows = slice(qc * UROWS, (qc + 1) * UROWS)
                        chunks = qc + 1 if plan.below else KC
                        v.tensor_reduce(neg_max[:, rows], maxes[:, qc, :, :, 0:chunks].rearrange("p j t c -> p (j t) c"), AX.X, ALU.max,
                                        negate=True).then_inc(s["nm_ready"], 1)

                def split_max(it, qc, i):
                    p1, p2, p3 = (m_parts[:, qc, part, :] for part in range(3))
                    if i == 0:
                        v.wait_ge(s["max_done"], it.n(NP, plan.turn[qc] + 1))
                        if not it.start:
                            v.wait_ge(m_in[qc], it.n(16 * MROWS, 0))
                        v.tensor_copy(p1, m_turned[:, :]).then_inc(s["m_step"], 1)
                    elif i == 1:
                        v.wait_ge(s["m_step"], it.n(6, 3 * qc + 1))
                        v.tensor_tensor(m_rest[:, :], m_turned[:, :], p1, ALU.subtract).then_inc(s["m_step"], 1)
                    elif i == 2:
                        v.wait_ge(s["m_step"], it.n(6, 3 * qc + 2))
                        v.tensor_copy(p2, m_rest[:, :]).then_inc(s["m_step"], 1)
                    else:
                        v.wait_ge(s["m_step"], it.n(6, 3 * qc + 3))
                        v.tensor_tensor(p3, m_rest[:, :], p2, ALU.subtract).then_inc(s["m_ready"], 1)

                def feed(it, pieces):
                    for d, a in pieces:
                        if it.ahead(d).exists:
                            max_piece(it.ahead(d), a)
                        for i in range(4):
                            for qc, back in plan.later(a, i):
                                if it.ahead(d - back).exists:
                                    split_max(it.ahead(d - back), qc, i)

                def turn_out(it, qc, first=False):
                    v.wait_ge(s["pv_done"], it.n(NS, plan.begin[qc + 1]))
                    if not (first and qc == 0):
                        v.wait_ge(s["o_done"], it.n(2, qc))
                    v.transpose(o_n[:, :, :].rearrange("p b r -> p (b r)"), o_ps[:, :]).then_inc(s["o_turned"], 1)

                def invert(it, qc, i):
                    if causal:
                        v.wait_ge(s["o_turned"], it.n(2, qc + 1))
                    else:
                        v.wait_ge(s["z_ready"], it.n(4, 2 * qc + i + 1))
                    src = o_n[:, :, HD] if causal else small[:, 2 * i, :]
                    if i == 1:
                        v.tensor_scalar(src, src, CLIP, None, ALU.max).then_inc(s["clipped"], 1)
                        v.wait_ge(s["clipped"], it.n(2, qc + 1))
                    v.reciprocal(small[:, 2 * i + 1, :], src).then_inc(s["z_inv"], 1)

                feed(It(0, 0), plan.start)

                def body(it, first, last):
                    for step in range(NS):
                        if step == 1 and not first:
                            turn_out(it.ahead(-1), 1)
                        if step == plan.begin[1] + 1:
                            turn_out(it, 0, first)
                        for slot in plan.feed[step * SLOTS:(step + 1) * SLOTS]:
                            feed(it, slot)
                        for i in range(NORM_R):
                            if step == 3 + 2 * i and not first:
                                invert(it.ahead(-1), 1, i)
                            if step == plan.begin[1] + 3 + 2 * i:
                                invert(it, 0, i)

                each_iteration(v, body)
                turn_out(It(0, ITERS - 1), 1)
                for i in range(NORM_R):
                    invert(It(0, ITERS - 1), 1, i)

            choose(v, path)

        @block.gpsimd
        def _(p):
            fills = [(k_st[SROWS:SROWS + MROWS, :, :, :], 1.0), (v_st[:, :, :, :, :], 0.0), (key_mask[:, :, :], 1.0),
                     (half[:, :], 0.5), (v_st[:, :, :, :, HD:HD + 1], 1.0)]
            if not causal:
                fills += [(key_mask[0:1, 0, :], 0.0), (v_st[0:1, :, 0, :, HD:HD + 1], 0.0),
                          (v_st[0:1, :, 0, :, HD + 1:HD + 2], 1.0)]
            for n, (tile, value) in enumerate(fills):
                p.memset(tile, value).then_inc(s["constants"], 1)
                p.wait_ge(s["constants"], n + 1)

            def path(plan):
                NS, NP = plan.NS, plan.NP

                def put_values(it, used):
                    p.wait_ge(v_in[it.par], it.pair * 16 + 16)
                    if used:
                        p.wait_ge(s["pv_done"], it.n(NS, -NS))
                    p.tensor_tensor(v_st[:, it.par, :, :, 0:HD], v_raw[:, it.par, :, :].rearrange("p t (j d) -> p t j d", d=HD),
                                    key_mask[:, :, :].unsqueeze(3).to_broadcast([P, QT, GH, HD]), ALU.mult).then_inc(s["v_ready"], 1)

                def normalise_out(it, qc, wait_slot):
                    u = qc
                    p.wait_ge(s["o_turned"], it.n(2, u + 1))
                    if wait_slot:
                        p.wait_ge(s["o_stored"], it.n(32 * GH, 16 * GH * qc))
                    rest, ones, one = o_n[:, :, 0:HD], o_n[:, :, HD], o_n[:, :, HD + 1]
                    out = o_out[:, :, :]

                    def wide(x):
                        return x.unsqueeze(2).to_broadcast([P, BLOCKS, HD])

                    if causal:
                        p.wait_ge(s["z_inv"], it.n(2, u + 1))
                        p.tensor_tensor(out, rest, wide(small[:, 1, :]), ALU.mult).then_inc(s["o_done"], 1)
                        return
                    n = 0
                    PER = 6

                    def chain(ins):
                        nonlocal n
                        n += 1
                        ins.then_inc(s["o_step"], 1)
                        p.wait_ge(s["o_step"], it.n(2 * PER, u * PER + n))

                    z, z_inv, share, share_inv, w_all, w_one, w_add, w_rest = (small[:, i, :] for i in range(8))
                    p.tensor_tensor(z, ones, one, ALU.add).then_inc(s["z_ready"], 1)
                    p.wait_ge(s["z_inv"], it.n(4, 2 * u + 1))
                    p.tensor_tensor(share, ones, z_inv, ALU.mult).then_inc(s["z_ready"], 1)
                    chain(p.tensor_tensor(w_all, z_inv, half[:, :], ALU.mult))
                    chain(p.tensor_tensor(w_one, w_all, one, ALU.mult))
                    if qc == 0:
                        p.wait_ge(f_in[it.par], it.pair * 16 + 16)
                    fv = v_first[:, it.par, :].unsqueeze(1).to_broadcast([P, BLOCKS, HD])
                    chain(p.tensor_tensor(o_first[:, :, :], fv, wide(w_one), ALU.mult))
                    p.wait_ge(s["z_inv"], it.n(4, 2 * u + 2))
                    chain(p.tensor_tensor(w_add, share_inv, w_all, ALU.mult))
                    chain(p.tensor_tensor(w_rest, w_add, w_all, ALU.add))
                    chain(p.tensor_tensor(o_rest[:, :, :], rest, wide(w_rest), ALU.mult))
                    p.tensor_tensor(out, o_rest[:, :, :], o_first[:, :, :], ALU.add).then_inc(s["o_done"], 1)

                def store(it, qc):
                    p.wait_ge(s["o_done"], it.n(2, qc + 1))
                    for j in range(GH):
                        head = (it.hg * GH + j) * HD
                        rows = E.ao_dram[bass.ds(it.b * S + qc * 512, 512), head:head + HD]
                        p.dma_start(rows.rearrange("(t r) d -> r t d", r=32),
                                      o_out[32 * j:32 * j + 32, :, :]).then_inc(s["o_stored"], 16)

                put_values(It(0, 0), False)

                def body(it, first, last):
                    if not last:
                        put_values(it.ahead(1), not first)
                    if not first:
                        normalise_out(it.ahead(-1), 1, True)
                        store(it.ahead(-1), 1)
                    normalise_out(it, 0, not first)
                    store(it, 0)

                each_iteration(p, body)
                normalise_out(It(0, ITERS - 1), 1, True)
                store(It(0, ITERS - 1), 1)

            choose(p, path)


def out_stage(nc, E, name):
    with ExitStack() as ctx:
        acc = ctx.enter_context(nc.psum_tensor(f"{name}_acc", [P, 2, CT, D], F32))
        T = ctx.enter_context(nc.psum_tensor(f"{name}_T", [P, KD, CHUNK], F32))
        s = semaphores(nc, E, name, "turned", "hi_ready", "lo_ready", "out_done", "x_new", "xb_ready",
                       "xn_ready", "next_step", "next_var", "next_std")
        loaded = [new_semaphore(nc, E, f"{name}_in{i}") for i in range(2)]
        block = ctx.enter_context(nc.Block())

        @block.sync
        def _(sp):
            def body(c, par, use, fresh):
                if not fresh:
                    sp.wait_ge(s["turned"], c * KD - KD)
                sp.dma_start(E.xn[:, par, :, :], E.ao_dram[bass.ds(c * CHUNK, CHUNK), :].rearrange("(t p) f -> p t f", p=P))\
                    .then_inc(loaded[par], 16)

            each_chunk_of_two(sp, body)

        @block.tensor
        def _(pe):
            def turn_rows(c, par, use, first):
                pe.wait_ge(loaded[par], use * 16 + 16)
                if not first:
                    pe.wait_ge(s["hi_ready"], c * KD)
                    pe.wait_ge(s["lo_ready"], c * KD)
                for k in range(KD):
                    for t in range(CT):
                        mm = pe.transpose(T[:, k, t * P:(t + 1) * P], E.xn[:, par, t, k * P:(k + 1) * P], E.ident[:, :])
                    mm.then_inc(s["turned"], 1)

            def product(c, par, fresh):
                pe.wait_ge(s["hi_ready"], c * KD + KD)
                pe.wait_ge(s["lo_ready"], c * KD + KD)
                if not fresh:
                    pe.wait_ge(s["x_new"], c * 2 - 2)
                for t in range(CT):
                    for k in range(KD):
                        mm = three_pass(pe, acc[:, par, t, :], pair(E.xt, slice(None), par, k, slice(t * P, (t + 1) * P)),
                                        pair(E.wo, slice(None), k, slice(None)), k == 0, k == KD - 1)
                mm.then_inc(s["out_done"], 1)

            def body(c, par, use, fresh):
                turn_rows(c, par, use, fresh and par == 0)
                if not (fresh and par == 0):
                    product(c - 1, 1 - par, fresh)

            each_chunk_of_two(pe, body)
            product(CHUNKS - 1, 1, False)
            turn(pe, E, T, CHUNKS, 0, s, ready=1)

        @block.scalar
        def _(act):
            def body(c, par, use, fresh):
                if not fresh:
                    act.wait_ge(s["out_done"], c - 1)
                part_hi(act, E, T, c, par, s)
                if fresh and par == 1:
                    norm_root(act, E, s["next_var"], s["next_std"], NEXT)

            each_chunk_of_two(act, body)
            act.wait_ge(s["out_done"], CHUNKS - 1)
            part_hi(act, E, T, CHUNKS, 0, s)

        @block.vector
        def _(v):
            def finish(c, par):
                v.wait_ge(s["out_done"], c + 1)
                v.wait_ge(s["xb_ready"], c + 1)
                for q in range(2):
                    at = bass.ds(c * CT + 2 * q, 2)
                    v.tensor_tensor(E.x[:, at, :], acc[:, par, 2 * q:2 * q + 2, :], E.x[:, at, :], ALU.add).then_inc(s["x_new"], 1)
                v.wait_ge(s["x_new"], c * 2 + 2)
                return statistics(v, E, c)

            def body(c, par, use, fresh):
                part_lo(v, E, T, c, par, s)
                if not (fresh and par == 0):
                    measured = finish(c - 1, 1 - par)
                if fresh and par == 1:
                    measured.then_inc(s["next_step"], 1)
                    v.wait_ge(s["next_step"], 1)
                    norm_variance(v, E, s["next_step"], s["next_var"], NEXT, 1)

            each_chunk_of_two(v, body)
            norm_rstd(v, E, s["next_step"], s["next_std"], NEXT, 1 + NORM_STEPS)
            v.wait_ge(s["turned"], (CHUNKS - 1) * KD)
            normalise(v, E, CHUNKS, 0, s, rows=0)
            finish(CHUNKS - 1, 1)
            part_lo(v, E, T, CHUNKS, 0, s)

        @block.gpsimd
        def _(p):
            for c in range(CHUNKS):
                at = slice(c * CT, (c + 1) * CT)
                p.tensor_tensor(E.x[:, at, :], E.x[:, at, :], E.bo[:, :].unsqueeze(1).to_broadcast([P, CT, D]),
                                ALU.add).then_inc(s["xb_ready"], 1)


def program(nc, io, out_dram):
    E = Env()
    E.semaphores = []
    with ExitStack() as ctx:
        def sb(n, shape, dt):
            return ctx.enter_context(nc.sbuf_tensor(n, shape, dt))

        E.q_dram = nc.dram_tensor("q_parts", [3, D, B * S], BF16)
        E.k_dram = nc.dram_tensor("k_parts", [3, D, B * S], BF16)
        E.v_dram = nc.dram_tensor("v_rows", [B * S, D], F32)
        E.ao_dram = nc.dram_tensor("attention_rows", [B * S, D], F32)
        E.x = sb("x", [P, TILES, D], F32)
        E.stats = sb("stats", [P, TILES, 6], F32)
        E.ident = sb("ident", [P, P], F32)
        E.whole = sb("whole", [1, 1], I32)

        def parts(stack, n, k, cols):
            return [stack.enter_context(nc.sbuf_tensor(f"{n}_{x}", [P, k, cols], F32R)) for x in ("hi", "lo")]

        with ExitStack() as layer:
            gate, up = parts(layer, "w_gate", KD, HID0), parts(layer, "w_up", KD, HID0)
            E.w_up, E.w_down = (gate, up), parts(layer, "w_down", HID0 // P, D)
            E.wq, E.wk, E.wv, E.wo = (parts(layer, f"w0{n}", KD, D) for n in "qkvo")
            b_raw = layer.enter_context(nc.sbuf_tensor("b_raw", [P, 2 * KD], F32))
            E.b_qk = layer.enter_context(nc.sbuf_tensor("b_qk", [P, 2 * KD], F32))
            E.bv = layer.enter_context(nc.sbuf_tensor("bv", [P, D], F32))
            E.bo = layer.enter_context(nc.sbuf_tensor("bo", [P, D], F32))

            def scale_small(v, s):
                v.wait_ge(s["small"], 16 * 4)
                v.tensor_scalar(E.b_qk[:, 0:KD], b_raw[:, 0:KD], 0.25, None, ALU.mult)
                v.tensor_copy(E.b_qk[:, KD:2 * KD], b_raw[:, KD:2 * KD])

            E.scale_small = scale_small
            front, late = ExitStack(), ExitStack()
            alloc_front(nc, E, front, "front0a")
            square = Split(nc, E, late, "square0",
                           [(w, io[f"w0{n}_t"], KD, D, False) for w, n in zip((E.wq, E.wk, E.wv, E.wo), "qkvo")])
            load_stage(nc, E, "load0",
                       [(gate, io["gate_t"], KD, HID0, True), (up, io["up_t"], KD, HID0, True),
                        (E.w_down, io["down_t"], HID0 // P, D, True)], square,
                       [(b_raw[:, 0:KD], io["bq"]), (b_raw[:, KD:2 * KD], io["bk"]),
                        (E.bv[:, :], io["bv"].partition_broadcast(P)), (E.bo[:, :], io["bo0"].partition_broadcast(P))],
                       io["x"], io["ident"])
            ffn_stage(nc, E, "ffn0a", True, late=square, follow=True)
            late.close()
            qkv_stage(nc, E, "qkv0", False)
            front.close()
            attention_stage(nc, E, "att0", False)
            with ExitStack() as front:
                alloc_front(nc, E, front, "front0b")
                out_stage(nc, E, "out0")
                ffn_stage(nc, E, "ffn0b", True)
        clear_semaphores(nc, E)

        with ExitStack() as layer:
            E.w_up = (parts(layer, "w1", KD, HID1),)
            E.w_down = parts(layer, "w2", HID1 // P, D)
            E.wq, E.wk, E.wv, E.wo = (parts(layer, f"w1{n}", KD, D) for n in "qkvo")
            E.b1 = layer.enter_context(nc.sbuf_tensor("b1", [P, HID1 // P], F32))
            E.b2_half = layer.enter_context(nc.sbuf_tensor("b2_half", [P, D], F32))
            E.bo = layer.enter_context(nc.sbuf_tensor("bo1", [P, D], F32))
            b2 = layer.enter_context(nc.sbuf_tensor("b2", [P, D], F32))
            E.cos = layer.enter_context(nc.sbuf_tensor("cos", [P, S // CHUNK, CHUNK], F32))
            E.sin = layer.enter_context(nc.sbuf_tensor("sin", [P, S // CHUNK, CHUNK], F32))
            E.mask_q = layer.enter_context(nc.sbuf_tensor("mask_q", [P, 2 * S], F16))
            E.mask_k = layer.enter_context(nc.sbuf_tensor("mask_k", [P, 2 * S], F16))
            E.outweighed = layer.enter_context(nc.sbuf_tensor("outweighed", [1, 1], I32))
            E.ident16 = layer.enter_context(nc.sbuf_tensor("ident16", [P, P], F16))

            def scale_small(v, s):
                v.wait_ge(s["small"], 16 * 2)
                v.tensor_scalar(E.b2_half[:, :], b2[:, :], 0.5, None, ALU.mult)

            E.scale_small = scale_small
            front, late = ExitStack(), ExitStack()
            alloc_front(nc, E, front, "front1a")
            square = Split(nc, E, late, "square1",
                           [(w, io[f"w1{n}_t"], KD, D, False) for w, n in zip((E.wq, E.wk, E.wv, E.wo), "qkvo")],
                           [(E.bo[:, :], io["bo1"].partition_broadcast(P)), (E.cos[:, :, :], io["cos"]),
                            (E.sin[:, :, :], io["sin"]), (E.mask_q[:, :], io["mask_q"]),
                            (E.mask_k[:, :], io["mask_k"]), (E.ident16[:, :], io["ident16"])])
            load_stage(nc, E, "load1",
                       [(E.w_up[0], io["w1"], KD, HID1, False), (E.w_down, io["w2"], HID1 // P, D, False)], square,
                       [(E.b1[:, :], io["b1"]), (b2[:, :], io["b2"].partition_broadcast(P))])
            ffn_stage(nc, E, "ffn1a", False, late=square, follow=True)
            late.close()
            qkv_stage(nc, E, "qkv1", True)
            front.close()
            attention_stage(nc, E, "att1", True)
            with ExitStack() as front:
                alloc_front(nc, E, front, "front1b")
                out_stage(nc, E, "out1")
                ffn_stage(nc, E, "ffn1b", False, out_dram)


def shape_constants():
    import numpy as np

    p, c = np.arange(P)[:, None], np.arange(2 * S)[None, :] - S
    neg = np.float16(-MASK)
    inv_freq = (np.float32(1.0) / np.float32(10000.0) ** (np.arange(0, HD, 2, dtype=np.float32) / np.float32(HD)))
    ang = (np.arange(S, dtype=np.float32)[:, None] * inv_freq.astype(np.float32)[None, :]).astype(np.float32)
    d = np.arange(P) % HD
    cos = np.cos(ang).astype(np.float32)[:, d // 2].T
    sin = np.sin(ang).astype(np.float32)[:, d // 2].T * np.where(d % 2, 1.0, -1.0).astype(np.float32)[:, None]
    return {
        "ident": np.eye(P, dtype=np.float32),
        "ident16": np.eye(P, dtype=np.float16),
        "mask_q": np.where(c > p, neg, np.float16(0)),
        "mask_k": np.where(c < p, neg, np.float16(0)),
        "cos": np.ascontiguousarray(cos.reshape(P, S // CHUNK, CHUNK)),
        "sin": np.ascontiguousarray(sin.astype(np.float32).reshape(P, S // CHUNK, CHUNK)),
    }


def kernel(**inputs):
    import numpy as np
    import concourse.bacc as bacc
    from concourse.bass_utils import run_bass_kernel_spmd

    a = {k: np.asarray(v) for k, v in inputs.items()}

    def columns(v):
        return np.ascontiguousarray(v.reshape(-1, P).T)

    arrays = {
        "x": np.ascontiguousarray(a["L0_attn_x"].reshape(B * S, D)),
        "gate_t": np.ascontiguousarray(a["L0_ffn_w_gate"].T),
        "up_t": np.ascontiguousarray(a["L0_ffn_w_up"].T),
        "down_t": np.ascontiguousarray(a["L0_ffn_w_down"].T),
        "bq": columns(a["L0_attn_bq"]), "bk": columns(a["L0_attn_bk"]),
        "bv": a["L0_attn_bv"], "bo0": a["L0_attn_bo"],
        "w1": a["L1_ffn_w1"], "w2": a["L1_ffn_w2"],
        "b1": columns(a["L1_ffn_b1"]), "b2": a["L1_ffn_b2"], "bo1": a["L1_attn_bo"],
    }
    for n in "qkvo":
        arrays[f"w0{n}_t"] = np.ascontiguousarray(a[f"L0_attn_W{n}"].T)
        arrays[f"w1{n}_t"] = np.ascontiguousarray(a[f"L1_attn_W{n}"].T)
    arrays.update(shape_constants())

    nc = bacc.Bacc("TRN2", target_bir_lowering=False, num_devices=1)
    io = {n: nc.dram_tensor(f"in_{n}", v.shape, mybir.dt.from_np(v.dtype), kind="ExternalInput").ap()
          for n, v in arrays.items()}
    out = nc.dram_tensor("out", (B * S, D), F32, kind="ExternalOutput").ap()
    program(nc, io, out)
    r = run_bass_kernel_spmd(nc, [{f"in_{n}": v for n, v in arrays.items()}], core_ids=[0])
    return r.results[0]["out"].reshape(B, S, D)
```
